# Optimizing a Trainium2 kernel written in Bass

```python
import numpy as np
import jax
import jax.numpy as jnp

def _softmax(x, axis=-1):
    return jax.nn.softmax(x, axis=axis)

def _gelu(x):
    return jax.nn.gelu(x, approximate=True)

def _silu(x):
    return jax.nn.silu(x)

def _sigmoid(x):
    return jax.nn.sigmoid(x)

def _layernorm(x, axis=-1, eps=1e-05):
    m = jnp.mean(x, axis=axis, keepdims=True)
    v = jnp.var(x, axis=axis, keepdims=True)
    return (x - m) / jnp.sqrt(v + eps)

def _scatter_add(tgt, idx, src, axis=0):
    return tgt.at[idx].add(src)

def _segment_sum(src, seg, n):
    return jax.ops.segment_sum(src, seg, n)
kernel_name = 'mk_recurrent_d4_jaxref_r8_e7e8e3'

def setup_inputs(seed: int=0):
    np.random.seed(seed)
    _w = jnp.asarray

    def _L0_attn_setup():
        import jax, jax.numpy as jnp
        import numpy as np
        DIM = 128
        HEADS = 16
        HEAD_DIM = 64
        ROT = 32
        BASE = 10000.0
        SEQ = 256
        BATCH = 2

        def _rotate_half(t):
            x1, x2 = (t[..., :ROT // 2], t[..., ROT // 2:])
            return jnp.concatenate([-x2, x1], axis=-1)

        def _apply_rope(t, cos, sin):
            t_rot, t_pass = (t[..., :ROT], t[..., ROT:])
            t_rot = t_rot * cos + _rotate_half(t_rot) * sin
            return jnp.concatenate([t_rot, t_pass], axis=-1)
        key = jax.random.key(seed)
        k1, k2, k3, k4 = jax.random.split(key, 4)
        s = 0.02
        return {'x': jax.random.normal(k1, (BATCH, SEQ, DIM), dtype=jnp.float32), 'w_q': jax.random.normal(k2, (DIM, HEADS * HEAD_DIM), dtype=jnp.float32) * s, 'w_kv': jax.random.normal(k3, (DIM, 2 * HEADS * HEAD_DIM), dtype=jnp.float32) * s, 'w_out': jax.random.normal(k4, (HEADS * HEAD_DIM, DIM), dtype=jnp.float32) * s}
    _L0_attn_in = _L0_attn_setup()

    def _L0_ffn_setup():
        import jax, jax.numpy as jnp
        import numpy as np
        DIM = 128
        HIDDEN = 384
        SCALE = 1.0 / 127.0

        def _dequant(w_int, dtype):
            return w_int.astype(dtype) * jnp.asarray(SCALE, dtype)
        key = jax.random.key(seed)
        k_x, k_g, k_u, k_d = jax.random.split(key, 4)
        x = jax.random.normal(k_x, (4, 256, DIM), dtype=jnp.float32)
        w_gate = jax.random.randint(k_g, (HIDDEN, DIM), -127, 128, dtype=jnp.int32)
        w_up = jax.random.randint(k_u, (HIDDEN, DIM), -127, 128, dtype=jnp.int32)
        w_down = jax.random.randint(k_d, (DIM, HIDDEN), -127, 128, dtype=jnp.int32)
        return {'x': x, 'w_gate': w_gate, 'w_up': w_up, 'w_down': w_down}
    _L0_ffn_in = _L0_ffn_setup()

    def _L1_attn_setup():
        import jax, jax.numpy as jnp
        import numpy as np
        B, T = (4, 256)
        D_MODEL = 128
        N_HEADS = 8
        HEAD_DIM = 32
        KV_LRANK = 64

        def _orthogonalize_per_head(w):
            chunks = w.reshape(N_HEADS, HEAD_DIM, D_MODEL)

            def ns(m):
                A = m @ m.T
                Bm = 1.5 * jnp.eye(HEAD_DIM, dtype=m.dtype) - 0.5 * A
                return Bm @ m
            return jax.vmap(ns)(chunks).reshape(w.shape)
        key = jax.random.key(seed)
        ks = jax.random.split(key, 6)

        def lin(k, out_dim, in_dim):
            bound = 1.0 / np.sqrt(in_dim)
            return jax.random.uniform(k, (out_dim, in_dim), jnp.float32, -bound, bound)
        Wq = _orthogonalize_per_head(lin(ks[0], N_HEADS * HEAD_DIM, D_MODEL))
        return {'x': jax.random.normal(ks[1], (B, T, D_MODEL), jnp.float32), 'Wq': Wq, 'Wkv_down': lin(ks[2], KV_LRANK, D_MODEL), 'Wk_up': lin(ks[3], N_HEADS * HEAD_DIM, KV_LRANK), 'Wv_up': lin(ks[4], N_HEADS * HEAD_DIM, KV_LRANK), 'Wo': lin(ks[5], D_MODEL, N_HEADS * HEAD_DIM)}
    _L1_attn_in = _L1_attn_setup()

    def _L1_ffn_setup():
        import jax, jax.numpy as jnp
        import numpy as np
        DIM = 128
        DEPTH = 2
        HEADS = 8
        DIM_HEAD = 64
        WINDOW = 64
        INNER = HEADS * DIM_HEAD
        HID = int(DIM * 4 * 2 / 3)
        B, N = (2, 1024)
        QK_SCALE = 8.0

        def shift_token(t):
            t1, t2 = jnp.split(t, 2, axis=-1)
            t2 = jnp.pad(t2, ((0, 0), (1, 0), (0, 0)))[:, :-1]
            return jnp.concatenate([t1, t2], axis=-1)

        def l2norm(t):
            return t / jnp.clip(jnp.linalg.norm(t, axis=-1, keepdims=True), 1e-12)

        def rotate_half(x):
            x1, x2 = jnp.split(x, 2, axis=-1)
            return jnp.concatenate([-x2, x1], axis=-1)

        def rotary_xpos(q, k):
            n = q.shape[-2]
            half_idx = jnp.arange(0, DIM_HEAD, 2, dtype=jnp.float32)
            inv_freq = 1.0 / 10000.0 ** (half_idx / DIM_HEAD)
            t = jnp.arange(n, dtype=jnp.float32)
            freqs = t[:, None] * inv_freq[None, :]
            freqs = jnp.concatenate([freqs, freqs], axis=-1)
            base = (half_idx + 0.4 * DIM_HEAD) / (1.4 * DIM_HEAD)
            power = (t - n // 2) / float(WINDOW // 2)
            scale = base[None, :] ** power[:, None]
            scale = jnp.concatenate([scale, scale], axis=-1)
            cos, sin = (jnp.cos(freqs), jnp.sin(freqs))
            q = q * cos * scale + rotate_half(q) * sin * scale
            k = k * cos / scale + rotate_half(k) * sin / scale
            return (q, k)

        def local_attention(q, k, v):
            b, h, n, d = q.shape
            w = n // WINDOW
            bq = q.reshape(b, h, w, WINDOW, d) * QK_SCALE
            bk = k.reshape(b, h, w, WINDOW, d)
            bv = v.reshape(b, h, w, WINDOW, d)

            def look_around(t):
                p = jnp.pad(t, ((0, 0), (0, 0), (1, 0), (0, 0), (0, 0)))
                return jnp.concatenate([p[:, :, :w], p[:, :, 1:]], axis=3)
            bk, bv = (look_around(bk), look_around(bv))
            bt = jnp.arange(n).reshape(w, WINDOW)
            btp = jnp.pad(bt, ((1, 0), (0, 0)), constant_values=-1)
            btk = jnp.concatenate([btp[:w], btp[1:]], axis=1)
            sim = jnp.einsum('bhwid,bhwjd->bhwij', bq, bk)
            i = bt[:, :, None]
            j = btk[:, None, :]
            mask = (i < j) | (i > j + WINDOW) | (j == -1)
            sim = jnp.where(mask, -jnp.finfo(sim.dtype).max, sim)
            attn = jax.nn.softmax(sim, axis=-1)
            out = jnp.einsum('bhwij,bhwjd->bhwid', attn, bv)
            return out.reshape(b, h, n, d)

        def _layer(x, wqkv, qs, ksc, wo, lg, lb, w1, b1, w2, b2):
            b, n, _ = x.shape
            h = shift_token(x)
            qkv = h @ wqkv
            q, k, v = jnp.split(qkv, 3, axis=-1)
            to_heads = lambda t: t.reshape(b, n, HEADS, DIM_HEAD).transpose(0, 2, 1, 3)
            q, k, v = (to_heads(q), to_heads(k), to_heads(v))
            q = l2norm(q) * qs
            k = l2norm(k) * ksc
            q, k = rotary_xpos(q, k)
            o = local_attention(q, k, v)
            o = o.transpose(0, 2, 1, 3).reshape(b, n, INNER)
            x = x + o @ wo
            h = shift_token(x)
            mu = h.mean(-1, keepdims=True)
            var = h.var(-1, keepdims=True)
            h = (h - mu) / jnp.sqrt(var + 1e-05) * lg + lb
            h = h @ w1 + b1
            a, g = jnp.split(h, 2, axis=-1)
            h = a * jax.nn.gelu(g, approximate=False)
            x = x + h @ w2 + b2
            return x
        key = jax.random.key(seed)
        ks = jax.random.split(key, 6)
        return {'x': jax.random.normal(ks[0], (B, N, DIM), jnp.float32), 'wqkv': jax.random.normal(ks[1], (DEPTH, DIM, 3 * INNER), jnp.float32) * 0.02, 'q_scale': jnp.ones((DEPTH, DIM_HEAD), jnp.float32), 'k_scale': jnp.ones((DEPTH, DIM_HEAD), jnp.float32), 'wo': jax.random.normal(ks[2], (DEPTH, INNER, DIM), jnp.float32) * 0.02, 'ln_g': jnp.ones((DEPTH, DIM), jnp.float32), 'ln_b': jnp.zeros((DEPTH, DIM), jnp.float32), 'w1': jax.random.normal(ks[3], (DEPTH, DIM, 2 * HID), jnp.float32) * 0.02, 'b1': jnp.zeros((DEPTH, 2 * HID), jnp.float32), 'w2': jax.random.normal(ks[4], (DEPTH, HID, DIM), jnp.float32) * 0.02, 'b2': jnp.zeros((DEPTH, DIM), jnp.float32)}
    _L1_ffn_in = _L1_ffn_setup()

    def _L2_attn_setup():
        import jax, jax.numpy as jnp
        import numpy as np
        import math
        D_MODEL = 128
        N_HEADS = 16
        D_K = D_MODEL // N_HEADS
        BATCH = 4
        SEQ = 256
        TRAINING_PROGRESS = 0.25
        CONVERGENCE_PHASE = 0.5
        TENSION = abs(1.0 - 1.0)

        def _pos_encoding(seq_len, d, yellow):
            phase_mod = 0.1 * math.sin(2.0 * math.pi * TRAINING_PROGRESS)
            i_even = jnp.arange(0, d, 2, dtype=jnp.float32)
            denom = jnp.power(10000.0, 2.0 * i_even / d) * (1.0 + yellow * phase_mod)
            pos = jnp.arange(seq_len, dtype=jnp.float32)
            ang = pos[:, None] / denom[None, :]
            pe = jnp.zeros((seq_len, d), jnp.float32)
            pe = pe.at[:, 0::2].set(jnp.sin(ang))
            pe = pe.at[:, 1::2].set(jnp.cos(ang))
            return pe
        key = jax.random.key(seed)
        ks = jax.random.split(key, 8)
        x = jax.random.normal(ks[0], (BATCH, SEQ, D_MODEL), dtype=jnp.float32)
        rby = jax.random.uniform(ks[1], (3,), dtype=jnp.float32)
        s = 0.02
        Wq = jax.random.normal(ks[2], (D_MODEL, D_MODEL), dtype=jnp.float32) * s
        Wk = jax.random.normal(ks[3], (D_MODEL, D_MODEL), dtype=jnp.float32) * s
        Wv = jax.random.normal(ks[4], (D_MODEL, D_MODEL), dtype=jnp.float32) * s
        Wo = jax.random.normal(ks[5], (D_MODEL, D_MODEL), dtype=jnp.float32) * s
        bq = jnp.zeros((D_MODEL,), jnp.float32)
        bk = jnp.zeros((D_MODEL,), jnp.float32)
        bv = jnp.zeros((D_MODEL,), jnp.float32)
        bo = jnp.zeros((D_MODEL,), jnp.float32)
        ln_gamma = jnp.ones((D_MODEL,), jnp.float32)
        ln_beta = jnp.zeros((D_MODEL,), jnp.float32)
        return {'x': x, 'rby': rby, 'Wq': Wq, 'bq': bq, 'Wk': Wk, 'bk': bk, 'Wv': Wv, 'bv': bv, 'Wo': Wo, 'bo': bo, 'ln_gamma': ln_gamma, 'ln_beta': ln_beta}
    _L2_attn_in = _L2_attn_setup()

    def _L2_ffn_setup():
        import jax, jax.numpy as jnp
        import numpy as np
        D_IN, D_HID = (128, 512)

        def _ternary(key, shape):
            return jax.random.randint(key, shape, -1, 2).astype(jnp.float32)

        def _tlin(x, w, s):
            return jnp.einsum('bsi,oi->bso', x, w) * s
        key = jax.random.key(seed)
        ks = jax.random.split(key, 12)
        inv = lambda fan: 1.0 / np.sqrt(fan).astype(np.float32)
        return {'x': jax.random.normal(ks[0], (4, 256, D_IN), dtype=jnp.float32), 'w1_w': _ternary(ks[1], (D_HID, D_IN)), 'w1_s': jax.random.uniform(ks[2], (D_HID,), dtype=jnp.float32) * inv(D_IN), 'w2_w': _ternary(ks[3], (D_HID, D_IN)), 'w2_s': jax.random.uniform(ks[4], (D_HID,), dtype=jnp.float32) * inv(D_IN), 'h1_w': _ternary(ks[5], (D_HID, D_HID)), 'h1_s': jax.random.uniform(ks[6], (D_HID,), dtype=jnp.float32) * inv(D_HID), 'h2_w': _ternary(ks[7], (D_HID, D_HID)), 'h2_s': jax.random.uniform(ks[8], (D_HID,), dtype=jnp.float32) * inv(D_HID), 'w3_w': _ternary(ks[9], (D_IN, D_HID)), 'w3_s': jax.random.uniform(ks[10], (D_IN,), dtype=jnp.float32) * inv(D_HID)}
    _L2_ffn_in = _L2_ffn_setup()

    def _L3_attn_setup():
        import jax, jax.numpy as jnp
        import numpy as np
        D = 128
        H = 16
        HD = 64
        AHD = H * HD
        B = 4
        S = 128
        EPS = 1e-05
        SMAX = float(D) ** 0.5

        def _ln(x, s, b):
            mu = jnp.mean(x, axis=-1, keepdims=True)
            var = jnp.mean(jnp.square(x - mu), axis=-1, keepdims=True)
            return (x - mu) * jax.lax.rsqrt(var + EPS) * s + b

        def _forward(x, lnq_s, lnq_b, Wq, bq, lnk_s, lnk_b, Wk, bk, lnv_s, lnv_b, Wv, bv, Wo, bo, lnm_s, lnm_b, W1, b1, W2, b2):
            Bq, Sq, _ = x.shape
            q = (_ln(x, lnq_s, lnq_b) @ Wq + bq).reshape(Bq, Sq, H, HD).transpose(0, 2, 1, 3)
            k = (_ln(x, lnk_s, lnk_b) @ Wk + bk).reshape(Bq, Sq, H, HD).transpose(0, 2, 1, 3)
            v = (_ln(x, lnv_s, lnv_b) @ Wv + bv).reshape(Bq, Sq, H, HD).transpose(0, 2, 1, 3)
            scores = jnp.einsum('bhqd,bhkd->bhqk', q, k) / SMAX
            mask = jnp.triu(jnp.full((Sq, Sq), -999.0, dtype=scores.dtype), k=Sq - 1)
            p = jax.nn.softmax(scores + mask, axis=-1)
            att = jnp.einsum('bhqk,bhkd->bhqd', p, v).transpose(0, 2, 1, 3).reshape(Bq, Sq, AHD)
            h = att @ Wo + bo + x
            y = _ln(h, lnm_s, lnm_b)
            m = jax.nn.gelu(y @ W1 + b1) @ W2 + b2
            return m + h
        key = jax.random.key(seed)
        ks = jax.random.split(key, 7)

        def lin(k, fan_in, fan_out):
            lim = 1.0 / np.sqrt(fan_in)
            kw, kb = jax.random.split(k)
            W = jax.random.uniform(kw, (fan_in, fan_out), minval=-lim, maxval=lim, dtype=jnp.float32)
            b = jax.random.uniform(kb, (fan_out,), minval=-lim, maxval=lim, dtype=jnp.float32)
            return (W, b)
        Wq, bq = lin(ks[0], D, AHD)
        Wk, bk = lin(ks[1], D, AHD)
        Wv, bv = lin(ks[2], D, AHD)
        Wo, bo = lin(ks[3], AHD, D)
        W1, b1 = lin(ks[4], D, 2 * D)
        W2, b2 = lin(ks[5], 2 * D, D)
        x = jax.random.normal(ks[6], (B, S, D), dtype=jnp.float32)
        ones = jnp.ones((D,), jnp.float32)
        zeros = jnp.zeros((D,), jnp.float32)
        return {'x': x, 'lnq_s': ones, 'lnq_b': zeros, 'Wq': Wq, 'bq': bq, 'lnk_s': ones, 'lnk_b': zeros, 'Wk': Wk, 'bk': bk, 'lnv_s': ones, 'lnv_b': zeros, 'Wv': Wv, 'bv': bv, 'Wo': Wo, 'bo': bo, 'lnm_s': ones, 'lnm_b': zeros, 'W1': W1, 'b1': b1, 'W2': W2, 'b2': b2}
    _L3_attn_in = _L3_attn_setup()

    def _L3_ffn_setup():
        import jax, jax.numpy as jnp
        import numpy as np
        EPS = 1e-12

        def rms_norm(t, gamma):
            n = jnp.maximum(jnp.linalg.norm(t, axis=-1, keepdims=True), EPS)
            scale = jnp.sqrt(jnp.asarray(t.shape[-1], t.dtype))
            return t / n * scale * gamma
        key = jax.random.key(seed)
        ks = jax.random.split(key, 4)
        b, s, d = (4, 512, 128)
        e, t = (8, 64)
        hidden = 4 * d
        return {'x': jax.random.normal(ks[0], (b, s, d), dtype=jnp.float32), 'gamma_x': jnp.ones((d,), dtype=jnp.float32), 'gamma_slot': jnp.ones((d,), dtype=jnp.float32), 'slot_embeds': jax.random.normal(ks[1], (e, t, d), dtype=jnp.float32), 'w1': jax.random.normal(ks[2], (d, hidden), dtype=jnp.float32) * (1.0 / np.sqrt(d)), 'w2': jax.random.normal(ks[3], (hidden, d), dtype=jnp.float32) * (1.0 / np.sqrt(hidden))}
    _L3_ffn_in = _L3_ffn_setup()
    _d = {'L0_attn_x': _L0_attn_in['x'], 'L0_attn_w_q': _L0_attn_in['w_q'], 'L0_attn_w_kv': _L0_attn_in['w_kv'], 'L0_attn_w_out': _L0_attn_in['w_out'], 'L0_ffn_w_gate': _L0_ffn_in['w_gate'], 'L0_ffn_w_up': _L0_ffn_in['w_up'], 'L0_ffn_w_down': _L0_ffn_in['w_down'], 'L1_attn_Wq': _L1_attn_in['Wq'], 'L1_attn_Wkv_down': _L1_attn_in['Wkv_down'], 'L1_attn_Wk_up': _L1_attn_in['Wk_up'], 'L1_attn_Wv_up': _L1_attn_in['Wv_up'], 'L1_attn_Wo': _L1_attn_in['Wo'], 'L1_ffn_wqkv': _L1_ffn_in['wqkv'], 'L1_ffn_q_scale': _L1_ffn_in['q_scale'], 'L1_ffn_k_scale': _L1_ffn_in['k_scale'], 'L1_ffn_wo': _L1_ffn_in['wo'], 'L1_ffn_ln_g': _L1_ffn_in['ln_g'], 'L1_ffn_ln_b': _L1_ffn_in['ln_b'], 'L1_ffn_w1': _L1_ffn_in['w1'], 'L1_ffn_b1': _L1_ffn_in['b1'], 'L1_ffn_w2': _L1_ffn_in['w2'], 'L1_ffn_b2': _L1_ffn_in['b2'], 'L2_attn_rby': _L2_attn_in['rby'], 'L2_attn_Wq': _L2_attn_in['Wq'], 'L2_attn_bq': _L2_attn_in['bq'], 'L2_attn_Wk': _L2_attn_in['Wk'], 'L2_attn_bk': _L2_attn_in['bk'], 'L2_attn_Wv': _L2_attn_in['Wv'], 'L2_attn_bv': _L2_attn_in['bv'], 'L2_attn_Wo': _L2_attn_in['Wo'], 'L2_attn_bo': _L2_attn_in['bo'], 'L2_attn_ln_gamma': _L2_attn_in['ln_gamma'], 'L2_attn_ln_beta': _L2_attn_in['ln_beta'], 'L2_ffn_w1_w': _L2_ffn_in['w1_w'], 'L2_ffn_w1_s': _L2_ffn_in['w1_s'], 'L2_ffn_w2_w': _L2_ffn_in['w2_w'], 'L2_ffn_w2_s': _L2_ffn_in['w2_s'], 'L2_ffn_h1_w': _L2_ffn_in['h1_w'], 'L2_ffn_h1_s': _L2_ffn_in['h1_s'], 'L2_ffn_h2_w': _L2_ffn_in['h2_w'], 'L2_ffn_h2_s': _L2_ffn_in['h2_s'], 'L2_ffn_w3_w': _L2_ffn_in['w3_w'], 'L2_ffn_w3_s': _L2_ffn_in['w3_s'], 'L3_attn_lnq_s': _L3_attn_in['lnq_s'], 'L3_attn_lnq_b': _L3_attn_in['lnq_b'], 'L3_attn_Wq': _L3_attn_in['Wq'], 'L3_attn_bq': _L3_attn_in['bq'], 'L3_attn_lnk_s': _L3_attn_in['lnk_s'], 'L3_attn_lnk_b': _L3_attn_in['lnk_b'], 'L3_attn_Wk': _L3_attn_in['Wk'], 'L3_attn_bk': _L3_attn_in['bk'], 'L3_attn_lnv_s': _L3_attn_in['lnv_s'], 'L3_attn_lnv_b': _L3_attn_in['lnv_b'], 'L3_attn_Wv': _L3_attn_in['Wv'], 'L3_attn_bv': _L3_attn_in['bv'], 'L3_attn_Wo': _L3_attn_in['Wo'], 'L3_attn_bo': _L3_attn_in['bo'], 'L3_attn_lnm_s': _L3_attn_in['lnm_s'], 'L3_attn_lnm_b': _L3_attn_in['lnm_b'], 'L3_attn_W1': _L3_attn_in['W1'], 'L3_attn_b1': _L3_attn_in['b1'], 'L3_attn_W2': _L3_attn_in['W2'], 'L3_attn_b2': _L3_attn_in['b2'], 'L3_ffn_gamma_x': _L3_ffn_in['gamma_x'], 'L3_ffn_gamma_slot': _L3_ffn_in['gamma_slot'], 'L3_ffn_slot_embeds': _L3_ffn_in['slot_embeds'], 'L3_ffn_w1': _L3_ffn_in['w1'], 'L3_ffn_w2': _L3_ffn_in['w2']}
    _x0 = _d['L0_attn_x']
    _d['L0_attn_x'] = jax.random.normal(jax.random.fold_in(jax.random.key(seed), 1), (1, 2048, 128), dtype=_x0.dtype)
    del _x0
    return _d

def reference(L0_attn_x, L0_attn_w_q, L0_attn_w_kv, L0_attn_w_out, L0_ffn_w_gate, L0_ffn_w_up, L0_ffn_w_down, L1_attn_Wq, L1_attn_Wkv_down, L1_attn_Wk_up, L1_attn_Wv_up, L1_attn_Wo, L1_ffn_wqkv, L1_ffn_q_scale, L1_ffn_k_scale, L1_ffn_wo, L1_ffn_ln_g, L1_ffn_ln_b, L1_ffn_w1, L1_ffn_b1, L1_ffn_w2, L1_ffn_b2, L2_attn_rby, L2_attn_Wq, L2_attn_bq, L2_attn_Wk, L2_attn_bk, L2_attn_Wv, L2_attn_bv, L2_attn_Wo, L2_attn_bo, L2_attn_ln_gamma, L2_attn_ln_beta, L2_ffn_w1_w, L2_ffn_w1_s, L2_ffn_w2_w, L2_ffn_w2_s, L2_ffn_h1_w, L2_ffn_h1_s, L2_ffn_h2_w, L2_ffn_h2_s, L2_ffn_w3_w, L2_ffn_w3_s, L3_attn_lnq_s, L3_attn_lnq_b, L3_attn_Wq, L3_attn_bq, L3_attn_lnk_s, L3_attn_lnk_b, L3_attn_Wk, L3_attn_bk, L3_attn_lnv_s, L3_attn_lnv_b, L3_attn_Wv, L3_attn_bv, L3_attn_Wo, L3_attn_bo, L3_attn_lnm_s, L3_attn_lnm_b, L3_attn_W1, L3_attn_b1, L3_attn_W2, L3_attn_b2, L3_ffn_gamma_x, L3_ffn_gamma_slot, L3_ffn_slot_embeds, L3_ffn_w1, L3_ffn_w2):

    def _L0_attn_ref(x, w_q, w_kv, w_out):
        import jax, jax.numpy as jnp
        import numpy as np
        DIM = 128
        HEADS = 16
        HEAD_DIM = 64
        ROT = 32
        BASE = 10000.0
        SEQ = 256
        BATCH = 2

        def _rotate_half(t):
            x1, x2 = (t[..., :ROT // 2], t[..., ROT // 2:])
            return jnp.concatenate([-x2, x1], axis=-1)

        def _apply_rope(t, cos, sin):
            t_rot, t_pass = (t[..., :ROT], t[..., ROT:])
            t_rot = t_rot * cos + _rotate_half(t_rot) * sin
            return jnp.concatenate([t_rot, t_pass], axis=-1)
        b, n, _ = x.shape
        q = (x @ w_q).reshape(b, n, HEADS, HEAD_DIM).transpose(0, 2, 1, 3)
        k, v = jnp.split(x @ w_kv, 2, axis=-1)
        k = k.reshape(b, n, HEADS, HEAD_DIM).transpose(0, 2, 1, 3)
        v = v.reshape(b, n, HEADS, HEAD_DIM).transpose(0, 2, 1, 3)
        inv_freq = 1.0 / BASE ** (jnp.arange(0, ROT, 2, dtype=jnp.float32) / ROT)
        freqs = jnp.arange(n, dtype=jnp.float32)[:, None] * inv_freq[None, :]
        freqs = jnp.concatenate([freqs, freqs], axis=-1)
        cos, sin = (jnp.cos(freqs), jnp.sin(freqs))
        q = _apply_rope(q, cos, sin)
        k = _apply_rope(k, cos, sin)
        scale = HEAD_DIM ** (-0.5)
        scores = jnp.einsum('bhid,bhjd->bhij', q, k) * scale
        causal_mask = jnp.tril(jnp.ones((n, n), dtype=bool))
        scores = jnp.where(causal_mask, scores, jnp.finfo(scores.dtype).min)
        attn = jax.nn.softmax(scores, axis=-1)
        out = jnp.einsum('bhij,bhjd->bhid', attn, v)
        out = out.transpose(0, 2, 1, 3).reshape(b, n, HEADS * HEAD_DIM)
        return out @ w_out

    def _L0_ffn_ref(x, w_gate, w_up, w_down):
        import jax, jax.numpy as jnp
        import numpy as np
        DIM = 128
        HIDDEN = 384
        SCALE = 1.0 / 127.0

        def _dequant(w_int, dtype):
            return w_int.astype(dtype) * jnp.asarray(SCALE, dtype)
        wg = _dequant(w_gate, x.dtype)
        wu = _dequant(w_up, x.dtype)
        wd = _dequant(w_down, x.dtype)
        gate = jnp.einsum('bsd,hd->bsh', x, wg)
        up = jnp.einsum('bsd,hd->bsh', x, wu)
        h = jax.nn.silu(gate) * up
        return jnp.einsum('bsh,dh->bsd', h, wd)

    def _L1_attn_ref(x, Wq, Wkv_down, Wk_up, Wv_up, Wo):
        import jax, jax.numpy as jnp
        import numpy as np
        B, T = (4, 256)
        D_MODEL = 128
        N_HEADS = 8
        HEAD_DIM = 32
        KV_LRANK = 64

        def _orthogonalize_per_head(w):
            chunks = w.reshape(N_HEADS, HEAD_DIM, D_MODEL)

            def ns(m):
                A = m @ m.T
                Bm = 1.5 * jnp.eye(HEAD_DIM, dtype=m.dtype) - 0.5 * A
                return Bm @ m
            return jax.vmap(ns)(chunks).reshape(w.shape)
        b, t, _ = x.shape
        q = (x @ Wq.T).reshape(b, t, N_HEADS, HEAD_DIM)
        kv_latent = x @ Wkv_down.T
        k = (kv_latent @ Wk_up.T).reshape(b, t, N_HEADS, HEAD_DIM)
        v = (kv_latent @ Wv_up.T).reshape(b, t, N_HEADS, HEAD_DIM)
        scale = HEAD_DIM ** (-0.5)
        scores = jnp.einsum('bqhd,bkhd->bhqk', q, k) * scale
        attn = jax.nn.softmax(scores, axis=-1)
        out = jnp.einsum('bhqk,bkhd->bqhd', attn, v)
        out = out.reshape(b, t, N_HEADS * HEAD_DIM)
        return out @ Wo.T

    def _L1_ffn_ref(x, wqkv, q_scale, k_scale, wo, ln_g, ln_b, w1, b1, w2, b2):
        import jax, jax.numpy as jnp
        import numpy as np
        DIM = 128
        DEPTH = 2
        HEADS = 8
        DIM_HEAD = 64
        WINDOW = 64
        INNER = HEADS * DIM_HEAD
        HID = int(DIM * 4 * 2 / 3)
        B, N = (2, 1024)
        QK_SCALE = 8.0

        def shift_token(t):
            t1, t2 = jnp.split(t, 2, axis=-1)
            t2 = jnp.pad(t2, ((0, 0), (1, 0), (0, 0)))[:, :-1]
            return jnp.concatenate([t1, t2], axis=-1)

        def l2norm(t):
            return t / jnp.clip(jnp.linalg.norm(t, axis=-1, keepdims=True), 1e-12)

        def rotate_half(x):
            x1, x2 = jnp.split(x, 2, axis=-1)
            return jnp.concatenate([-x2, x1], axis=-1)

        def rotary_xpos(q, k):
            n = q.shape[-2]
            half_idx = jnp.arange(0, DIM_HEAD, 2, dtype=jnp.float32)
            inv_freq = 1.0 / 10000.0 ** (half_idx / DIM_HEAD)
            t = jnp.arange(n, dtype=jnp.float32)
            freqs = t[:, None] * inv_freq[None, :]
            freqs = jnp.concatenate([freqs, freqs], axis=-1)
            base = (half_idx + 0.4 * DIM_HEAD) / (1.4 * DIM_HEAD)
            power = (t - n // 2) / float(WINDOW // 2)
            scale = base[None, :] ** power[:, None]
            scale = jnp.concatenate([scale, scale], axis=-1)
            cos, sin = (jnp.cos(freqs), jnp.sin(freqs))
            q = q * cos * scale + rotate_half(q) * sin * scale
            k = k * cos / scale + rotate_half(k) * sin / scale
            return (q, k)

        def local_attention(q, k, v):
            b, h, n, d = q.shape
            w = n // WINDOW
            bq = q.reshape(b, h, w, WINDOW, d) * QK_SCALE
            bk = k.reshape(b, h, w, WINDOW, d)
            bv = v.reshape(b, h, w, WINDOW, d)

            def look_around(t):
                p = jnp.pad(t, ((0, 0), (0, 0), (1, 0), (0, 0), (0, 0)))
                return jnp.concatenate([p[:, :, :w], p[:, :, 1:]], axis=3)
            bk, bv = (look_around(bk), look_around(bv))
            bt = jnp.arange(n).reshape(w, WINDOW)
            btp = jnp.pad(bt, ((1, 0), (0, 0)), constant_values=-1)
            btk = jnp.concatenate([btp[:w], btp[1:]], axis=1)
            sim = jnp.einsum('bhwid,bhwjd->bhwij', bq, bk)
            i = bt[:, :, None]
            j = btk[:, None, :]
            mask = (i < j) | (i > j + WINDOW) | (j == -1)
            sim = jnp.where(mask, -jnp.finfo(sim.dtype).max, sim)
            attn = jax.nn.softmax(sim, axis=-1)
            out = jnp.einsum('bhwij,bhwjd->bhwid', attn, bv)
            return out.reshape(b, h, n, d)

        def _layer(x, wqkv, qs, ksc, wo, lg, lb, w1, b1, w2, b2):
            b, n, _ = x.shape
            h = shift_token(x)
            qkv = h @ wqkv
            q, k, v = jnp.split(qkv, 3, axis=-1)
            to_heads = lambda t: t.reshape(b, n, HEADS, DIM_HEAD).transpose(0, 2, 1, 3)
            q, k, v = (to_heads(q), to_heads(k), to_heads(v))
            q = l2norm(q) * qs
            k = l2norm(k) * ksc
            q, k = rotary_xpos(q, k)
            o = local_attention(q, k, v)
            o = o.transpose(0, 2, 1, 3).reshape(b, n, INNER)
            x = x + o @ wo
            h = shift_token(x)
            mu = h.mean(-1, keepdims=True)
            var = h.var(-1, keepdims=True)
            h = (h - mu) / jnp.sqrt(var + 1e-05) * lg + lb
            h = h @ w1 + b1
            a, g = jnp.split(h, 2, axis=-1)
            h = a * jax.nn.gelu(g, approximate=False)
            x = x + h @ w2 + b2
            return x
        for l in range(DEPTH):
            x = _layer(x, wqkv[l], q_scale[l], k_scale[l], wo[l], ln_g[l], ln_b[l], w1[l], b1[l], w2[l], b2[l])
        return x

    def _L2_attn_ref(x, rby, Wq, bq, Wk, bk, Wv, bv, Wo, bo, ln_gamma, ln_beta):
        import jax, jax.numpy as jnp
        import numpy as np
        import math
        D_MODEL = 128
        N_HEADS = 16
        D_K = D_MODEL // N_HEADS
        BATCH = 4
        SEQ = 256
        TRAINING_PROGRESS = 0.25
        CONVERGENCE_PHASE = 0.5
        TENSION = abs(1.0 - 1.0)

        def _pos_encoding(seq_len, d, yellow):
            phase_mod = 0.1 * math.sin(2.0 * math.pi * TRAINING_PROGRESS)
            i_even = jnp.arange(0, d, 2, dtype=jnp.float32)
            denom = jnp.power(10000.0, 2.0 * i_even / d) * (1.0 + yellow * phase_mod)
            pos = jnp.arange(seq_len, dtype=jnp.float32)
            ang = pos[:, None] / denom[None, :]
            pe = jnp.zeros((seq_len, d), jnp.float32)
            pe = pe.at[:, 0::2].set(jnp.sin(ang))
            pe = pe.at[:, 1::2].set(jnp.cos(ang))
            return pe
        B, S, d = x.shape
        red, blue, yellow = (rby[0], rby[1], rby[2])
        x = x + _pos_encoding(S, d, yellow)[None, :, :]

        def proj(W, b):
            return (x @ W.T + b).reshape(B, S, N_HEADS, D_K).transpose(0, 2, 1, 3)
        Q, K, V = (proj(Wq, bq), proj(Wk, bk), proj(Wv, bv))
        scale = jnp.sqrt(D_K * (1.0 + TENSION * red))
        logits = jnp.einsum('bhqd,bhkd->bhqk', Q, K) / scale
        scale_matrix = 1.0 + red * 0.1 + blue * 0.05 + yellow * 0.15
        logits = logits * scale_matrix
        attn = jax.nn.softmax(logits, axis=-1)
        eps_adaptive = 0.1 * math.sin(2.0 * math.pi * CONVERGENCE_PHASE)
        out = jnp.einsum('bhqk,bhkd->bhqd', attn, V) * (1.0 + yellow * eps_adaptive)
        out = out.transpose(0, 2, 1, 3).reshape(B, S, d)
        out = out @ Wo.T + bo
        x = x + out
        mean = jnp.mean(x, axis=-1, keepdims=True)
        var = jnp.var(x, axis=-1, keepdims=True)
        eps_rby = 1e-05 * (1.0 + blue * 0.1)
        gamma_rby = ln_gamma * (1.0 + red * 0.1 + yellow * 0.05)
        normalized = (x - mean) / jnp.sqrt(var + eps_rby)
        return normalized * gamma_rby + ln_beta

    def _L2_ffn_ref(x, w1_w, w1_s, w2_w, w2_s, h1_w, h1_s, h2_w, h2_s, w3_w, w3_s):
        import jax, jax.numpy as jnp
        import numpy as np
        D_IN, D_HID = (128, 512)

        def _ternary(key, shape):
            return jax.random.randint(key, shape, -1, 2).astype(jnp.float32)

        def _tlin(x, w, s):
            return jnp.einsum('bsi,oi->bso', x, w) * s
        h = jax.nn.silu(_tlin(x, w1_w, w1_s)) * _tlin(x, w2_w, w2_s)
        h = jax.nn.gelu(_tlin(h, h1_w, h1_s), approximate=False)
        h = jax.nn.gelu(_tlin(h, h2_w, h2_s), approximate=False)
        return _tlin(h, w3_w, w3_s)

    def _L3_attn_ref(x, lnq_s, lnq_b, Wq, bq, lnk_s, lnk_b, Wk, bk, lnv_s, lnv_b, Wv, bv, Wo, bo, lnm_s, lnm_b, W1, b1, W2, b2):
        import jax, jax.numpy as jnp
        import numpy as np
        D = 128
        H = 16
        HD = 64
        AHD = H * HD
        B = 4
        S = 128
        EPS = 1e-05
        SMAX = float(D) ** 0.5

        def _ln(x, s, b):
            mu = jnp.mean(x, axis=-1, keepdims=True)
            var = jnp.mean(jnp.square(x - mu), axis=-1, keepdims=True)
            return (x - mu) * jax.lax.rsqrt(var + EPS) * s + b

        def _forward(x, lnq_s, lnq_b, Wq, bq, lnk_s, lnk_b, Wk, bk, lnv_s, lnv_b, Wv, bv, Wo, bo, lnm_s, lnm_b, W1, b1, W2, b2):
            Bq, Sq, _ = x.shape
            q = (_ln(x, lnq_s, lnq_b) @ Wq + bq).reshape(Bq, Sq, H, HD).transpose(0, 2, 1, 3)
            k = (_ln(x, lnk_s, lnk_b) @ Wk + bk).reshape(Bq, Sq, H, HD).transpose(0, 2, 1, 3)
            v = (_ln(x, lnv_s, lnv_b) @ Wv + bv).reshape(Bq, Sq, H, HD).transpose(0, 2, 1, 3)
            scores = jnp.einsum('bhqd,bhkd->bhqk', q, k) / SMAX
            mask = jnp.triu(jnp.full((Sq, Sq), -999.0, dtype=scores.dtype), k=Sq - 1)
            p = jax.nn.softmax(scores + mask, axis=-1)
            att = jnp.einsum('bhqk,bhkd->bhqd', p, v).transpose(0, 2, 1, 3).reshape(Bq, Sq, AHD)
            h = att @ Wo + bo + x
            y = _ln(h, lnm_s, lnm_b)
            m = jax.nn.gelu(y @ W1 + b1) @ W2 + b2
            return m + h
        return _forward(x, lnq_s, lnq_b, Wq, bq, lnk_s, lnk_b, Wk, bk, lnv_s, lnv_b, Wv, bv, Wo, bo, lnm_s, lnm_b, W1, b1, W2, b2)

    def _L3_ffn_ref(x, gamma_x, gamma_slot, slot_embeds, w1, w2):
        import jax, jax.numpy as jnp
        import numpy as np
        EPS = 1e-12

        def rms_norm(t, gamma):
            n = jnp.maximum(jnp.linalg.norm(t, axis=-1, keepdims=True), EPS)
            scale = jnp.sqrt(jnp.asarray(t.shape[-1], t.dtype))
            return t / n * scale * gamma
        b, s, d = x.shape
        e, t, _ = slot_embeds.shape
        xn = rms_norm(x, gamma_x)
        se = rms_norm(slot_embeds, gamma_slot)
        logits = jnp.einsum('bsd,etd->bset', xn, se)
        dispatch = jax.nn.softmax(logits, axis=1)
        slots = jnp.einsum('bsd,bset->betd', xn, dispatch)
        h = jax.nn.gelu(slots @ w1, approximate=False)
        processed = h @ w2
        combine = jax.nn.softmax(logits.reshape(b, s, e * t), axis=-1)
        out = jnp.einsum('bnd,bsn->bsd', processed.reshape(b, e * t, d), combine)
        return out
    x = L0_attn_x
    xn = _layernorm(x, axis=-1)
    s = _L0_attn_ref(xn, L0_attn_w_q, L0_attn_w_kv, L0_attn_w_out)
    g = _silu(_L0_ffn_ref(xn, L0_ffn_w_gate, L0_ffn_w_up, L0_ffn_w_down))
    x = x + s * g
    xn = _layernorm(x, axis=-1)
    s = _L1_attn_ref(xn, L1_attn_Wq, L1_attn_Wkv_down, L1_attn_Wk_up, L1_attn_Wv_up, L1_attn_Wo)
    g = _silu(_L1_ffn_ref(xn, L1_ffn_wqkv, L1_ffn_q_scale, L1_ffn_k_scale, L1_ffn_wo, L1_ffn_ln_g, L1_ffn_ln_b, L1_ffn_w1, L1_ffn_b1, L1_ffn_w2, L1_ffn_b2))
    x = x + s * g
    xn = _layernorm(x, axis=-1)
    s = _L2_attn_ref(xn, L2_attn_rby, L2_attn_Wq, L2_attn_bq, L2_attn_Wk, L2_attn_bk, L2_attn_Wv, L2_attn_bv, L2_attn_Wo, L2_attn_bo, L2_attn_ln_gamma, L2_attn_ln_beta)
    g = _silu(_L2_ffn_ref(xn, L2_ffn_w1_w, L2_ffn_w1_s, L2_ffn_w2_w, L2_ffn_w2_s, L2_ffn_h1_w, L2_ffn_h1_s, L2_ffn_h2_w, L2_ffn_h2_s, L2_ffn_w3_w, L2_ffn_w3_s))
    x = x + s * g
    xn = _layernorm(x, axis=-1)
    s = _L3_attn_ref(xn, L3_attn_lnq_s, L3_attn_lnq_b, L3_attn_Wq, L3_attn_bq, L3_attn_lnk_s, L3_attn_lnk_b, L3_attn_Wk, L3_attn_bk, L3_attn_lnv_s, L3_attn_lnv_b, L3_attn_Wv, L3_attn_bv, L3_attn_Wo, L3_attn_bo, L3_attn_lnm_s, L3_attn_lnm_b, L3_attn_W1, L3_attn_b1, L3_attn_W2, L3_attn_b2)
    g = _silu(_L3_ffn_ref(xn, L3_ffn_gamma_x, L3_ffn_gamma_slot, L3_ffn_slot_embeds, L3_ffn_w1, L3_ffn_w2))
    x = x + s * g
    return x

_drawn_inputs = setup_inputs


def setup_inputs(seed=0):
    import zlib

    import numpy as np

    out = dict(_drawn_inputs(seed))
    spreads = {'L1_ffn_q_scale': (1.0, 0.2),
     'L1_ffn_k_scale': (1.0, 0.2),
     'L1_ffn_ln_g': (1.0, 0.2),
     'L1_ffn_ln_b': (0.0, 0.1),
     'L1_ffn_b1': (0.0, 0.1),
     'L1_ffn_b2': (0.0, 0.1),
     'L2_attn_bq': (0.0, 0.1),
     'L2_attn_bk': (0.0, 0.1),
     'L2_attn_bv': (0.0, 0.1),
     'L2_attn_bo': (0.0, 0.1),
     'L2_attn_ln_gamma': (1.0, 0.2),
     'L2_attn_ln_beta': (0.0, 0.1),
     'L3_attn_lnq_s': (1.0, 0.2),
     'L3_attn_lnq_b': (0.0, 0.1),
     'L3_attn_lnk_s': (1.0, 0.2),
     'L3_attn_lnk_b': (0.0, 0.1),
     'L3_attn_lnv_s': (1.0, 0.2),
     'L3_attn_lnv_b': (0.0, 0.1),
     'L3_attn_lnm_s': (1.0, 0.2),
     'L3_attn_lnm_b': (0.0, 0.1),
     'L3_ffn_gamma_x': (1.0, 0.2),
     'L3_ffn_gamma_slot': (1.0, 0.2)}
    factors = {}
    for name, (base, spread) in spreads.items():
        noise = np.random.default_rng([zlib.crc32(name.encode()), seed]).standard_normal(out[name].shape)
        drawn = base * np.exp(spread * noise) if base else spread * noise
        out[name] = jnp.asarray(drawn.astype(out[name].dtype))
    for name, factor in factors.items():
        out[name] = (out[name] * factor).astype(out[name].dtype)
    return out
```

```python
from contextlib import ExitStack

import numpy as np

import concourse.bass as bass
from concourse import mybir

F32 = mybir.dt.float32
F32R = mybir.dt.float32r
BF16 = mybir.dt.bfloat16
I32 = mybir.dt.int32
ACT = mybir.ActivationFunctionType
ALU = mybir.AluOpType
AX = mybir.AxisListType

P = 128
T = 2048
NT = T // P
D = 128
BANK = 512
KC = 512
NEG = -1.0e30


class Queue:

    def __init__(self, nc, engine, name):
        self.e = engine
        self.sem = nc.alloc_semaphore("done_" + name)
        self.count = 0
        self.seen = {}

    def done(self, ins):
        ins.then_inc(self.sem, 1)
        self.count += 1
        return (self.sem, self.count)

    def wait(self, *tickets):
        for t in tickets:
            if t is not None and self.seen.get(t[0].num, 0) < t[1]:
                self.e.wait_ge(t[0], t[1])
                self.seen[t[0].num] = t[1]


class Loads:

    def __init__(self, nc, name):
        self.sem = nc.alloc_semaphore("loaded_" + name)
        self.count = 0

    def add(self, ins):
        ins.then_inc(self.sem, 16)
        self.count += 16

    def all(self):
        return (self.sem, self.count)


class Core:

    def __init__(self, nc, ctx):
        self.nc = nc
        self.ctx = ctx
        self.pe = Queue(nc, nc.tensor, "pe")
        self.act = Queue(nc, nc.scalar, "act")
        self.dve = Queue(nc, nc.vector, "dve")
        self.pool = Queue(nc, nc.gpsimd, "pool")
        self.sp = Queue(nc, nc.sync, "sp")
        self.loads = Loads(nc, "all")
        self.stores = Loads(nc, "out")
        self.queues = [self.pe, self.act, self.dve, self.pool, self.sp]
        self.counts = [q.sem for q in self.queues] + [self.loads.sem, self.stores.sem]

    def barrier(self):
        if self.loads.count:
            self.sp.wait(self.loads.all())
        nums = [s.num for s in self.counts]
        assert nums == list(range(nums[0], nums[0] + len(nums)))
        self.nc.all_engine_barrier(sems_to_clear=range(nums[0], nums[0] + len(nums)))
        for q in self.queues:
            q.count = 0
            q.seen = {}
        self.loads.count = 0
        self.stores.count = 0

    def load(self, out, in_, queue=None):
        q = queue or self.sp
        self.loads.add(q.e.dma_start(out, in_))


def free(ap):
    return ap.bitcast(F32)


class Attention:

    def __init__(self, core, psum, name, heads, hd, causal=False, last_key_mask=False, scale=1.0):
        self.scale = scale
        self.c = core
        self.name = name
        self.hd = hd
        self.wide = hd == 64
        self.G = 4 if hd == 8 else 2
        self.M = P // self.G
        self.groups = heads // self.G
        self.QC = 1024 // self.G
        self.nchunk = T // self.QC
        self.qt = self.QC // P
        self.causal = causal
        self.last_key_mask = last_key_mask
        self.row = 64 if self.wide else 96
        self.rows = P if self.wide else 96
        self.psum = psum
        ctx, nc = core.ctx, core.nc
        sb = lambda n, s, d: ctx.enter_context(nc.sbuf_tensor(name + "_" + n, s, d))
        G = self.G
        self.Ka = [sb(f"Ka{h}", [P, T], F32R) for h in range(G)]
        self.Qa = [sb(f"Qa{h}", [P, T], F32R) for h in range(G)]
        self.Kb = [sb(f"Kb{h}", [P, T], F32R) for h in range(G)] if self.wide else self.Ka
        self.Qb = [sb(f"Qb{h}", [P, T], F32R) for h in range(G)] if self.wide else self.Qa
        self.V = sb("V", [P, NT, G, self.M], F32)
        self.W = [sb(f"weights{i}", [P, 1024], F32) for i in range(4)]
        self.wsum = [sb(f"wsum{i}", [P, 1024], F32) for i in range(2)] if self.wide else None
        self.Wo = sb("Wo", [P, G // 2, 258], F32)
        self.OT = [sb(f"OT{i}", [P, self.QC], F32) for i in range(2)]
        self.stage = [sb(f"stage{i}", [P, BANK], F32) for i in range(3)]
        self.part = [sb(f"part{i}", [P, G, self.qt, T // KC], F32) for i in range(2)]
        self.negmax = [sb(f"negmax{i}", [P, G, self.qt], F32) for i in range(2)]
        self.rden = [sb(f"rden{i}", [P, 2], F32) for i in range(2)]
        self.zero = sb("zero", [P, BANK], F32)

    def once(self):
        c, nc = self.c, self.c.nc
        dve = c.dve
        z = dve.done(dve.e.memset(self.zero[:, :], 0.0))
        z1 = dve.done(dve.e.memset(self.stage[0][:, :], 1.0))
        dve.wait(z, z1)
        lo = self.row
        for h in range(self.G):
            for t in (self.Kb[h], self.Qb[h]):
                for b in range(T // BANK):
                    s = slice(b * BANK, (b + 1) * BANK)
                    f = dve.done(dve.e.tensor_copy(t[lo:P, s], self.zero[lo:P, :]))
            dve.wait(f)
            for b in range(T // BANK):
                dve.done(dve.e.tensor_copy(self.Kb[h][lo:lo + 1, b * BANK:(b + 1) * BANK], self.stage[0][lo:lo + 1, :]))
        v = c.pool.done(c.pool.e.memset(self.V[:, :, :, :], 0.0))
        w = c.pool.done(c.pool.e.memset(self.Wo[:, :, :], 0.0))
        c.pool.wait(v, w)
        if not self.wide:
            v = c.pool.done(c.pool.e.memset(self.V[:, :, :, self.hd:self.hd + 1], 1.0))
            for j in range(self.G // 2):
                for i in range(2):
                    h = 2 * j + i
                    r = h * self.M + self.hd
                    c.dve.wait(w)
                    c.dve.done(c.dve.e.tensor_copy(self.Wo[:, j, 129 * i + 128:129 * i + 129], self.c.ident[:, r:r + 1]))
        c.barrier()

    def project(self, g):
        c = self.c
        pe, act, dve, pool = c.pe, c.act, c.dve, c.pool
        S = self.psum.S
        R = self.rows
        slot = [None] * 4
        staged = [()] * 3
        high = None
        n = 0
        k = 0
        self.turned_read = [None, None]
        pe.wait(c.loads.all())
        act.wait(c.loads.all())
        for h in range(self.G):
            for which in (0, 1):
                for b in range(T // BANK):
                    s = slice(b * BANK, (b + 1) * BANK)
                    st = self.stage[k % 3]
                    cols = []
                    for w, src, K in self.proj(h, which):
                        bank = n % 4
                        n += 1
                        ps = S[:, bank * BANK:(bank + 1) * BANK]
                        pe.wait(slot[bank])
                        made = pe.done(pe.e.matmul(ps[0:R, :], w[0:K, 0:R], src[0:K, s], start=True, stop=True))
                        cols.append((bank, ps, made))
                    act.wait(*staged[k % 3])
                    dve.wait(*staged[k % 3])
                    if len(cols) == 1:
                        bank, ps, made = cols[0]
                        scale, bias = self.affine(h, which)
                        act.wait(made)
                        got = slot[bank] = act.done(act.e.activation(st[0:R, :], ps[0:R, :], ACT.Identity, scale=scale, bias=bias))
                    else:
                        cosT, sinT = self.rotary(which)
                        (b0, p0, m0), (b1, p1, m1) = cols
                        turned = self.turned[k % 2]
                        dve.wait(m0, m1, self.turned_read[k % 2])
                        slot[b0] = dve.done(dve.e.tensor_tensor(st[:, :], p0[:, :], cosT[:, s], ALU.mult))
                        slot[b1] = dve.done(dve.e.tensor_tensor(turned[:, :], p1[:, :], sinT[:, s], ALU.mult))
                        pool.wait(slot[b0], slot[b1])
                        got = self.turned_read[k % 2] = pool.done(pool.e.tensor_tensor(st[:, :], st[:, :], turned[:, :], ALU.add))
                    dve.wait(got)
                    Xa = self.Ka[h] if which == 0 else self.Qa[h]
                    hi = dve.done(dve.e.tensor_copy(Xa[0:R, s], st[0:R, :]))
                    dve.wait(hi)
                    if self.wide and which == 0:
                        act.wait(got)
                        high = act.done(act.e.activation(self.Kb[h][0:64, s], st[0:64, :], ACT.Copy))
                        last = dve.done(dve.e.tensor_tensor(Xa[64:P, s], st[64:P, :], free(Xa[64:P, s]), ALU.subtract))
                    elif self.wide:
                        last = dve.done(dve.e.tensor_tensor(self.Qb[h][0:64, s], st[0:64, :], free(Xa[0:64, s]), ALU.subtract))
                    else:
                        q = slice(32, 64) if which == 0 else slice(64, 96)
                        last = dve.done(dve.e.tensor_tensor(Xa[q, s], st[q, :], free(Xa[q, s]), ALU.subtract))
                    staged[k % 3] = (last, high)
                    k += 1
        self.split = (last, high)
        hd, G = self.hd, self.G
        src, K = self.vsrc()
        for b in range(NT // 4):
            bank = n % 4
            n += 1
            ps = S[:, bank * BANK:(bank + 1) * BANK]
            pe.wait(slot[bank])
            for j in range(4):
                kt = 4 * b + j
                o = ps[:, j * P:j * P + G * hd]
                mm = pe.e.matmul(o, src[0:K, kt * P:(kt + 1) * P], self.Wv[0:K, 0:G * hd], start=True, stop=self.vbias is None)
                if self.vbias is not None:
                    mm = pe.e.matmul(o, c.onerow[:, 0:P], self.vbias[:, 0:G * hd], start=False, stop=True)
            made = pe.done(mm)
            act.wait(made)
            view = ps.rearrange("p (t x) -> p t x", t=4)
            for h in range(G):
                slot[bank] = act.done(act.e.activation(self.V[:, 4 * b:4 * b + 4, h, 0:hd], view[:, :, h * hd:(h + 1) * hd], ACT.Copy))
        self.vmade = slot[bank]
        self.slot = slot

    def attend(self, g):
        c = self.c
        pe, act, dve, pool = c.pe, c.act, c.dve, c.pool
        S, MX, O, Y = self.psum.S, self.psum.MX, self.psum.O, self.psum.Y
        G, QC, qt, M = self.G, self.QC, self.qt, self.M
        K0 = self.rows

        mxread = [None, None]
        mxn = [0]

        def pieces(ch):
            out = []
            for h in range(G):
                for j in range(qt):
                    tile = ch * qt + j
                    n = tile // 4 + 1 if self.causal else T // KC
                    out += [(h, j, tile, p, n) for p in range(n)]
            return out

        def piece(ch, h, j, tile, p, n):
            i = mxn[0] % 2
            mxn[0] += 1
            ps = MX[:, i * BANK:(i + 1) * BANK]
            q = slice(tile * P, (tile + 1) * P)
            kk = slice(p * KC, (p + 1) * KC)
            extra = []
            if self.causal and p == tile // 4:
                extra = [(c.identb, c.maskq[:, tile % 4, :], slice(0, KC))]
            if self.last_key_mask and tile == 0 and p == T // KC - 1:
                extra = [(c.identb, c.lastq[:, 0, :], slice(KC - P, KC)), (c.identb, c.lastq[:, 1, :], slice(KC - P, KC))]
            pe.wait(mxread[i])
            mm = pe.e.matmul(ps, self.Qa[h][0:K0, q], self.Ka[h][0:K0, kk], start=True, stop=not extra)
            for a, b, w in extra:
                mm = pe.e.matmul(ps[:, w], a[:, :], b, start=False, stop=b is extra[-1][1])
            made = pe.done(mm)
            dve.wait(made)
            mxread[i] = dve.done(dve.e.tensor_reduce(self.part[ch % 2][:, h, j, p:p + 1], ps, AX.X, ALU.max))

        rowread = [None, None]
        self.shifted = {}

        def shift(ch):
            n = [(ch * qt + j) // 4 + 1 if self.causal else T // KC for j in range(qt)]
            dve.wait(mxread[0], mxread[1])
            if len(set(n)) == 1:
                m = dve.done(dve.e.tensor_reduce(self.negmax[ch % 2][:, :, :], self.part[ch % 2][:, :, :, 0:n[0]], AX.X, ALU.max, negate=True))
            r = self.row
            pe.wait(m, mxread[0], mxread[1])
            for h in range(G):
                for j in range(qt):
                    o = (h * qt + j) * P
                    mm = pe.e.matmul(MX[r:r + 1, o:o + P], self.negmax[ch % 2][:, h, j:j + 1], c.ident[:, :], start=True, stop=True)
            made = pe.done(mm)
            act.wait(made, *self.split)
            for h in range(G):
                t = act.done(act.e.activation(self.Qb[h][r:r + 1, ch * QC:(ch + 1) * QC], MX[r:r + 1, h * QC:(h + 1) * QC], ACT.Copy))
            mxread[0] = mxread[1] = t
            self.shifted[ch] = t

        steps = []
        for ch in range(self.nchunk):
            nk = (ch + 1) * qt if self.causal else NT
            steps += [(ch, kt, nk) for kt in range(nk)]
        exped = {}
        used = {}
        summed = {}

        def scores(s):
            ch, kt, nk = steps[s]
            buf = S[:, (s % 2) * 1024:(s % 2) * 1024 + 1024]
            pe.wait(exped.get(s - 2), self.shifted[ch])
            if s < 2:
                pe.wait(*self.slot)
            kk = slice(kt * P, (kt + 1) * P)
            qq = slice(ch * QC, (ch + 1) * QC)
            for h in range(G):
                o = buf[:, h * QC:(h + 1) * QC]
                extra = []
                if self.causal and kt >= ch * qt:
                    extra = [(c.identb, c.maskk[:, kt - ch * qt, :], slice(0, QC))]
                if self.last_key_mask and ch == 0 and kt == NT - 1:
                    extra = [(c.identb, c.lastk[:, 0, :], slice(0, P)), (c.identb, c.lastk[:, 1, :], slice(0, P))]
                mm = pe.e.matmul(o, self.Ka[h][:, kk], self.Qa[h][:, qq], start=True, stop=not (self.wide or extra))
                if self.wide:
                    mm = pe.e.matmul(o, self.Kb[h][:, kk], self.Qb[h][:, qq], start=False, stop=not extra)
                for a, b, w in extra:
                    mm = pe.e.matmul(o[:, w], a[:, :], b, start=False, stop=b is extra[-1][1])
            made = pe.done(mm)
            w = self.W[s % 4]
            act.wait(made, *used.get(s - 4, ()))
            exped[s] = act.done(act.e.activation(w[:, :], buf, ACT.Exp, scale=self.scale))

        def sums(s):
            ch, kt, nk = steps[s]
            if not self.wide or kt == 0:
                return ()
            acc = self.wsum[ch % 2]
            a = self.W[(s - 1) % 4] if kt == 1 else acc
            pool.wait(exped[s], summed.get(s - 1), self.ydone.get(ch - 2))
            summed[s] = pool.done(pool.e.tensor_tensor(acc[:, :], a[:, :], self.W[s % 4][:, :], ALU.add))
            return (summed[s],)

        otcopied = {}
        self.ydone = {}

        def values(s):
            ch, kt, nk = steps[s]
            pe.wait(exped[s])
            if kt == 0:
                pe.wait(self.vmade, otcopied.get(ch - 1))
            for h in range(G):
                mm = pe.e.matmul(O[h * M:(h + 1) * M, 0:QC], self.V[:, kt, h, :], self.W[s % 4][:, h * QC:(h + 1) * QC], start=kt == 0, stop=kt == nk - 1)
            t = pe.done(mm)
            used[s] = (t,)
            p = sums(s)
            used[s] += p
            if self.wide and kt == 1:
                used[s - 1] += p
            if kt == nk - 1:
                act.wait(t, self.ydone.get(ch - 2))
                otcopied[ch] = act.done(act.e.activation(self.OT[ch % 2][:, :], O[:, 0:QC], ACT.Copy))

        yread = [None]
        acc = self.c.SACC

        def unit(ch, s_last, j, half):
            tile = ch * qt + j
            pe.wait(otcopied[ch], yread[0], summed.get(s_last))
            mm = pe.e.matmul(Y[:, 0:258], self.OT[ch % 2][:, j * P:(j + 1) * P], self.Wo[:, half, :], start=True, stop=True)
            if self.wide:
                for i in range(2):
                    mm = pe.e.matmul(Y[:, 258 + i:259 + i], self.wsum[ch % 2][:, i * QC + j * P:i * QC + (j + 1) * P], c.ones[:, 0:1], start=True, stop=True)
            made = pe.done(mm)
            u = self.un % 2
            self.un += 1
            dve.wait(made)
            den = Y[:, 258:260] if self.wide else Y[:, 128:258:129]
            r = dve.done(dve.e.reciprocal(self.rden[u][:, :], den))
            dve.wait(r, self.accw.get(tile))
            a = dve.done(dve.e.scalar_tensor_tensor(acc[:, tile, :], Y[:, 0:128], self.rden[u][:, 0:1], acc[:, tile, :], ALU.mult, ALU.add))
            dve.wait(a)
            yread[0] = self.accw[tile] = dve.done(dve.e.scalar_tensor_tensor(acc[:, tile, :], Y[:, 129:257], self.rden[u][:, 1:2], acc[:, tile, :], ALU.mult, ALU.add))
            self.ydone[ch] = made

        self.un = 0
        self.accw = {}
        pe.wait(*self.split)
        for a in pieces(0):
            piece(0, *a)
        shift(0)
        scores(0)
        units = []
        s = 0
        for ch in range(self.nchunk):
            nk = steps[s][2]
            todo = pieces(ch + 1) if ch + 1 < self.nchunk else []
            per = -(-len(todo) // (nk - 1))
            for kt in range(nk):
                if todo:
                    for a in todo[:per]:
                        piece(ch + 1, *a)
                    todo = todo[per:]
                if kt == nk - 1 and ch + 1 < self.nchunk:
                    shift(ch + 1)
                if s + 1 < len(steps):
                    scores(s + 1)
                values(s)
                for _ in range(1 if nk > 4 else 2):
                    if units:
                        unit(*units.pop(0))
                s += 1
            while units:
                unit(*units.pop(0))
            units = [(ch, s - 1, j, half) for j in range(qt) for half in range(G // 2)]
        while units:
            unit(*units.pop(0))


class RotaryAttention(Attention):

    def __init__(self, core, psum, io):
        super().__init__(core, psum, "L0", 16, 64, causal=True, scale=64 ** -0.5)
        c, nc, ctx = core, core.nc, core.ctx
        self.io = io
        sb = lambda n, s, d=F32: ctx.enter_context(nc.sbuf_tensor("L0_" + n, s, d))
        self.w = [[sb(f"w{h}{x}", [P, P]) for x in "kq"] for h in range(2)]
        self.wturned = [[sb(f"wt{h}{x}", [P, P]) for x in "kq"] for h in range(2)]
        self.Wv = sb("Wv", [P, P])
        self.cosT = sb("cos", [P, T])
        self.sinT = sb("sin", [P, T])
        self.turned = [sb(f"turned{i}", [P, BANK]) for i in range(2)]
        self.vbias = None
        core.load(self.cosT[:, :], io["rope_cos"])
        core.load(self.sinT[:, :], io["rope_sin"])
        for h in range(2):
            for x in range(2):
                core.pool.done(nc.gpsimd.memset(self.wturned[h][x][:, :], 0.0))
        self.once()

    def load(self, g):
        c, io = self.c, self.io
        kv = io["L0_attn_w_kv"]
        for h in range(2):
            for x, src in enumerate((kv, io["L0_attn_w_q"])):
                w = src[:, bass.ds(g * P + h * 64, 64)]
                turned0 = src[:, bass.ds(g * P + h * 64 + 16, 16)]
                turned1 = src[:, bass.ds(g * P + h * 64, 16)]
                for half in (0, 64):
                    c.load(self.w[h][x][:, half:half + 64], w)
                    c.load(self.wturned[h][x][:, half:half + 16], turned0)
                    c.load(self.wturned[h][x][:, half + 16:half + 32], turned1)
            wo = io["L0_attn_w_out"][bass.ds(g * P + h * 64, 64), :]
            c.load(self.Wo[h * 64:h * 64 + 64, 0, 129 * h:129 * h + 128], wo)
        c.load(self.Wv[:, :], kv[:, bass.ds(g * P + 1024, P)])

    def proj(self, h, which):
        return [(self.w[h][which], self.c.XNT, P), (self.wturned[h][which], self.c.XNT, P)]

    def rotary(self, which):
        return self.cosT, self.sinT

    def vsrc(self):
        return self.c.XNT, P


class LatentAttention(Attention):

    def __init__(self, core, psum, io):
        super().__init__(core, psum, "L1", 8, 32, scale=32 ** -0.5)
        c, nc, ctx = core, core.nc, core.ctx
        self.io = io
        sb = lambda n, s, d=F32: ctx.enter_context(nc.sbuf_tensor("L1_" + n, s, d))
        self.w = [[sb(f"w{h}{x}", [P, 96]) for x in "kq"] for h in range(2)]
        self.Wv = sb("Wv", [64, 64])
        self.down = sb("down", [P, 64])
        self.latent = sb("latent", [64, T])
        self.vbias = None
        core.load(self.down[:, :], io["L1_attn_Wkv_down"])
        c.pe.wait(c.loads.all())
        for b in range(4):
            s = slice(b * BANK, (b + 1) * BANK)
            ps = psum.S[0:64, s]
            made = c.pe.done(c.pe.e.matmul(ps, self.down[:, :], c.XNT[:, s], start=True, stop=True))
            c.act.wait(made)
            c.act.done(c.act.e.activation(self.latent[:, s], ps, ACT.Copy))
        self.once()

    def load(self, g):
        c, io = self.c, self.io
        for h in range(2):
            for third in range(3):
                s = slice(32 * third, 32 * third + 32)
                c.load(self.w[h][0][0:64, s], io["L1_attn_Wk_up"][:, bass.ds(g * 64 + h * 32, 32)])
                c.load(self.w[h][1][:, s], io["L1_attn_Wq"][:, bass.ds(g * 64 + h * 32, 32)])
            c.load(self.Wo[h * 64:h * 64 + 32, 0, 129 * h:129 * h + 128], io["L1_attn_Wo"][bass.ds(g * 64 + h * 32, 32), :])
        c.load(self.Wv[:, :], io["L1_attn_Wv_up"][:, bass.ds(g * 64, 64)])

    def proj(self, h, which):
        return [(self.w[h][which], (self.latent, self.c.XNT)[which], (64, P)[which])]

    def affine(self, h, which):
        return 1.0, 0.0

    def vsrc(self):
        return self.latent, 64


class NarrowAttention(Attention):

    def __init__(self, core, psum, io, factor, xp):
        super().__init__(core, psum, "L2", 16, 8)
        c, nc, ctx = core, core.nc, core.ctx
        self.io, self.factor, self.xp = io, factor, xp
        sb = lambda n, s, d=F32: ctx.enter_context(nc.sbuf_tensor("L2_" + n, s, d))
        self.w = sb("w", [P, 2, 4, 96])
        self.bias = sb("bias", [96, 2, 4])
        self.qbias = sb("qbias", [96, 4])
        self.Wv = sb("Wv", [P, 32])
        self.vbias = sb("bv", [1, 32])
        core.pool.done(nc.gpsimd.memset(self.w[:, :, :, :], 0.0))
        core.pool.done(nc.gpsimd.memset(self.bias[:, :, :], 0.0))
        self.once()

    def load(self, g):
        c, io = self.c, self.io
        for x, n in enumerate("kq"):
            W = io["L2_attn_W" + n][:, bass.ds(g * 32, 32)].rearrange("p (h d) -> p h d", h=4)
            b = io["L2_attn_b" + n][bass.ds(g * 32, 32)].rearrange("(h d) -> d h", h=4)
            for third in range(3):
                s = slice(32 * third, 32 * third + 8)
                c.load(self.w[:, x, :, s], W)
                with self.c.nc.allow_non_contiguous_dma("32 elements"):
                    c.load(self.bias[s, x, :], b)
        for h in range(4):
            c.load(self.Wo[h * 32:h * 32 + 8, h // 2, 129 * (h % 2):129 * (h % 2) + 128], io["L2_attn_Wo"][bass.ds(g * 32 + h * 8, 8), :])
        c.load(self.Wv[:, :], io["L2_attn_Wv"][:, bass.ds(g * 32, 32)])
        c.load(self.vbias[:, :], io["L2_attn_bv"][bass.ds(g * 32, 32)].rearrange("(a n) -> a n", a=1))
        c.dve.wait(c.loads.all())
        t = c.dve.done(c.dve.e.tensor_scalar(self.qbias[:, :], self.bias[:, 1, :], self.factor[0:96, :], None, ALU.mult))
        c.act.wait(t)

    def proj(self, h, which):
        return [(self.w[:, which, h, :], self.xp, P)]

    def affine(self, h, which):
        if which:
            return self.factor[0:96, :], self.qbias[:, h:h + 1]
        return 1.0, self.bias[:, 0, h:h + 1]

    def vsrc(self):
        return self.xp, P


class NormedAttention(Attention):

    def __init__(self, core, psum, io, srcs):
        super().__init__(core, psum, "L3", 16, 64, last_key_mask=True)
        c, nc, ctx = core, core.nc, core.ctx
        self.io, self.srcs = io, srcs
        sb = lambda n, s, d=F32: ctx.enter_context(nc.sbuf_tensor("L3_" + n, s, d))
        self.w = [[sb(f"w{h}{x}", [P, P]) for x in "kq"] for h in range(2)]
        self.Wv = sb("Wv", [P, P])
        self.bias = sb("bias", [P, 2, 2])
        self.qbias = sb("qbias", [P, 2])
        self.vbias = sb("bv", [1, P])
        self.smax = 1.0 / float(D) ** 0.5
        self.once()

    def load(self, g):
        c, io = self.c, self.io
        for x, n in enumerate("kq"):
            for h in range(2):
                for half in (0, 64):
                    c.load(self.w[h][x][:, half:half + 64], io["L3_attn_W" + n][:, bass.ds(g * P + h * 64, 64)])
            for half in (0, 64):
                with self.c.nc.allow_non_contiguous_dma("128 elements"):
                    c.load(self.bias[half:half + 64, x, :], io["L3_attn_b" + n][bass.ds(g * P, P)].rearrange("(h d) -> d h", h=2))
        for h in range(2):
            c.load(self.Wo[h * 64:h * 64 + 64, 0, 129 * h:129 * h + 128], io["L3_attn_Wo"][bass.ds(g * P + h * 64, 64), :])
        c.load(self.Wv[:, :], io["L3_attn_Wv"][:, bass.ds(g * P, P)])
        c.load(self.vbias[:, :], io["L3_attn_bv"][bass.ds(g * P, P)].rearrange("(a n) -> a n", a=1))
        c.dve.wait(c.loads.all())
        t = c.dve.done(c.dve.e.tensor_scalar(self.qbias[:, :], self.bias[:, 1, :], self.smax, None, ALU.mult))
        c.act.wait(t)

    def proj(self, h, which):
        return [(self.w[h][which], self.srcs[which], P)]

    def affine(self, h, which):
        if which:
            return self.smax, self.qbias[:, h:h + 1]
        return 1.0, self.bias[:, 0, h:h + 1]

    def vsrc(self):
        return self.srcs[2], P


class Psum:

    def __init__(self, nc, ctx):
        self.all = ctx.enter_context(nc.psum_tensor("banks", [P, 8 * BANK], F32))
        self.S = self.all[:, 0:4 * BANK]
        self.MX = self.all[:, 4 * BANK:6 * BANK]
        self.O = self.all[:, 6 * BANK:7 * BANK]
        self.Y = self.all[:, 7 * BANK:8 * BANK]

    def bank(self, i):
        return self.all[:, i * BANK:(i + 1) * BANK]


def run_groups(core, att):
    with core.nc.Fori(0, att.groups) as g:
        att.load(g)
        att.project(g)
        att.attend(g)
        core.barrier()


def rstd_of(core, var, eps, tmp, out, n):
    act, dve = core.act, core.dve
    a, b = tmp
    e = dve.done(dve.e.tensor_scalar(a, var, eps, None, ALU.add))
    act.wait(e)
    r = act.done(act.e.activation(b, a, ACT.Sqrt))
    dve.wait(r, e)
    y = dve.done(dve.e.reciprocal(out, b))
    dve.wait(y)
    t = dve.done(dve.e.tensor_tensor(b, out, out, ALU.mult))
    dve.wait(t)
    t = dve.done(dve.e.tensor_tensor(b, b, a, ALU.mult))
    dve.wait(t)
    t = dve.done(dve.e.tensor_scalar(b, b, -0.5, 1.5, ALU.mult, ALU.add))
    dve.wait(t)
    return dve.done(dve.e.tensor_tensor(out, out, b, ALU.mult))


class Norm:

    def __init__(self, core, name, n=NT):
        nc, ctx = core.nc, core.ctx
        self.c = core
        self.n = n
        sb = lambda x, s: ctx.enter_context(nc.sbuf_tensor(name + "_" + x, s, F32))
        self.stats = sb("stats", [P, n, 6])
        self.mv = sb("mv", [P, n, 2])
        self.a = sb("a", [P, n])
        self.b = sb("b", [P, n])
        self.rstd = sb("rstd", [P, n])

    def run(self, src, dst, eps=1e-5, ready=(), readers=()):
        dve = self.c.dve
        dve.wait(*ready)
        for i in range(self.n):
            t = dve.done(dve.e.bn_stats(self.stats[:, i, :], src(i)))
        dve.wait(t)
        for i in range(self.n):
            t = dve.done(dve.e.bn_aggr(self.mv[:, i, :], self.stats[:, i, :]))
        dve.wait(t)
        t = rstd_of(self.c, self.mv[:, :, 1], eps, (self.a[:, :], self.b[:, :]), self.rstd[:, :], self.n)
        dve.wait(t, *readers)
        out = []
        for i in range(self.n):
            out.append(dve.done(dve.e.tensor_scalar(dst(i), src(i), self.mv[:, i, 0:1], self.rstd[:, i:i + 1], ALU.subtract, ALU.mult)))
        return out


def to_features(core, psum, src, dst, made, scale=1.0, bias=0.0):
    pe, act = core.pe, core.act
    read = [None] * 2
    for b in range(4):
        ps = psum.bank(b % 2)
        pe.wait(read[b % 2], made[4 * b + 3])
        for j in range(4):
            m = pe.e.transpose(ps[:, j * P:(j + 1) * P], src[:, 4 * b + j, :], core.ident[:, :])
        m = pe.done(m)
        act.wait(m)
        read[b % 2] = act.done(act.e.activation(dst[:, b * BANK:(b + 1) * BANK], ps, ACT.Identity, scale=scale, bias=bias))
    return read[1]


def quantized_ffn(core, psum, io):
    nc = core.nc
    pe, act, dve = core.pe, core.act, core.dve
    with ExitStack() as ctx:
        sb = lambda n, s, d=F32: ctx.enter_context(nc.sbuf_tensor("F0_" + n, s, d))
        H = 384
        raw = [sb(f"raw{i}", [P, H], I32) for i in range(3)]
        w = [sb(f"w{i}", [P, H]) for i in range(3)]
        g = [sb(f"g{i}", [P, BANK]) for i in range(2)]
        h = sb("h", [P, 2, 3, BANK])
        core.load(raw[0][:, :], io["L0_ffn_w_gate"])
        core.load(raw[1][:, :], io["L0_ffn_w_up"])
        core.load(raw[2][:, :].rearrange("p (j d) -> p j d", j=3), io["L0_ffn_w_down"].rearrange("(j p) d -> p j d", p=P))
        dve.wait(core.loads.all())
        for i in range(3):
            ready = dve.done(dve.e.tensor_scalar(w[i][:, :], raw[i][:, :], 1.0 / 127.0, None, ALU.mult))
        pe.wait(ready)
        read = [None] * 8
        gread = [None] * 2
        hread = [None] * 2
        n = 0
        for c in range(4):
            s = slice(c * BANK, (c + 1) * BANK)
            for j in range(3):
                a, b = psum.bank(2 * (n % 2)), psum.bank(2 * (n % 2) + 1)
                pe.wait(read[2 * (n % 2)], read[2 * (n % 2) + 1])
                pe.e.matmul(a, w[0][:, j * P:(j + 1) * P], core.XNT[:, s], start=True, stop=True)
                made = pe.done(pe.e.matmul(b, w[1][:, j * P:(j + 1) * P], core.XNT[:, s], start=True, stop=True))
                act.wait(made, gread[n % 2])
                sg = read[2 * (n % 2)] = act.done(act.e.activation(g[n % 2][:, :], a, ACT.Silu))
                dve.wait(sg, hread[c % 2])
                up = read[2 * (n % 2) + 1] = gread[n % 2] = dve.done(dve.e.tensor_tensor(h[:, c % 2, j, :], g[n % 2][:, :], b, ALU.mult))
                n += 1
            y = psum.bank(4 + c % 2)
            pe.wait(up, read[4 + c % 2])
            for q in range(4):
                for j in range(3):
                    mm = pe.e.matmul(y[:, q * P:(q + 1) * P], h[:, c % 2, j, q * P:(q + 1) * P], w[2][:, j * P:(j + 1) * P], start=j == 0, stop=j == 2)
            hread[c % 2] = pe.done(mm)
            act.wait(hread[c % 2])
            read[4 + c % 2] = act.done(act.e.activation(core.GATE[:, 4 * c:4 * c + 4, :], y.rearrange("p (q d) -> p q d", q=4), ACT.Silu))
        core.barrier()


def transformer_gate(core, psum, io):
    nc = core.nc
    pe, act, dve, pool = core.pe, core.act, core.dve, core.pool
    HEADS, HID = 8, 341
    HT = [(0, 128), (128, 128), (256, 85)]
    with ExitStack() as ctx:
        sb = lambda n, s, d=F32: ctx.enter_context(nc.sbuf_tensor("F1_" + n, s, d))
        state = core.SACC
        xs = sb("xs", [P, 5, D])
        hT = sb("hT", [P, BANK])
        carry = sb("carry", [P, 1])
        wqkv = sb("wqkv", [P, 1536])
        wo = sb("wo", [P, 4, P])
        w1 = sb("w1", [P, 2 * HID])
        w2 = sb("w2", [P, 3, P])
        b1 = sb("b1", [P, 2, 3])
        b2 = sb("b2", [1, P])
        lgb = sb("lgb", [P, 2])
        gains = sb("gains", [P, 2, 64])
        tab = sb("tab", [P, 4, 4, 64])
        ssq = sb("ssq", [P, 3, 4, 2, HEADS])
        sq = [sb(f"sq{i}", [P, BANK]) for i in range(2)]
        qn = [[sb(f"{x}n{i}", [P, HEADS, 64]) for i in range(4)] for x in "qk"]
        rot = [sb(f"rot{i}", [P, HEADS, 64]) for i in range(2)]
        qT = [sb(f"qT{i}", [P, 4, P]) for i in range(2)]
        kT = sb("kT", [P, 4, 2, 5 * P])
        V = sb("V", [P, 5, BANK])
        mask = sb("mask", [P, 2, 256], BF16)
        maskf = sb("maskf", [P, 1])
        wts = [sb(f"wts{i}", [P, HEADS, 256]) for i in range(2)]
        wT = sb("wT", [P, 16, P])
        nm = sb("nm", [P, 4, HEADS])
        den = sb("den", [P, 4, HEADS])
        o = [sb(f"o{i}", [P, BANK]) for i in range(2)]
        oT = [sb(f"oT{i}", [P, BANK]) for i in range(2)]
        z = sb("z", [P, 4, D])
        zT = sb("zT", [P, BANK])
        g = [sb(f"g{i}", [P, BANK]) for i in range(2)]
        u = sb("u", [P, 3, BANK])
        moves = sb("moves", [P, 2, P])
        st6, mv = sb("st6", [P, 4, 6]), sb("mv", [P, 4, 2])
        ra, rb, rstd = sb("ra", [P, 4]), sb("rb", [P, 4]), sb("rstd", [P, 4])
        S4 = psum.S
        core.load(moves[:, :, :], io["row_moves"])
        core.load(mask[:, 1, :], io["band_mask"].bitcast(BF16)[1])
        t = pool.done(pool.e.tensor_copy(state[:, :, :], core.XN[:, :, :]))
        pool.done(pool.e.memset(kT[:, :, :, :], 0.0))
        core.sp.wait(core.loads.all())
        core.barrier()
        for l in range(2):
            core.load(wqkv[:, :], io["L1_ffn_wqkv"][l])
            core.load(wo[:, :, :], io["L1_ffn_wo"][l].rearrange("(j p) d -> p j d", p=P))
            core.load(w1[:, :], io["L1_ffn_w1"][l])
            core.load(b2[:, :], io["L1_ffn_b2"][l].rearrange("(a d) -> a d", a=1))
            core.load(gains[:, 0, :], io["L1_ffn_q_scale"][l].partition_broadcast(P))
            core.load(gains[:, 1, :], io["L1_ffn_k_scale"][l].partition_broadcast(P))
            with nc.allow_non_contiguous_dma("small columns"):
                core.load(lgb[:, 0:1], io["L1_ffn_ln_g"][l].rearrange("(p a) -> p a", a=1))
                core.load(lgb[:, 1:2], io["L1_ffn_ln_b"][l].rearrange("(p a) -> p a", a=1))
                for j, (a, n) in enumerate(HT):
                    core.load(w2[0:n, j, :], io["L1_ffn_w2"][l][a:a + n, :])
                    for half in range(2):
                        core.load(b1[0:n, half, j:j + 1], io["L1_ffn_b1"][l][half * HID + a:half * HID + a + n].rearrange("(p a) -> p a", a=1))
            t = [pool.done(pool.e.memset(x, 0.0)) for x in (kT[:, :, :, 0:P], V[:, 0, :], xs[:, 0, :], carry[:, :])]
            core.sp.wait(core.loads.all())
            core.barrier()
            with nc.Fori(0, 4) as c:
                core.load(tab[:, :, :, :], io["xpos"][:, bass.ds(c * 4, 4), :, :])
                core.load(mask[:, 0, :], io["first_masks"].bitcast(BF16)[bass.ds(c, 1), :, :].rearrange("a p k -> p (a k)"))
                m = pool.done(pool.e.tensor_copy(xs[:, 1:5, :], state[:, bass.ds(c * 4, 4), :]))
                pe.wait(m)
                for j in range(4):
                    m = pe.e.transpose(psum.bank(0)[:, j * P:(j + 1) * P], xs[:, 1 + j, :], core.ident[:, :])
                m = pe.done(m)
                act.wait(m)
                a0 = act.done(act.e.activation(hT[0:64, :], psum.bank(0)[0:64, :], ACT.Copy))
                act.done(act.e.activation(hT[64:P, 1:BANK], psum.bank(0)[64:P, 0:BANK - 1], ACT.Copy))
                m = act.done(act.e.activation(hT[64:P, 0:1], carry[64:P, :], ACT.Copy))
                act.wait(m)
                hmade = act.done(act.e.activation(carry[64:P, :], psum.bank(0)[64:P, BANK - 1:BANK], ACT.Copy))
                dve.wait(core.loads.all())
                pe.wait(core.loads.all())
                for x in range(2):
                    gx = gains[:, x:x + 1, :]
                    dve.done(dve.e.tensor_tensor(tab[:, :, 2 * x, :], tab[:, :, 2 * x, :], gx.to_broadcast([P, 4, 64]), ALU.mult))
                    dve.done(dve.e.tensor_tensor(tab[:, :, 2 * x + 1, 0:32], tab[:, :, 2 * x + 1, 0:32], gx[:, :, 32:64].to_broadcast([P, 4, 32]), ALU.mult))
                    tabs = dve.done(dve.e.tensor_tensor(tab[:, :, 2 * x + 1, 32:64], tab[:, :, 2 * x + 1, 32:64], gx[:, :, 0:32].to_broadcast([P, 4, 32]), ALU.mult))
                read = [None] * 8
                n = 0
                sqread = [None] * 2
                pe.wait(hmade)
                for i in range(4):
                    for x in range(3):
                        b0 = n % 8
                        n += 1
                        ps = psum.bank(b0)
                        pe.wait(read[b0])
                        m = pe.done(pe.e.matmul(ps, hT[:, i * P:(i + 1) * P], wqkv[:, x * BANK:(x + 1) * BANK], start=True, stop=True))
                        act.wait(m)
                        if x == 2:
                            vmade = read[b0] = act.done(act.e.activation(V[:, 1 + i, :], ps, ACT.Copy))
                            continue
                        act.wait(sqread[x])
                        s2 = act.done(act.e.activation(sq[x][:, :], ps, ACT.Square))
                        read[b0] = act.done(act.e.activation(qn[x][i][:, :, :], ps.rearrange("p (h d) -> p h d", h=HEADS), ACT.Copy))
                        copied = read[b0]
                        dve.wait(s2)
                        sqread[x] = dve.done(dve.e.tensor_reduce(ssq[:, 0, i, x, :], sq[x][:, :].rearrange("p (h d) -> p h d", h=HEADS), AX.X, ALU.add))
                A, B, C = (ssq[:, i, :, :, :] for i in range(3))
                act.wait(sqread[0], sqread[1])
                m = act.done(act.e.activation(B, A, ACT.Sqrt))
                dve.wait(m, sqread[1])

                def chain(ins):
                    t = dve.done(ins)
                    dve.wait(t)
                    return t

                chain(dve.e.tensor_scalar(B, B, 1e-12, None, ALU.max))
                chain(dve.e.reciprocal(C, B))
                chain(dve.e.tensor_tensor(C, C, A, ALU.mult))
                chain(dve.e.tensor_tensor(B, B, C, ALU.add))
                chain(dve.e.tensor_scalar(B, B, 0.5, 1e-12, ALU.mult, ALU.max))
                chain(dve.e.reciprocal(A, B))
                dve.wait(copied, tabs)
                rread = [None] * 2
                for i in range(4):
                    for x in range(2):
                        v = qn[x][i]
                        over = lambda y, w=64: y.to_broadcast([P, HEADS, w])
                        chain(dve.e.tensor_tensor(v[:, :, :], v[:, :, :], ssq[:, 0, i, x, :].rearrange("p (h a) -> p h a", a=1).to_broadcast([P, HEADS, 64]), ALU.mult))
                        r = rot[x]
                        dve.wait(rread[x])
                        dve.done(dve.e.tensor_tensor(r[:, :, 0:32], v[:, :, 32:64], over(tab[:, i, 2 * x + 1:2 * x + 2, 0:32], 32), ALU.mult))
                        m = dve.done(dve.e.tensor_tensor(r[:, :, 32:64], v[:, :, 0:32], over(tab[:, i, 2 * x + 1:2 * x + 2, 32:64], 32), ALU.mult))
                        dve.wait(m)
                        m = dve.done(dve.e.tensor_tensor(v[:, :, :], v[:, :, :], over(tab[:, i, 2 * x:2 * x + 1, :]), ALU.mult))
                        pool.wait(m)
                        rread[x] = turned = pool.done(pool.e.tensor_tensor(v[:, :, :], v[:, :, :], r[:, :, :], ALU.add))
                        if x == 1:
                            kturned = turned
                    b0 = n % 8
                    n += 1
                    pe.wait(read[b0], kturned)
                    for j in range(4):
                        m = pe.e.transpose(psum.bank(b0)[:, j * P:(j + 1) * P], qn[1][i][:, 2 * j:2 * j + 2, :].rearrange("p h d -> p (h d)"), core.ident[:, :])
                    m = pe.done(m)
                    act.wait(m)
                    ps = psum.bank(b0).rearrange("p (j t) -> p j t", j=4)
                    s = slice((1 + i) * P, (2 + i) * P)
                    act.done(act.e.activation(kT[0:64, :, 0, s], ps[0:64, :, :], ACT.Copy))
                    kmade = read[b0] = act.done(act.e.activation(kT[64:P, :, 1, s], ps[64:P, :, :], ACT.Copy))
                sread = [read[0], read[1], read[2], read[3]]
                wread = [None] * 2
                wTread = None
                n = 0
                free4 = list(read[4:8])
                xnew = []

                def take():
                    nonlocal n
                    b0 = n % 4
                    n += 1
                    return b0

                for i in range(4):
                    b0 = take()
                    ps = psum.bank(4 + b0)
                    pe.wait(free4[b0])
                    for j in range(4):
                        m = pe.e.transpose(ps[:, j * P:(j + 1) * P], qn[0][i][:, 2 * j:2 * j + 2, :].rearrange("p h d -> p (h d)"), core.ident[:, :])
                    m = pe.done(m)
                    act.wait(m)
                    qmade = free4[b0] = act.done(act.e.activation(qT[i % 2][:, :, :], ps.rearrange("p (j t) -> p j t", j=4), ACT.Copy))
                    pe.wait(qmade, kmade, *sread)
                    for h in range(HEADS):
                        so = S4[:, h * 256:(h + 1) * 256]
                        pe.e.matmul(so, qT[i % 2][:, h // 2, :], kT[:, h // 2, h % 2, i * P:(i + 2) * P], start=True, stop=False)
                        m = pe.e.matmul(so, core.identb[:, :], mask[:, min(i, 1), :], start=False, stop=True)
                    m = pe.done(m)
                    dve.wait(m)
                    m = dve.done(dve.e.tensor_reduce(nm[:, i, :], S4.rearrange("p (h k) -> p h k", h=HEADS), AX.X, ALU.max, negate=True))
                    dve.wait(m)
                    m = dve.done(dve.e.tensor_scalar(nm[:, i, :], nm[:, i, :], 8.0, None, ALU.mult))
                    act.wait(m, wread[i % 2])
                    for h in range(HEADS):
                        m = act.done(act.e.activation(wts[i % 2][:, h, :], S4[:, h * 256:(h + 1) * 256], ACT.Exp, bias=nm[:, i, h:h + 1], scale=8.0, accum_out=den[:, i, h:h + 1]))
                    dve.wait(m)
                    rden = dve.done(dve.e.reciprocal(den[:, i, :], den[:, i, :]))
                    pe.wait(m)
                    for h in range(HEADS):
                        for k in range(2):
                            t = pe.e.transpose(S4[:, (2 * h + k) * P:(2 * h + k + 1) * P], wts[i % 2][:, h, k * P:(k + 1) * P], core.ident[:, :])
                    t = wread[i % 2] = pe.done(t)
                    act.wait(t, wTread)
                    dve.wait(t, wTread)
                    flat = wT[:, :, :].rearrange("p a b -> p (a b)")
                    ta = act.done(act.e.activation(flat[:, 0:1024], S4[:, 0:1024], ACT.Copy))
                    tb = dve.done(dve.e.tensor_copy(flat[:, 1024:2048], S4[:, 1024:2048]))
                    sread = [ta, tb]
                    b0 = take()
                    ps = psum.bank(4 + b0)
                    pe.wait(ta, tb, vmade, free4[b0])
                    for h in range(HEADS):
                        for k in range(2):
                            m = pe.e.matmul(ps[:, h * 64:(h + 1) * 64], wT[:, 2 * h + k, :], V[:, i + k, h * 64:(h + 1) * 64], start=k == 0, stop=k == 1)
                    wTread = m = pe.done(m)
                    dve.wait(m, rden)
                    m = free4[b0] = dve.done(dve.e.tensor_tensor(o[i % 2][:, :].rearrange("p (h d) -> p h d", h=HEADS), ps.rearrange("p (h d) -> p h d", h=HEADS), den[:, i, :].rearrange("p (h a) -> p h a", a=1).to_broadcast([P, HEADS, 64]), ALU.mult))
                    b0 = take()
                    ps = psum.bank(4 + b0)
                    pe.wait(m, free4[b0])
                    for j in range(4):
                        m = pe.e.transpose(ps[:, j * P:(j + 1) * P], o[i % 2][:, j * P:(j + 1) * P], core.ident[:, :])
                    m = pe.done(m)
                    act.wait(m)
                    m = free4[b0] = act.done(act.e.activation(oT[i % 2][:, :], ps, ACT.Copy))
                    b0 = take()
                    ps = psum.bank(4 + b0)
                    pe.wait(m, free4[b0])
                    for j in range(4):
                        m = pe.e.matmul(ps[:, 0:P], oT[i % 2][:, j * P:(j + 1) * P], wo[:, j, :], start=j == 0, stop=j == 3)
                    m = pe.done(m)
                    dve.wait(m)
                    m = free4[b0] = dve.done(dve.e.tensor_tensor(xs[:, 1 + i, :], xs[:, 1 + i, :], ps[:, 0:P], ALU.add))
                    xnew.append(m)
                bs = [4 + take() for _ in range(4)]
                for i in range(4):
                    ps = psum.bank(bs[i])
                    pe.wait(xnew[i], free4[bs[i] - 4])
                    pe.e.matmul(ps[:, 0:64], core.ident[:, :], xs[:, 1 + i, 0:64], start=True, stop=True)
                    pe.e.matmul(ps[:, 64:P], moves[:, 0, :], xs[:, 1 + i, 64:P], start=True, stop=False)
                    m = pe.done(pe.e.matmul(ps[:, 64:P], moves[:, 1, :], xs[:, i, 64:P], start=False, stop=True))
                    dve.wait(m)
                    t = dve.done(dve.e.bn_stats(st6[:, i, :], ps[:, 0:P]))
                dve.wait(t)
                for i in range(4):
                    t = dve.done(dve.e.bn_aggr(mv[:, i, :], st6[:, i, :]))
                dve.wait(t)
                t = rstd_of(core, mv[:, :, 1], 1e-5, (ra[:, :], rb[:, :]), rstd[:, :], 4)
                dve.wait(t)
                for i in range(4):
                    t = free4[bs[i] - 4] = dve.done(dve.e.tensor_scalar(z[:, i, :], psum.bank(bs[i])[:, 0:P], mv[:, i, 0:1], rstd[:, i:i + 1], ALU.subtract, ALU.mult))
                pe.wait(t, *sread)
                for i in range(4):
                    m = pe.e.transpose(psum.bank(0)[:, i * P:(i + 1) * P], z[:, i, :], core.ident[:, :])
                m = pe.done(m)
                act.wait(m, core.loads.all())
                m = act.done(act.e.activation(zT[:, :], psum.bank(0), ACT.Identity, scale=lgb[:, 0:1], bias=lgb[:, 1:2]))
                pe.wait(m)
                for j, (a, w) in enumerate(HT):
                    pa, pg = psum.bank(1 + j), psum.bank(4 + j)
                    pe.wait(free4[j])
                    pe.e.matmul(pa[0:w, :], w1[:, a:a + w], zT[:, :], start=True, stop=True)
                    m = pe.done(pe.e.matmul(pg[0:w, :], w1[:, HID + a:HID + a + w], zT[:, :], start=True, stop=True))
                    act.wait(m)
                    if j == 2:
                        act.wait(umade)
                    m = act.done(act.e.activation(g[j % 2][0:w, :], pg[0:w, :], ACT.Gelu, bias=b1[0:w, 1, j:j + 1]))
                    dve.wait(m)
                    t = dve.done(dve.e.scalar_tensor_tensor(u[0:w, j, :], pa[0:w, :], b1[0:w, 0, j:j + 1], g[j % 2][0:w, :], ALU.add, ALU.mult))
                    if j == 0:
                        umade = t
                pe.wait(t, free4[3])
                ps = psum.bank(7)
                for i in range(4):
                    for j, (a, w) in enumerate(HT):
                        pe.e.matmul(ps[:, i * P:(i + 1) * P], u[0:w, j, i * P:(i + 1) * P], w2[0:w, j, :], start=j == 0, stop=False)
                    m = pe.e.matmul(ps[:, i * P:(i + 1) * P], core.onerow[:, 0:P], b2[:, :], start=False, stop=True)
                m = pe.done(m)
                dve.wait(m)
                t = dve.done(dve.e.tensor_tensor(state[:, bass.ds(c * 4, 4), :], xs[:, 1:5, :], ps.rearrange("p (i d) -> p i d", i=4), ALU.add))
                pool.wait(t, m, vmade, kmade)
                pool.done(pool.e.tensor_copy(xs[:, 0, :], xs[:, 4, :]))
                pool.done(pool.e.tensor_copy(V[:, 0, :], V[:, 4, :]))
                pool.done(pool.e.tensor_copy(kT[:, :, :, 0:P], kT[:, :, :, 4 * P:5 * P]))
                core.barrier()
        act.done(act.e.activation(core.GATE[:, :, :], state[:, :, :], ACT.Silu))
        core.barrier()
        pool.done(pool.e.memset(state[:, :, :], 0.0))
        core.barrier()


def ternary_ffn(core, psum, io):
    nc = core.nc
    pe, act, dve = core.pe, core.act, core.dve
    with ExitStack() as ctx:
        sb = lambda n, s, d=F32: ctx.enter_context(nc.sbuf_tensor("F2_" + n, s, d))
        H = 512
        w1, w2 = sb("w1", [P, H]), sb("w2", [P, H])
        h1, h2 = sb("h1", [P, 4, H]), sb("h2", [P, 4, H])
        w3 = sb("w3", [P, 4, P])
        s3 = sb("s3", [P, P])
        sc = sb("sc", [P, 4, 4])
        a = [sb(f"a{i}", [P, BANK]) for i in range(2)]
        u = [sb(f"u{i}", [P, 4, BANK]) for i in range(3)]
        core.load(w1[:, :], io["L2_ffn_w1_w"])
        core.load(w2[:, :], io["L2_ffn_w2_w"])
        for t, n in ((h1, "h1_w"), (h2, "h2_w"), (w3, "w3_w")):
            core.load(t[:, :, :], io["L2_ffn_" + n].rearrange("(j p) o -> p j o", p=P))
        core.load(s3[:, :], io["L2_ffn_w3_s"].partition_broadcast(P))
        with nc.allow_non_contiguous_dma("512 scales"):
            for i, n in enumerate(("w1_s", "w2_s", "h1_s", "h2_s")):
                core.load(sc[:, i, :], io["L2_ffn_" + n].rearrange("(j p) -> p j", p=P))
        dve.wait(core.loads.all())
        for j in range(4):
            ready = dve.done(dve.e.tensor_tensor(w3[:, j, :], w3[:, j, :], s3[:, :], ALU.mult))
        pe.wait(core.loads.all(), ready)
        act.wait(core.loads.all())
        read = [None] * 8
        n = 0
        aread = [None] * 2
        uread = [None] * 3
        for c in range(4):
            s = slice(c * BANK, (c + 1) * BANK)
            for j in range(4):
                js = slice(j * P, (j + 1) * P)
                b0, b1 = n % 8, (n + 1) % 8
                n += 2
                p0, p1 = psum.bank(b0), psum.bank(b1)
                pe.wait(read[b0], read[b1])
                pe.e.matmul(p0, w1[:, js], core.XNT[:, s], start=True, stop=True)
                made = pe.done(pe.e.matmul(p1, w2[:, js], core.XNT[:, s], start=True, stop=True))
                act.wait(made, aread[j % 2])
                sg = read[b0] = act.done(act.e.activation(a[j % 2][:, :], p0, ACT.Silu, scale=sc[:, 0, j:j + 1]))
                dve.wait(sg, uread[0])
                last = read[b1] = aread[j % 2] = dve.done(dve.e.scalar_tensor_tensor(u[0][:, j, :], p1, sc[:, 1, j:j + 1], a[j % 2][:, :], ALU.mult, ALU.mult))
            for layer, w in ((1, h1), (2, h2)):
                for j in range(4):
                    b0 = n % 8
                    n += 1
                    p0 = psum.bank(b0)
                    pe.wait(read[b0], last)
                    for i in range(4):
                        mm = pe.e.matmul(p0, w[:, i, j * P:(j + 1) * P], u[layer - 1][:, i, :], start=i == 0, stop=i == 3)
                    uread[layer - 1] = made = pe.done(mm)
                    act.wait(made, uread[layer])
                    nxt = read[b0] = act.done(act.e.activation(u[layer][:, j, :], p0, ACT.Gelu, scale=sc[:, layer + 1, j:j + 1]))
                last = nxt
            b0 = n % 8
            n += 1
            y = psum.bank(b0)
            pe.wait(read[b0], last)
            for q in range(4):
                for j in range(4):
                    mm = pe.e.matmul(y[:, q * P:(q + 1) * P], u[2][:, j, q * P:(q + 1) * P], w3[:, j, :], start=j == 0, stop=j == 3)
            uread[2] = made = pe.done(mm)
            act.wait(made)
            read[b0] = act.done(act.e.activation(core.GATE[:, 4 * c:4 * c + 4, :], y.rearrange("p (q d) -> p q d", q=4), ACT.Silu))
        core.barrier()


def attention2(core, psum, io):
    nc, ctx = core.nc, core.ctx
    pe, act, dve, pool = core.pe, core.act, core.dve, core.pool
    sb = lambda n, s, d=F32: ctx.enter_context(nc.sbuf_tensor("A2_" + n, s, d))
    rby = sb("rby", [P, 3])
    f = sb("f", [P, 8])
    factor = sb("factor", [P, 1])
    denom = sb("denom", [P, 2])
    core.load(denom[:, :], io["position_denominators"])
    core.load(rby[:, :], io["L2_attn_rby"].partition_broadcast(P))
    dve.wait(core.loads.all())
    red, blue, yellow = rby[:, 0:1], rby[:, 1:2], rby[:, 2:3]

    def chain(ins):
        t = dve.done(ins)
        dve.wait(t)
        return t

    chain(dve.e.tensor_scalar(f[:, 0:1], red, 0.1, 1.0, ALU.mult, ALU.add))
    chain(dve.e.scalar_tensor_tensor(f[:, 0:1], blue, 0.05, f[:, 0:1], ALU.mult, ALU.add))
    chain(dve.e.scalar_tensor_tensor(f[:, 0:1], yellow, 0.15, f[:, 0:1], ALU.mult, ALU.add))
    chain(dve.e.tensor_scalar(f[:, 1:2], red, 0.0, 1.0, ALU.mult, ALU.add))
    chain(dve.e.tensor_scalar(f[:, 1:2], f[:, 1:2], float(1.0 / np.sqrt(8.0)), None, ALU.mult))
    chain(dve.e.tensor_tensor(factor[:, :], f[:, 0:1], f[:, 1:2], ALU.mult))
    chain(dve.e.tensor_scalar(f[:, 2:3], yellow, float(0.1 * np.sin(np.pi)), 1.0, ALU.mult, ALU.add))
    chain(dve.e.tensor_scalar(f[:, 3:4], blue, 0.1, 1.0, ALU.mult, ALU.add))
    chain(dve.e.tensor_scalar(f[:, 3:4], f[:, 3:4], 1e-5, None, ALU.mult))
    chain(dve.e.tensor_scalar(f[:, 4:5], red, 0.1, 1.0, ALU.mult, ALU.add))
    chain(dve.e.scalar_tensor_tensor(f[:, 4:5], yellow, 0.05, f[:, 4:5], ALU.mult, ALU.add))
    xp = sb("xp", [P, T])
    xpt = sb("xpt", [P, NT, D])
    with ExitStack() as tmp:
        st = lambda n, s, d=F32: tmp.enter_context(nc.sbuf_tensor("A2p_" + n, s, d))
        pos = st("pos", [P, T])
        turns = st("turns", [P, T])
        whole = st("whole", [P, T], I32)
        iota = pool.done(pool.e.iota(pos[:, :], pattern=[[1, T]], base=0, channel_multiplier=0, allow_small_or_imprecise_dtypes=True))
        dve.wait(iota)
        chain(dve.e.tensor_scalar(f[:, 5:6], yellow, float(0.1 * np.sin(np.pi / 2)), 1.0, ALU.mult, ALU.add))
        chain(dve.e.tensor_tensor(f[:, 5:6], f[:, 5:6], denom[:, 0:1], ALU.mult))
        chain(dve.e.reciprocal(f[:, 6:7], f[:, 5:6]))
        chain(dve.e.tensor_scalar(pos[:, :], pos[:, :], f[:, 6:7], None, ALU.mult))
        chain(dve.e.tensor_scalar(turns[:, :], pos[:, :], float(1 / (2 * np.pi)), denom[:, 1:2], ALU.mult, ALU.add))
        chain(dve.e.tensor_copy(whole[:, :], turns[:, :]))
        chain(dve.e.tensor_copy(turns[:, :], whole[:, :]))
        rest = 2 * np.pi
        for bits in (2 ** 5, 2 ** 17, None):
            part = float(np.floor(rest * bits) / bits) if bits else float(np.float32(rest))
            rest -= part
            chain(dve.e.scalar_tensor_tensor(pos[:, :], turns[:, :], -part, pos[:, :], ALU.mult, ALU.add))
        chain(dve.e.tensor_scalar(f[:, 7:8], denom[:, 1:2], float(np.float32(2 * np.pi)), None, ALU.mult))
        chain(dve.e.tensor_scalar(pos[:, :], pos[:, :], f[:, 7:8], 3.1415925, ALU.add, ALU.min))
        t = chain(dve.e.tensor_scalar(pos[:, :], pos[:, :], -3.1415925, None, ALU.max))
        act.wait(t)
        t = act.done(act.e.activation(pos[:, :], pos[:, :], ACT.Sin))
        dve.wait(t)
        t = chain(dve.e.tensor_tensor(xp[:, :], core.XNT[:, :], pos[:, :], ALU.add))
        pe.wait(t)
        read = [None] * 2
        for b in range(4):
            ps = psum.bank(b % 2)
            pe.wait(read[b % 2])
            for j in range(4):
                m = pe.e.transpose(ps[:, j * P:(j + 1) * P], xp[:, (4 * b + j) * P:(4 * b + j + 1) * P], core.ident[:, :])
            m = pe.done(m)
            act.wait(m)
            read[b % 2] = act.done(act.e.activation(xpt[:, 4 * b:4 * b + 4, :], ps.rearrange("p (q d) -> p q d", q=4), ACT.Copy))
        core.barrier()
    with ExitStack() as own:
        core.ctx = own
        run_groups(core, NarrowAttention(core, psum, io, factor, xp))
        core.ctx = ctx
    with ExitStack() as own:
        core.ctx = own
        rows = own.enter_context(nc.sbuf_tensor("A2_rows", [P, 3, D], F32))
        for i, n in enumerate(("bo", "ln_gamma", "ln_beta")):
            core.load(rows[:, i, :], io["L2_attn_" + n].partition_broadcast(P))
        dve.wait(core.loads.all())
        chain(dve.e.tensor_scalar(rows[:, 1, :], rows[:, 1, :], f[:, 4:5], None, ALU.mult))
        A = core.SACC
        over = lambda i: rows[:, i:i + 1, :].to_broadcast([P, NT, D])
        chain(dve.e.scalar_tensor_tensor(xpt[:, :, :], A[:, :, :], f[:, 2:3], xpt[:, :, :], ALU.mult, ALU.add))
        t = chain(dve.e.tensor_tensor(xpt[:, :, :], xpt[:, :, :], over(0), ALU.add))
        n = Norm(core, "A2n")
        made = n.run(lambda i: xpt[:, i, :], lambda i: A[:, i, :], eps=f[:, 3:4])
        dve.wait(made[-1])
        chain(dve.e.tensor_tensor(A[:, :, :], A[:, :, :], over(1), ALU.mult))
        chain(dve.e.tensor_tensor(A[:, :, :], A[:, :, :], over(2), ALU.add))
        core.ctx = ctx


def attention3(core, psum, io):
    nc, ctx = core.nc, core.ctx
    pe, act, dve, pool = core.pe, core.act, core.dve, core.pool
    sb = lambda n, s, d=F32: ctx.enter_context(nc.sbuf_tensor("A3_" + n, s, d))
    gains = sb("gains", [P, 8])
    with nc.allow_non_contiguous_dma("columns of 128"):
        for i, n in enumerate(("lnk_s", "lnk_b", "lnq_s", "lnq_b", "lnv_s", "lnv_b", "lnm_s", "lnm_b")):
            core.load(gains[:, i:i + 1], io["L3_attn_" + n].rearrange("(p a) -> p a", a=1))
    core.lastq = ctx.enter_context(nc.sbuf_tensor("lastq", [P, 2, P], BF16))
    core.lastk = ctx.enter_context(nc.sbuf_tensor("lastk", [P, 2, P], BF16))
    core.load(core.lastq[:, :, :], io["last_q"].bitcast(BF16))
    core.load(core.lastk[:, :, :], io["last_k"].bitcast(BF16))
    with ExitStack() as own:
        core.ctx = own
        srcs = [own.enter_context(nc.sbuf_tensor(f"A3_src{i}", [P, T], F32)) for i in range(3)]
        with ExitStack() as inner:
            core.ctx = inner
            z = inner.enter_context(nc.sbuf_tensor("A3_z", [P, NT, D], F32))
            n = Norm(core, "A3n")
            made = n.run(lambda i: core.XN[:, i, :], lambda i: z[:, i, :])
            act.wait(core.loads.all())
            to_features(core, psum, z, srcs[0], made)
            core.barrier()
            for i in (2, 1, 0):
                act.done(act.e.activation(srcs[i][:, :], srcs[0][:, :], ACT.Identity, scale=gains[:, 2 * i:2 * i + 1], bias=gains[:, 2 * i + 1:2 * i + 2]))
            core.barrier()
        core.ctx = own
        run_groups(core, NormedAttention(core, psum, io, srcs))
        core.ctx = ctx
    with ExitStack() as own:
        core.ctx = own
        st = lambda n, s, d=F32: own.enter_context(nc.sbuf_tensor("A3m_" + n, s, d))
        rows = st("rows", [P, 2, D])
        core.load(rows[:, 0, :], io["L3_attn_bo"].partition_broadcast(P))
        core.load(rows[:, 1, :], io["L3_attn_b2"].partition_broadcast(P))
        W1, W2, b1 = st("W1", [P, 256]), st("W2", [P, 2, P]), st("b1", [P, 2])
        core.load(W1[:, :], io["L3_attn_W1"])
        core.load(W2[:, :, :], io["L3_attn_W2"].rearrange("(j p) d -> p j d", p=P))
        with nc.allow_non_contiguous_dma("256 biases"):
            core.load(b1[:, :], io["L3_attn_b1"].rearrange("(j p) -> p j", p=P))
        z, yT, u = st("z", [P, NT, D]), st("yT", [P, T]), st("u", [P, 2, 2, BANK])
        H = core.SACC
        over = lambda i, n=NT: rows[:, i:i + 1, :].to_broadcast([P, n, D])
        dve.wait(core.loads.all())
        t = dve.done(dve.e.tensor_tensor(H[:, :, :], H[:, :, :], core.XN[:, :, :], ALU.add))
        dve.wait(t)
        t = dve.done(dve.e.tensor_tensor(H[:, :, :], H[:, :, :], over(0), ALU.add))
        n = Norm(core, "A3o")
        made = n.run(lambda i: H[:, i, :], lambda i: z[:, i, :], ready=(t,))
        to_features(core, psum, z, yT, made, scale=gains[:, 6:7], bias=gains[:, 7:8])
        dve.wait(made[-1])
        t = dve.done(dve.e.tensor_tensor(H[:, :, :], H[:, :, :], over(1), ALU.add))
        dve.wait(t)
        pe.wait((act.sem, act.count), core.loads.all())
        act.wait(core.loads.all())
        read = [None] * 8
        uread = [None] * 2
        for c in range(4):
            s = slice(c * BANK, (c + 1) * BANK)
            for j in range(2):
                b0 = 2 + (2 * c + j) % 4
                pe.wait(read[b0])
                made = pe.done(pe.e.matmul(psum.bank(b0), W1[:, j * P:(j + 1) * P], yT[:, s], start=True, stop=True))
                act.wait(made, uread[c % 2])
                last = read[b0] = act.done(act.e.activation(u[:, c % 2, j, :], psum.bank(b0), ACT.Gelu_apprx_tanh, bias=b1[:, j:j + 1]))
            b0 = 6 + c % 2
            y = psum.bank(b0)
            pe.wait(last, read[b0])
            for q in range(4):
                for j in range(2):
                    mm = pe.e.matmul(y[:, q * P:(q + 1) * P], u[:, c % 2, j, q * P:(q + 1) * P], W2[:, j, :], start=j == 0, stop=j == 1)
            uread[c % 2] = made = pe.done(mm)
            dve.wait(made)
            read[b0] = dve.done(dve.e.tensor_tensor(H[:, 4 * c:4 * c + 4, :], H[:, 4 * c:4 * c + 4, :], y.rearrange("p (q d) -> p q d", q=4), ALU.add))
        core.barrier()
        core.ctx = ctx


def rms_rows(core, src, dst, sq, ss, gain, n, ready=()):
    act, dve = core.act, core.dve
    dve.wait(*ready)
    t = dve.done(dve.e.tensor_tensor(sq[:, 0:n, :], src, src, ALU.mult))
    dve.wait(t)
    t = dve.done(dve.e.tensor_reduce(ss[:, 0, 0:n], sq[:, 0:n, :], AX.X, ALU.add))
    act.wait(t)
    r = act.done(act.e.activation(ss[:, 1, 0:n], ss[:, 0, 0:n], ACT.Sqrt))
    dve.wait(r)
    t = dve.done(dve.e.tensor_scalar(ss[:, 1, 0:n], ss[:, 1, 0:n], 1e-12, None, ALU.max))
    dve.wait(t)
    t = dve.done(dve.e.reciprocal(ss[:, 2, 0:n], ss[:, 1, 0:n]))
    dve.wait(t)
    t = dve.done(dve.e.tensor_tensor(ss[:, 2, 0:n], ss[:, 2, 0:n], ss[:, 0, 0:n], ALU.mult))
    dve.wait(t)
    t = dve.done(dve.e.tensor_tensor(ss[:, 1, 0:n], ss[:, 1, 0:n], ss[:, 2, 0:n], ALU.add))
    dve.wait(t)
    t = dve.done(dve.e.tensor_scalar(ss[:, 1, 0:n], ss[:, 1, 0:n], 0.5, 1e-12, ALU.mult, ALU.max))
    dve.wait(t)
    t = dve.done(dve.e.reciprocal(ss[:, 0, 0:n], ss[:, 1, 0:n]))
    dve.wait(t)
    t = dve.done(dve.e.tensor_scalar(ss[:, 0, 0:n], ss[:, 0, 0:n], float(np.sqrt(np.float32(D))), None, ALU.mult))
    dve.wait(t)
    for i in range(n):
        t = dve.done(dve.e.scalar_tensor_tensor(dst[:, i, :], src[:, i, :], ss[:, 0, i:i + 1], gain, ALU.mult, ALU.mult))
    return t


def soft_moe(core, psum, io):
    nc = core.nc
    pe, act, dve, pool = core.pe, core.act, core.dve, core.pool
    NS = 4
    with ExitStack() as ctx:
        sb = lambda n, s, d=F32: ctx.enter_context(nc.sbuf_tensor("F3_" + n, s, d))
        xr = sb("xr", [P, NT, 129])
        xrT = sb("xrT", [P, T])
        se = sb("se", [P, NS, D])
        seT = sb("seT", [P, BANK])
        gain = sb("gain", [P, 2, D])
        sq = sb("sq", [P, NT, D])
        ss = sb("ss", [P, 3, NT])
        w1, w2 = sb("w1", [P, BANK]), sb("w2", [P, NS, D])
        tokmax = sb("tokmax", [P, NT])
        slotpart = sb("slotpart", [P, NS, 4])
        slotmax = sb("slotmax", [P, NS])
        rows = sb("rows", [1, T + BANK])
        E = [sb(f"E{i}", [P, BANK]) for i in range(2)]
        rden = sb("rden", [P, NT])
        slots = sb("slots", [P, NS, D])
        slotsT = sb("slotsT", [P, BANK])
        hid = sb("hid", [P, NS, BANK])
        proc = sb("proc", [P, NS, 129])
        Ct = [sb(f"C{i}", [P, NS, BANK]) for i in range(2)]
        core.load(se[:, :, :], io["L3_ffn_slot_embeds"].rearrange("(a e) t d -> (e t) a d", a=NS))
        core.load(gain[:, 0, :], io["L3_ffn_gamma_x"].partition_broadcast(P))
        core.load(gain[:, 1, :], io["L3_ffn_gamma_slot"].partition_broadcast(P))
        core.load(w1[:, :], io["L3_ffn_w1"])
        core.load(w2[:, :, :], io["L3_ffn_w2"].rearrange("(j p) d -> p j d", p=P))
        pool.done(pool.e.memset(xr[:, :, 128:129], 1.0))
        pool.done(pool.e.memset(proc[:, :, 128:129], 1.0))
        a = rms_rows(core, core.XN[:, :, :], xr[:, :, 0:128], sq, ss, gain[:, 0, :], NT, ready=(core.loads.all(),))
        dve.wait(a)
        b = rms_rows(core, se[:, :, :], se, sq, ss, gain[:, 1, :], NS)
        core.barrier()
        for i in range(5):
            src = (lambda j: xr[:, 4 * i + j, 0:128]) if i < 4 else (lambda j: se[:, j, :])
            for j in range(4):
                m = pe.e.transpose(psum.bank(i)[:, j * P:(j + 1) * P], src(j), core.ident[:, :])
            m = pe.done(m)
            act.wait(m)
            act.done(act.e.activation(xrT[:, i * BANK:(i + 1) * BANK] if i < 4 else seT[:, :], psum.bank(i), ACT.Copy))
        core.barrier()
        read = [None] * 8
        for i in range(NT):
            b0 = i % 4
            pe.wait(read[b0])
            m = pe.done(pe.e.matmul(psum.bank(b0), xrT[:, i * P:(i + 1) * P], seT[:, :], start=True, stop=True))
            dve.wait(m)
            t = read[b0] = dve.done(dve.e.tensor_reduce(tokmax[:, i:i + 1], psum.bank(b0), AX.X, ALU.max, negate=True))
        for i in range(NS):
            for j in range(4):
                b0 = (4 * i + j) % 4
                pe.wait(read[b0])
                m = pe.done(pe.e.matmul(psum.bank(b0), seT[:, i * P:(i + 1) * P], xrT[:, j * BANK:(j + 1) * BANK], start=True, stop=True))
                dve.wait(m)
                t = read[b0] = dve.done(dve.e.tensor_reduce(slotpart[:, i, j:j + 1], psum.bank(b0), AX.X, ALU.max))
        dve.wait(t)
        t = dve.done(dve.e.tensor_reduce(slotmax[:, :], slotpart[:, :, :], AX.X, ALU.max, negate=True))
        pe.wait(t)
        for i in range(NT + NS):
            src = tokmax[:, i:i + 1] if i < NT else slotmax[:, i - NT:i - NT + 1]
            m = pe.e.matmul(psum.all[0:1, i * P:(i + 1) * P], src, core.ident[:, :], start=True, stop=True)
        m = pe.done(m)
        act.wait(m)
        act.done(act.e.activation(rows[:, :], psum.all[0:1, 0:T + BANK], ACT.Copy))
        core.barrier()
        read = [None] * 8
        eread = [None] * 2
        for i in range(NT):
            b0 = 4 + i % 2
            pe.wait(read[b0])
            pe.e.matmul(psum.bank(b0), xrT[:, i * P:(i + 1) * P], seT[:, :], start=True, stop=False)
            m = pe.done(pe.e.matmul(psum.bank(b0), core.onerow[:, 0:P], rows[:, T:T + BANK], start=False, stop=True))
            act.wait(m, eread[i % 2])
            t = read[b0] = act.done(act.e.activation(E[i % 2][:, :], psum.bank(b0), ACT.Exp))
            pe.wait(t)
            for j in range(NS):
                m = pe.e.matmul(psum.bank(j)[:, 0:129], E[i % 2][:, j * P:(j + 1) * P], xr[:, i, :], start=i == 0, stop=i == NT - 1)
            eread[i % 2] = pe.done(m)
        dve.wait(eread[1])
        for j in range(NS):
            t = dve.done(dve.e.reciprocal(rden[:, j:j + 1], psum.bank(j)[:, 128:129]))
            dve.wait(t)
            t = dve.done(dve.e.tensor_scalar(slots[:, j, :], psum.bank(j)[:, 0:128], rden[:, j:j + 1], None, ALU.mult))
        pe.wait(t)
        for j in range(NS):
            m = pe.e.transpose(psum.bank(0)[:, j * P:(j + 1) * P], slots[:, j, :], core.ident[:, :])
        m = pe.done(m)
        act.wait(m)
        t = act.done(act.e.activation(slotsT[:, :], psum.bank(0), ACT.Copy))
        pe.wait(t)
        for j in range(NS):
            m = pe.done(pe.e.matmul(psum.bank(1 + j), w1[:, j * P:(j + 1) * P], slotsT[:, :], start=True, stop=True))
            act.wait(m)
            t = act.done(act.e.activation(hid[:, j, :], psum.bank(1 + j), ACT.Gelu))
        pe.wait(t)
        for q in range(NS):
            for j in range(NS):
                m = pe.e.matmul(psum.bank(5)[:, q * P:(q + 1) * P], hid[:, j, q * P:(q + 1) * P], w2[:, j, :], start=j == 0, stop=j == NS - 1)
        m = pe.done(m)
        act.wait(m)
        act.done(act.e.activation(proc[:, :, 0:128], psum.bank(5).rearrange("p (q d) -> p q d", q=NS), ACT.Copy))
        core.barrier()
        read = [None] * 8
        cread = [None] * 2
        n = 0
        for c in range(4):
            s = slice(c * BANK, (c + 1) * BANK)
            for j in range(NS):
                b0 = n % 4
                n += 1
                pe.wait(read[b0])
                pe.e.matmul(psum.bank(b0), seT[:, j * P:(j + 1) * P], xrT[:, s], start=True, stop=False)
                m = pe.done(pe.e.matmul(psum.bank(b0), core.onerow[:, 0:P], rows[:, s], start=False, stop=True))
                act.wait(m, cread[c % 2])
                t = read[b0] = act.done(act.e.activation(Ct[c % 2][:, j, :], psum.bank(b0), ACT.Exp))
            pe.wait(t)
            for q in range(4):
                b0 = 4 + q
                y = psum.bank(b0)
                pe.wait(read[b0])
                for j in range(NS):
                    m = pe.e.matmul(y[:, 0:129], Ct[c % 2][:, j, q * P:(q + 1) * P], proc[:, j, :], start=j == 0, stop=j == NS - 1)
                cread[c % 2] = m = pe.done(m)
                i = 4 * c + q
                dve.wait(m)
                r = dve.done(dve.e.reciprocal(rden[:, i:i + 1], y[:, 128:129]))
                dve.wait(r)
                read[b0] = dve.done(dve.e.tensor_scalar(core.GATE[:, i, :], y[:, 0:128], rden[:, i:i + 1], None, ALU.mult))
        act.wait(read[7])
        act.done(act.e.activation(core.GATE[:, :, :], core.GATE[:, :, :], ACT.Silu))
        core.barrier()


def residual(core, ready=()):
    dve, pool = core.dve, core.pool
    dve.wait(*ready)
    for i in range(4):
        s = slice(4 * i, 4 * i + 4)
        m = dve.done(dve.e.tensor_tensor(core.GATE[:, s, :], core.GATE[:, s, :], core.SACC[:, s, :], ALU.mult))
        dve.wait(m)
        t = dve.done(dve.e.tensor_tensor(core.X[:, s, :], core.X[:, s, :], core.GATE[:, s, :], ALU.add))
    return t


def norm_layer(core, psum):
    with ExitStack() as ctx:
        core.ctx, keep = ctx, core.ctx
        n = Norm(core, f"N{core.layer}")
        core.ctx = keep
        made = n.run(lambda i: core.X[:, i, :], lambda i: core.XN[:, i, :])
        to_features(core, psum, core.XN, core.XNT, made)
        core.pool.done(core.pool.e.memset(core.SACC[:, :, :], 0.0))
        core.barrier()


START = 0


def program(nc, io, out, stop=99):
    with ExitStack() as ctx:
        core = Core(nc, ctx)
        psum = Psum(nc, ctx)
        sb = lambda n, s, d=F32: ctx.enter_context(nc.sbuf_tensor(n, s, d))
        core.X = sb("X", [P, NT, D])
        core.XN = sb("XN", [P, NT, D])
        core.XNT = sb("XNT", [P, T])
        core.SACC = sb("SACC", [P, NT, D])
        core.GATE = sb("GATE", [P, NT, D])
        core.ident = sb("ident", [P, P])
        core.identb = sb("identb", [P, P], BF16)
        core.ones = sb("ones", [P, 1])
        core.onerow = sb("onerow", [1, BANK])
        core.load(core.X[:, :, :], io["L0_attn_x"].rearrange("a (t p) d -> p (a t) d", p=P))
        core.load(core.ident[:, :], io["identity"])
        core.dve.wait(core.loads.all())
        core.dve.done(core.dve.e.tensor_copy(core.identb[:, :], core.ident[:, :]))
        core.dve.done(core.dve.e.memset(core.ones[:, :], 1.0))
        core.dve.done(core.dve.e.memset(core.onerow[:, :], 1.0))
        core.barrier()

        def layer(n, gate, attention):
            core.layer = n
            norm_layer(core, psum)
            gate()
            with ExitStack() as own:
                core.ctx = own
                attention()
                residual(core)
                core.barrier()
            core.ctx = ctx

        def attention0():
            core.maskq = core.ctx.enter_context(nc.sbuf_tensor("maskq", [P, 4, BANK], BF16))
            core.maskk = core.ctx.enter_context(nc.sbuf_tensor("maskk", [P, 4, BANK], BF16))
            core.load(core.maskq[:, :, :], io["mask_q"].bitcast(BF16))
            core.load(core.maskk[:, :, :], io["mask_k"].bitcast(BF16))
            run_groups(core, RotaryAttention(core, psum, io))

        def attention1():
            run_groups(core, LatentAttention(core, psum, io))

        if START < 1:
            layer(0, lambda: quantized_ffn(core, psum, io), attention0)
        if stop > 1 and START < 2:
            layer(1, lambda: transformer_gate(core, psum, io), attention1)
        if stop > 2 and START < 3:
            layer(2, lambda: ternary_ffn(core, psum, io), lambda: attention2(core, psum, io))
        if stop > 3:
            layer(3, lambda: soft_moe(core, psum, io), lambda: attention3(core, psum, io))

        core.stores.add(nc.sync.dma_start(out.rearrange("a (t p) d -> p (a t) d", p=P), core.X[:, :, :]))
        core.sp.wait(core.stores.all())


def bf16_bits(a):
    return np.ascontiguousarray((a.astype(np.float32).view(np.uint32) >> 16).astype(np.uint16))


def constants():
    c = {"identity": np.eye(P, dtype=np.float32)}
    inv = (1.0 / 10000.0 ** (np.arange(0, 32, 2, dtype=np.float32) / np.float32(32))).astype(np.float32)
    f = np.arange(T, dtype=np.float32)[:, None] * inv[None, :]
    cos, sin = np.cos(f).T.astype(np.float32), np.sin(f).T.astype(np.float32)
    rest = np.ones((32, T), np.float32)
    c["rope_cos"] = np.concatenate([cos, cos, rest] * 2)
    c["rope_sin"] = np.concatenate([-sin, sin, 0 * rest] * 2)
    p = np.arange(P)[:, None, None]
    j = np.arange(4)[None, :, None]
    x = np.arange(BANK)[None, None, :]
    c["mask_q"] = bf16_bits(np.where(x <= P * j + p, 0.0, NEG))
    c["mask_k"] = bf16_bits(np.where(P * j + p <= x, 0.0, NEG))
    half = np.arange(0, 64, 2, dtype=np.float32)
    inv = (1.0 / 10000.0 ** (half / np.float32(64))).astype(np.float32)
    t = np.arange(T, dtype=np.float32)
    f = t[:, None] * inv[None, :]
    base = ((half + np.float32(25.6)) / np.float32(89.6)).astype(np.float32)
    power = (t - np.float32(T // 2)) / np.float32(32.0)
    scale = np.power(base[None, :], power[:, None]).astype(np.float32)
    scale, cos, sin = (np.concatenate([y, y], 1) for y in (scale, np.cos(f), np.sin(f)))
    sign = np.where(np.arange(64) < 32, -1.0, 1.0).astype(np.float32)
    tabs = np.stack([cos * scale, sin * sign * scale, cos / scale, sin * sign / scale], 1).astype(np.float32)
    c["xpos"] = np.ascontiguousarray(tabs.reshape(NT, P, 4, 64).transpose(1, 0, 2, 3))
    q, k = np.arange(P)[:, None], np.arange(-P, P)[None, :]
    band = np.where((k <= q) & (q <= k + 64), 0.0, NEG)
    nokeys = np.where(k < 0, NEG, band)
    c["band_mask"] = bf16_bits(np.stack([nokeys, band]))
    c["first_masks"] = bf16_bits(np.stack([nokeys, band, band, band]))
    moves = np.zeros((P, 2, P), np.float32)
    moves[np.arange(P - 1), 0, np.arange(1, P)] = 1.0
    moves[P - 1, 1, 0] = 1.0
    c["row_moves"] = moves
    even = (np.arange(D) // 2 * 2).astype(np.float32)
    c["position_denominators"] = np.stack([np.power(np.float32(10000.0), np.float32(2.0) * even / np.float32(D)), 0.25 * (np.arange(D) % 2)], 1).astype(np.float32)
    last = np.zeros((P, 2, P), np.float32)
    last[0, :, P - 1] = (-992.0, -7.0)
    c["last_q"] = bf16_bits(last)
    c["last_k"] = bf16_bits(last.transpose(2, 1, 0))
    return c


TURN = ["L0_ffn_w_gate", "L0_ffn_w_up", "L0_ffn_w_down", "L1_attn_Wq", "L1_attn_Wkv_down", "L1_attn_Wk_up",
        "L1_attn_Wv_up", "L1_attn_Wo", "L2_attn_Wq", "L2_attn_Wk", "L2_attn_Wv", "L2_attn_Wo",
        "L2_ffn_w1_w", "L2_ffn_w2_w", "L2_ffn_h1_w", "L2_ffn_h2_w", "L2_ffn_w3_w"]


def kernel(**inputs):
    import concourse.bacc as bacc
    from concourse.bass_utils import run_bass_kernel_spmd

    arrays = {}
    for name, a in inputs.items():
        a = np.asarray(a)
        arrays[name] = np.ascontiguousarray(a.T if name in TURN else a)
    arrays.update(constants())
    nc = bacc.Bacc("TRN2", target_bir_lowering=False, num_devices=1)
    io = {n: nc.dram_tensor(n, a.shape, mybir.dt.from_np(a.dtype), kind="ExternalInput").ap() for n, a in arrays.items()}
    out = nc.dram_tensor("out", (1, T, D), F32, kind="ExternalOutput").ap()
    program(nc, io, out)
    r = run_bass_kernel_spmd(nc, [arrays], core_ids=[0])
    return r.results[0]["out"]
```

```python
from contextlib import ExitStack

import numpy as np

import concourse.bass as bass
from concourse import mybir

F32 = mybir.dt.float32
F32R = mybir.dt.float32r
BF16 = mybir.dt.bfloat16
I32 = mybir.dt.int32
ACT = mybir.ActivationFunctionType
ALU = mybir.AluOpType
AX = mybir.AxisListType

P = 128
T = 2048
NT = T // P
D = 128
BANK = 512
KC = 512
NEG = -1.0e30


class Queue:

    def __init__(self, nc, engine, name):
        self.e = engine
        self.sem = nc.alloc_semaphore("done_" + name)
        self.count = 0
        self.seen = {}

    def done(self, ins):
        ins.then_inc(self.sem, 1)
        self.count += 1
        return (self.sem, self.count)

    def wait(self, *tickets):
        for t in tickets:
            if t is not None and self.seen.get(t[0].num, 0) < t[1]:
                self.e.wait_ge(t[0], t[1])
                self.seen[t[0].num] = t[1]


class Loads:

    def __init__(self, nc, name):
        self.sem = nc.alloc_semaphore("loaded_" + name)
        self.count = 0

    def add(self, ins):
        ins.then_inc(self.sem, 16)
        self.count += 16

    def all(self):
        return (self.sem, self.count)


class Core:

    def __init__(self, nc, ctx):
        self.nc = nc
        self.ctx = ctx
        self.pe = Queue(nc, nc.tensor, "pe")
        self.act = Queue(nc, nc.scalar, "act")
        self.dve = Queue(nc, nc.vector, "dve")
        self.pool = Queue(nc, nc.gpsimd, "pool")
        self.sp = Queue(nc, nc.sync, "sp")
        self.loads = Loads(nc, "all")
        self.stores = Loads(nc, "out")
        self.queues = [self.pe, self.act, self.dve, self.pool, self.sp]
        self.sides = [Loads(nc, f"side{d}") for d in range(2)]
        self.transfers = [self.loads, self.stores] + self.sides
        self.counts = [q.sem for q in self.queues + self.transfers]

    def barrier(self):
        for l in self.transfers:
            if l.count:
                self.sp.wait(l.all())
        nums = [s.num for s in self.counts]
        assert nums == list(range(nums[0], nums[0] + len(nums)))
        self.nc.all_engine_barrier(sems_to_clear=range(nums[0], nums[0] + len(nums)))
        for q in self.queues:
            q.count = 0
            q.seen = {}
        for l in self.transfers:
            l.count = 0

    def load(self, out, in_, queue=None):
        q = queue or self.sp
        self.loads.add(q.e.dma_start(out, in_))


def free(ap):
    return ap.bitcast(F32)


class Attention:

    def __init__(self, core, psum, name, heads, hd, causal=False, last_key_mask=False, scale=1.0):
        self.c = core
        self.name = name
        self.hd = hd
        self.scale = scale
        self.wide = hd == 64
        self.G = 4 if hd == 8 else 2
        self.M = P // self.G
        self.groups = heads // self.G
        self.QC = 1024 // self.G
        self.nchunk = T // self.QC
        self.qt = self.QC // P
        self.causal = causal
        self.last_key_mask = last_key_mask
        self.row = 64 if self.wide else 96
        self.rows = P if self.wide else 96
        self.psum = psum
        self.vbias = [None, None]
        ctx, nc = core.ctx, core.nc
        sb = lambda n, s, d=F32: ctx.enter_context(nc.sbuf_tensor(name + "_" + n, s, d))
        G = self.G
        self.Ka = [[sb(f"Ka{d}{h}", [P, T], F32R) for h in range(G)] for d in range(2)]
        self.Kb = [[sb(f"Kb{d}{h}", [P, T], F32R) for h in range(G)] for d in range(2)] if self.wide else self.Ka
        self.Qa = [sb(f"Qa{h}", [P, 2 * BANK], F32R) for h in range(G)]
        self.Qb = [sb(f"Qb{h}", [P, 2 * BANK], F32R) for h in range(G)] if self.wide else self.Qa
        self.V = [sb(f"V{d}", [P, NT, G, self.M]) for d in range(2)]
        self.W = [sb(f"weights{i}", [P, 1024]) for i in range(4)]
        self.wsum = [sb(f"wsum{i}", [P, 1024]) for i in range(2)] if self.wide else None
        self.Wo = [sb(f"Wo{d}", [P, G // 2, 258]) for d in range(2)]
        self.OT = [sb(f"OT{i}", [P, self.QC]) for i in range(2)]
        self.stage = [sb(f"stage{i}", [P, BANK]) for i in range(2)]
        self.part = [sb(f"part{i}", [P, G, self.qt, T // KC]) for i in range(2)]
        self.negmax = [sb(f"negmax{i}", [P, G, self.qt]) for i in range(2)]
        self.rden = [sb(f"rden{i}", [P, 2]) for i in range(2)]
        self.arrived = core.sides
        self.scaled = None if self.wide else [sb(f"scaled{i}", [P, 2, D]) for i in range(2)]

    def once(self):
        c = self.c
        dve, pool = c.dve, c.pool
        zero, one = self.stage
        z = dve.done(dve.e.memset(zero[:, :], 0.0))
        z1 = dve.done(dve.e.memset(one[:, :], 1.0))
        dve.wait(z, z1)
        lo = self.row
        for t in [k for side in self.Kb for k in side] + self.Qb:
            for b in range(t.shape[1] // BANK):
                f = dve.done(dve.e.tensor_copy(t[lo:P, b * BANK:(b + 1) * BANK], zero[lo:P, :]))
        dve.wait(f)
        for t in [k for side in self.Kb for k in side]:
            for b in range(T // BANK):
                dve.done(dve.e.tensor_copy(t[lo:lo + 1, b * BANK:(b + 1) * BANK], one[lo:lo + 1, :]))
        for d in range(2):
            v = pool.done(pool.e.memset(self.V[d][:, :, :, :], 0.0))
            w = pool.done(pool.e.memset(self.Wo[d][:, :, :], 0.0))
            if not self.wide:
                pool.wait(v)
                pool.done(pool.e.memset(self.V[d][:, :, :, self.hd:self.hd + 1], 1.0))
                dve.wait(w)
                for h in range(self.G):
                    r = h * self.M + self.hd
                    dve.done(dve.e.tensor_copy(self.Wo[d][:, h // 2, 129 * (h % 2) + 128:129 * (h % 2) + 129], c.ident[:, r:r + 1]))
        c.barrier()

    def begin(self, banks):
        self.banks = banks
        self.bankread = [()] * len(banks)
        self.bank = -1
        self.staged = [(), ()]
        self.k = 0
        self.mxread = [None, None]
        self.mxn = 0
        self.qfree = {}
        self.kmade = {}
        self.qmade = {}
        self.vmade = {}
        self.s = 0
        self.chunks = 0
        self.exped, self.used, self.summed = {}, {}, {}
        self.otcopied, self.otread = {}, {}
        self.accw = {}
        self.turned_read = None
        self.un = 0
        self.rread = [None, None]
        self.units = []
        self.kused = None
        self.vread = {}

    def take(self):
        self.bank = (self.bank + 1) % len(self.banks)
        self.Y = self.banks[self.bank]
        self.c.pe.wait(*self.bankread[self.bank])

    def release(self, *readers):
        self.bankread[self.bank] = readers

    def fetch(self, side, g):
        c = self.c
        c.sp.wait((c.pe.sem, c.pe.count), (c.dve.sem, c.dve.count), (c.act.sem, c.act.count))
        self.load(side, g)

    def fetched(self, side):
        self.c.pe.wait(self.arrived[side].all())
        self.prepare(side)

    def prepare(self, side):
        pass

    def split(self, side, h, which, b, staged, i):
        c = self.c
        act, dve = c.act, c.dve
        st = self.stage[i]
        R = self.rows
        dve.wait(staged)
        high = None
        if which == 0:
            s = slice(b * BANK, (b + 1) * BANK)
            Xa = self.Ka[side][h]
            before = self.kfree
        else:
            s = slice(b % 2 * BANK, b % 2 * BANK + BANK)
            Xa = self.Qa[h]
            before = self.qfree.get(b % 2)
        dve.wait(before)
        hi = dve.done(dve.e.tensor_copy(Xa[0:R, s], st[0:R, :]))
        dve.wait(hi)
        if self.wide and which == 0:
            act.wait(staged, before)
            high = act.done(act.e.activation(self.Kb[side][h][0:64, s], st[0:64, :], ACT.Copy))
            last = dve.done(dve.e.tensor_tensor(Xa[64:P, s], st[64:P, :], free(Xa[64:P, s]), ALU.subtract))
        elif self.wide:
            last = dve.done(dve.e.tensor_tensor(self.Qb[h][0:64, s], st[0:64, :], free(Xa[0:64, s]), ALU.subtract))
        else:
            q = slice(32, 64) if which == 0 else slice(64, 96)
            c.pool.wait(hi, staged, (c.pool.sem, c.pool.count))
            last = c.pool.done(c.pool.e.tensor_tensor(Xa[q, s], st[q, :], free(Xa[q, s]), ALU.subtract))
        self.staged[i] = (last, high)
        if which == 0:
            self.kmade[side, b] = (last, high)
        else:
            self.qmade[b % 2, h] = (last,)

    def product(self, side, h, which, b, part):
        c = self.c
        w, src, K = self.proj(side, h, which)[part]
        self.take()
        s = slice(b * BANK, (b + 1) * BANK)
        return c.pe.done(c.pe.e.matmul(self.Y[0:self.rows, :], w[0:K, 0:self.rows], src[0:K, s], start=True, stop=True))

    def project(self, side, h, which, b):
        c = self.c

        def plain():
            made = self.product(side, h, which, b, 0)
            scale, bias = self.affine(side, h, which)
            i = self.k % 2
            self.k += 1
            st = self.stage[i]
            c.act.wait(made, *self.staged[i])
            got = c.act.done(c.act.e.activation(st[0:self.rows, :], self.Y[0:self.rows, :], ACT.Identity, scale=scale, bias=bias))
            self.release(got)
            self.split(side, h, which, b, got, i)

        return [plain]

    def vunit(self, side, b):
        c = self.c
        pe, act = c.pe, c.act
        hd, G = self.hd, self.G
        src, K = self.vsrc()
        self.take()
        for j in range(4):
            kt = 4 * b + j
            o = self.Y[:, j * P:j * P + G * hd]
            mm = pe.e.matmul(o, src[0:K, kt * P:(kt + 1) * P], self.Wv[side][0:K, 0:G * hd], start=True, stop=self.vbias[side] is None)
            if self.vbias[side] is not None:
                mm = pe.e.matmul(o, c.onerow[:, 0:P], self.vbias[side][:, 0:G * hd], start=False, stop=True)
        made = pe.done(mm)
        act.wait(made, self.vread.get(side))
        view = self.Y.rearrange("p (t x) -> p t x", t=4)[:, :, 0:G * hd].rearrange("p t (h d) -> p t h d", h=G)
        t = act.done(act.e.activation(self.V[side][:, 4 * b:4 * b + 4, :, 0:hd], view, ACT.Copy))
        self.release(t)
        self.vmade[side] = t

    def pieces(self, ch):
        out = []
        for h in range(self.G):
            for j in range(self.qt):
                n = (ch * self.qt + j) // 4 + 1 if self.causal else T // KC
                out += [(h, j, p, n) for p in range(n)]
        return out

    def columns(self, ch, j=0):
        return ch * self.QC % (2 * BANK) + j * P

    def piece(self, side, ch, slot, h, j, p, n):
        c = self.c
        tile = ch * self.qt + j
        i = self.mxn % 2
        self.mxn += 1
        ps = self.psum.MX[:, i * BANK:(i + 1) * BANK]
        q = slice(self.columns(ch, j), self.columns(ch, j) + P)
        extra = []
        if self.causal and p == tile // 4:
            extra = [(c.maskq[:, tile % 4, :], slice(0, KC))]
        if self.last_key_mask and tile == 0 and p == T // KC - 1:
            extra = [(c.lastq[:, x, :], slice(KC - P, KC)) for x in range(2)]
        c.pe.wait(self.mxread[i], *self.kmade.get((side, p), ()), *self.qmade.get((ch * self.QC // BANK % 2, h), ()))
        K = self.rows
        mm = c.pe.e.matmul(ps, self.Qa[h][0:K, q], self.Ka[side][h][0:K, p * KC:(p + 1) * KC], start=True, stop=not extra)
        for x, (b, w) in enumerate(extra):
            mm = c.pe.e.matmul(ps[:, w], c.identb[:, :], b, start=False, stop=x == len(extra) - 1)
        made = c.pe.done(mm)
        c.dve.wait(made)
        self.mxread[i] = c.dve.done(c.dve.e.tensor_reduce(self.part[slot][:, h, j, p:p + 1], ps, AX.X, ALU.max))

    def maxima(self, ch, slot):
        n = (ch * self.qt) // 4 + 1 if self.causal else T // KC
        dve = self.c.dve
        dve.wait(*self.mxread)
        self.maxed = dve.done(dve.e.tensor_reduce(self.negmax[slot][:, :, :], self.part[slot][:, :, :, 0:n], AX.X, ALU.max, negate=True))

    def shift(self, ch, slot):
        c = self.c
        MX, r, QC = self.psum.MX, self.row, self.QC
        c.pe.wait(self.maxed, *self.mxread)
        for h in range(self.G):
            for j in range(self.qt):
                o = (h * self.qt + j) * P
                mm = c.pe.e.matmul(MX[r:r + 1, o:o + P], self.negmax[slot][:, h, j:j + 1], c.ident[:, :], start=True, stop=True)
        made = c.pe.done(mm)
        block = ch * QC // BANK % 2
        a = self.columns(ch)
        for q in (c.act, c.dve):
            q.wait(made, self.qfree.get(block), *(t for h in range(self.G) for t in self.qmade.get((block, h), ())))
        for h in range(self.G):
            row, new = self.Qb[h][r:r + 1, a:a + QC], MX[r:r + 1, h * QC:(h + 1) * QC]
            if h < self.G // 2:
                first = c.act.done(c.act.e.activation(row, new, ACT.Copy))
            else:
                second = c.dve.done(c.dve.e.tensor_copy(row, new))
        self.mxread = [first, second]
        self.shifted = (first, second)

    def scores(self, side, ch, kt, s, between=()):
        c = self.c
        G, QC = self.G, self.QC
        buf = self.psum.S[:, (s % 2) * 1024:(s % 2) * 1024 + 1024]
        between = list(between)
        c.pe.wait(self.exped.get(s - 2), *(self.shifted if kt == 0 else ()), *self.kmade.get((side, kt // 4), ()))
        kk = slice(kt * P, (kt + 1) * P)
        a = self.columns(ch)
        qq = slice(a, a + QC)
        for h in range(G):
            o = buf[:, h * QC:(h + 1) * QC]
            extra = []
            if self.causal and kt >= ch * self.qt:
                extra = [(c.maskk[:, kt - ch * self.qt, :], slice(0, QC))]
            if self.last_key_mask and ch == 0 and kt == NT - 1:
                extra = [(c.lastk[:, x, :], slice(0, P)) for x in range(2)]
            mm = c.pe.e.matmul(o, self.Ka[side][h][:, kk], self.Qa[h][:, qq], start=True, stop=not (self.wide or extra))
            if self.wide:
                mm = c.pe.e.matmul(o, self.Kb[side][h][:, kk], self.Qb[h][:, qq], start=False, stop=not extra)
            for x, (b, w) in enumerate(extra):
                mm = c.pe.e.matmul(o[:, w], c.identb[:, :], b, start=False, stop=x == len(extra) - 1)
            if h == G - 1:
                made = c.pe.done(mm)
            elif self.wide and between:
                between.pop(0)()
        self.qfree[ch * QC // BANK % 2] = made
        self.kused = made
        for f in between:
            f()
        c.act.wait(made, *self.used.get(s - 4, ()))
        self.exped[s] = c.act.done(c.act.e.activation(self.W[s % 4][:, :], buf, ACT.Exp, scale=self.scale))

    def sums(self, s, kt, n):
        pool = self.c.pool
        if not self.wide or kt == 0:
            return ()
        acc = self.wsum[n % 2]
        a = self.W[(s - 1) % 4] if kt == 1 else acc
        pool.wait(self.exped[s], self.summed.get(s - 1), self.otread.get(n - 2))
        self.summed[s] = pool.done(pool.e.tensor_tensor(acc[:, :], a[:, :], self.W[s % 4][:, :], ALU.add))
        if kt == 1:
            self.used[s - 1] += (self.summed[s],)
        return (self.summed[s],)

    def values(self, side, kt, nk, s, n, between=()):
        c = self.c
        G, QC, M = self.G, self.QC, self.M
        O = self.psum.O
        c.pe.wait(self.exped[s])
        if kt == 0:
            c.pe.wait(self.vmade.get(side), self.otcopied.get(n - 1))
        for h in range(G):
            if h == G // 2:
                for f in between:
                    f()
            mm = c.pe.e.matmul(O[h * M:(h + 1) * M, 0:QC], self.V[side][:, kt, h, :], self.W[s % 4][:, h * QC:(h + 1) * QC], start=kt == 0, stop=kt == nk - 1)
        t = self.vread[side] = c.pe.done(mm)
        self.used[s] = (t,)
        self.used[s] += self.sums(s, kt, n)
        if kt == nk - 1:
            c.act.wait(t, self.otread.get(n - 2))
            self.otcopied[n] = c.act.done(c.act.e.activation(self.OT[n % 2][:, :], O[:, 0:QC], ACT.Copy))

    def unit(self, side, ch, n, s, j, half):
        c = self.c
        dve, acc = c.dve, c.SACC
        self.take()
        Y = self.Y
        tile = ch * self.qt + j
        c.pe.wait(self.otcopied[n], self.summed.get(s))
        mm = c.pe.e.matmul(Y[:, 0:258], self.OT[n % 2][:, j * P:(j + 1) * P], self.Wo[side][:, half, :], start=True, stop=True)
        if self.wide:
            for i in range(2):
                mm = c.pe.e.matmul(Y[:, 258 + i:259 + i], self.wsum[n % 2][:, i * self.QC + j * P:i * self.QC + (j + 1) * P], c.ones[:, 0:1], start=True, stop=True)
        made = self.otread[n] = c.pe.done(mm)
        r = self.rden[self.un % 2]
        dve.wait(made, self.rread[self.un % 2])
        t = dve.done(dve.e.reciprocal(r[:, :], Y[:, 258:260] if self.wide else Y[:, 128:258:129]))
        if self.wide:
            dve.wait(t, self.accw.get(tile))
            t = dve.done(dve.e.scalar_tensor_tensor(acc[:, tile, :], Y[:, 0:128], r[:, 0:1], acc[:, tile, :], ALU.mult, ALU.add))
            dve.wait(t)
            t = self.accw[tile] = read = dve.done(dve.e.scalar_tensor_tensor(acc[:, tile, :], Y[:, 129:257], r[:, 1:2], acc[:, tile, :], ALU.mult, ALU.add))
        else:
            two = self.scaled[self.un % 2]
            c.act.wait(t, self.rread[self.un % 2])
            for x in range(2):
                read = c.act.done(c.act.e.activation(two[:, x, :], Y[:, 129 * x:129 * x + 128], ACT.Copy, scale=r[:, x:x + 1]))
            c.pool.wait(read, self.accw.get(tile))
            for x in range(2):
                c.pool.wait((c.pool.sem, c.pool.count))
                t = self.accw[tile] = c.pool.done(c.pool.e.tensor_tensor(acc[:, tile, :], acc[:, tile, :], two[:, x, :], ALU.add))
        self.rread[self.un % 2] = t
        self.release(read)
        self.un += 1

    def qblock(self, side, b):
        return [u for h in range(self.G) for u in self.project(side, h, 1, b)]

    def keys(self, side):
        return [u for b in range(T // BANK) for h in range(self.G) for u in self.project(side, h, 0, b)]

    def preparation(self, side, ch, slot):
        per = BANK // self.QC
        pieces = [[lambda a=a: self.piece(side, ch, slot, *a) for a in self.pieces(ch) if a[0] == h] for h in range(self.G)]
        out = []
        if ch % per == 0:
            queries = [self.project(side, h, 1, ch // per) for h in range(self.G)]
            out += queries.pop(0)
        else:
            queries = []
        for h in range(self.G):
            if queries:
                out += queries.pop(0)
            out += pieces[h]
        return out + [lambda: self.maxima(ch, slot)]

    def first(self):
        self.begin([self.psum.Y] + [self.psum.bank(i) for i in range(4)])
        self.kfree = None
        self.fetch(0, 0)
        self.fetched(0)
        for f in self.keys(0) + self.qblock(0, 0) + [lambda b=b: self.vunit(0, b) for b in range(4)]:
            f()
        for a in self.pieces(0):
            self.piece(0, 0, 0, *a)
        self.maxima(0, 0)
        self.shift(0, 0)
        self.c.barrier()

    def stretch(self, plan):
        self.begin([self.psum.Y])
        self.shifted = ()
        G, per = self.G, BANK // self.QC
        for at, (side, nxt) in enumerate(plan):
            other = 1 - side
            steps = []
            for ch in range(self.nchunk):
                nk = (ch + 1) * self.qt if self.causal else NT
                steps += [(ch, kt, nk) for kt in range(nk)]
            self.kfree = self.kused
            ahead = []
            if nxt is not None:
                ahead = [lambda: self.fetched(other)] + self.keys(other) + [lambda b=b: self.vunit(other, b) for b in range(4)]
            last = len(steps) if self.causal else sum(1 for ch, kt, nk in steps if ch < self.nchunk - per)
            done, begun = 0, None
            if at == 0:
                self.scores(side, 0, 0, self.s)
            for i, (ch, kt, nk) in enumerate(steps):
                s = self.s
                n = self.chunks
                nch = (ch + 1) % self.nchunk
                nside = side if ch + 1 < self.nchunk else other
                more = ch + 1 < self.nchunk or nxt is not None
                if kt == 0:
                    todo = self.preparation(nside, nch, (n + 1) % 2) if more else []
                    total, due, turn = len(todo), max(2, nk - 2), None
                between = []
                while todo and (len(todo) > total - total * (kt + 1) // due or kt + 1 >= due):
                    between.append(todo.pop(0))
                    if not todo:
                        turn = kt + 1
                for f in between[:1]:
                    f()
                keep = 2 if len(between) > 3 or self.wide and len(between) == 2 else 1
                late = between[1 + keep:]
                between = between[1:1 + keep]
                if i + 1 < len(steps):
                    self.scores(side, steps[i + 1][0], steps[i + 1][1], s + 1, between)
                elif nxt is not None and at + 1 < len(plan):
                    self.scores(other, 0, 0, s + 1, between)
                else:
                    for f in between:
                        f()
                if begun is None and not self.units and nxt is not None:
                    begun = i + 5
                    self.fetch(other, nxt)
                if begun is not None and i >= begun:
                    want = min(len(ahead) + done, -(-(i - begun + 1) * (len(ahead) + done) // (last - begun - 1)))
                    while done < want and ahead:
                        ahead.pop(0)()
                        done += 1
                if kt == turn:
                    self.shift(nch, (n + 1) % 2)
                self.values(side, kt, nk, s, n, late)
                if self.units and (nk <= 8 or kt % 2):
                    self.unit(*self.units.pop(0))
                if kt == nk - 1:
                    while self.units:
                        self.unit(*self.units.pop(0))
                    self.units = [(side, ch, n, s, j, half) for j in range(self.qt) for half in range(G // 2)]
                    self.chunks += 1
                self.s += 1
        while self.units:
            self.unit(*self.units.pop(0))
        self.c.barrier()

    def run(self):
        self.first()
        if self.groups > 2:
            with self.c.nc.Fori(0, self.groups // 2 - 1) as i:
                self.stretch([(0, i * 2 + 1), (1, i * 2 + 2)])
        self.stretch([(0, self.groups - 1), (1, None)])


class RotaryAttention(Attention):

    def __init__(self, core, psum, io):
        super().__init__(core, psum, "L0", 16, 64, causal=True, scale=64 ** -0.5)
        c, nc, ctx = core, core.nc, core.ctx
        self.io = io
        sb = lambda n, s, d=F32: ctx.enter_context(nc.sbuf_tensor("L0_" + n, s, d))
        self.w = [[[sb(f"w{d}{h}{x}", [P, P]) for x in "kq"] for h in range(2)] for d in range(2)]
        self.wturned = [[[sb(f"wt{d}{h}{x}", [P, P]) for x in "kq"] for h in range(2)] for d in range(2)]
        self.Wv = [sb(f"Wv{d}", [P, P]) for d in range(2)]
        self.cosT = sb("cos", [P, T])
        self.sinT = sb("sin", [P, T])
        self.turned = sb("turned", [P, BANK])
        core.load(self.cosT[:, :], io["rope_cos"])
        core.load(self.sinT[:, :], io["rope_sin"])
        for t in (t for side in self.wturned for h in side for t in h):
            core.pool.done(nc.gpsimd.memset(t[:, :], 0.0))
        self.once()

    def load(self, side, g):
        io = self.io
        load = lambda o, i: self.arrived[side].add(self.c.nc.sync.dma_start(o, i))
        kv = io["L0_attn_w_kv"]
        for h in range(2):
            for x, src in enumerate((kv, io["L0_attn_w_q"])):
                w = src[:, bass.ds(g * P + h * 64, 64)]
                turned0 = src[:, bass.ds(g * P + h * 64 + 16, 16)]
                turned1 = src[:, bass.ds(g * P + h * 64, 16)]
                for half in (0, 64):
                    load(self.w[side][h][x][:, half:half + 64], w)
                    load(self.wturned[side][h][x][:, half:half + 16], turned0)
                    load(self.wturned[side][h][x][:, half + 16:half + 32], turned1)
            wo = io["L0_attn_w_out"][bass.ds(g * P + h * 64, 64), :]
            load(self.Wo[side][h * 64:h * 64 + 64, 0, 129 * h:129 * h + 128], wo)
        load(self.Wv[side][:, :], kv[:, bass.ds(g * P + 1024, P)])

    def proj(self, side, h, which):
        return [(self.w[side][h][which], self.c.XNT, P), (self.wturned[side][h][which], self.c.XNT, P)]

    def project(self, side, h, which, b):
        c = self.c
        s = slice(b * BANK, (b + 1) * BANK)

        def straight():
            made = self.product(side, h, which, b, 0)
            c.dve.wait(made, *self.staged[which])
            t = c.dve.done(c.dve.e.tensor_tensor(self.stage[which][:, :], self.Y, self.cosT[:, s], ALU.mult))
            self.release(t)

        def turned():
            made = self.product(side, h, which, b, 1)
            c.dve.wait(made, self.turned_read)
            t = c.dve.done(c.dve.e.tensor_tensor(self.turned[:, :], self.Y, self.sinT[:, s], ALU.mult))
            self.release(t)
            c.dve.wait(t)
            st = self.stage[which]
            c.dve.wait(t)
            got = self.turned_read = c.dve.done(c.dve.e.tensor_tensor(st[:, :], st[:, :], self.turned[:, :], ALU.add))
            self.split(side, h, which, b, got, which)

        return [straight, turned]

    def vsrc(self):
        return self.c.XNT, P


class LatentAttention(Attention):

    def __init__(self, core, psum, io):
        super().__init__(core, psum, "L1", 8, 32, scale=32 ** -0.5)
        c, nc, ctx = core, core.nc, core.ctx
        self.io = io
        sb = lambda n, s, d=F32: ctx.enter_context(nc.sbuf_tensor("L1_" + n, s, d))
        self.w = [[[sb(f"w{d}{h}{x}", [P, 96]) for x in "kq"] for h in range(2)] for d in range(2)]
        self.Wv = [sb(f"Wv{d}", [64, 64]) for d in range(2)]
        self.down = sb("down", [P, 64])
        self.latent = sb("latent", [64, T])
        core.load(self.down[:, :], io["L1_attn_Wkv_down"])
        c.pe.wait(c.loads.all())
        for b in range(4):
            s = slice(b * BANK, (b + 1) * BANK)
            ps = psum.S[0:64, s]
            made = c.pe.done(c.pe.e.matmul(ps, self.down[:, :], c.XNT[:, s], start=True, stop=True))
            c.act.wait(made)
            c.act.done(c.act.e.activation(self.latent[:, s], ps, ACT.Copy))
        self.once()

    def load(self, side, g):
        io = self.io
        load = lambda o, i: self.arrived[side].add(self.c.nc.sync.dma_start(o, i))
        for h in range(2):
            for third in range(3):
                s = slice(32 * third, 32 * third + 32)
                load(self.w[side][h][0][0:64, s], io["L1_attn_Wk_up"][:, bass.ds(g * 64 + h * 32, 32)])
                load(self.w[side][h][1][:, s], io["L1_attn_Wq"][:, bass.ds(g * 64 + h * 32, 32)])
            load(self.Wo[side][h * 64:h * 64 + 32, 0, 129 * h:129 * h + 128], io["L1_attn_Wo"][bass.ds(g * 64 + h * 32, 32), :])
        load(self.Wv[side][:, :], io["L1_attn_Wv_up"][:, bass.ds(g * 64, 64)])

    def proj(self, side, h, which):
        return [(self.w[side][h][which], (self.latent, self.c.XNT)[which], (64, P)[which])]

    def affine(self, side, h, which):
        return 1.0, 0.0

    def vsrc(self):
        return self.latent, 64


class NarrowAttention(Attention):

    def __init__(self, core, psum, io, factor, xp):
        super().__init__(core, psum, "L2", 16, 8)
        c, nc, ctx = core, core.nc, core.ctx
        self.io, self.factor, self.xp = io, factor, xp
        sb = lambda n, s, d=F32: ctx.enter_context(nc.sbuf_tensor("L2_" + n, s, d))
        self.w = [sb(f"w{d}", [P, 2, 4, 96]) for d in range(2)]
        self.bias = [sb(f"bias{d}", [96, 2, 4]) for d in range(2)]
        self.qbias = [sb(f"qbias{d}", [96, 4]) for d in range(2)]
        self.Wv = [sb(f"Wv{d}", [P, 32]) for d in range(2)]
        self.vbias = [sb(f"bv{d}", [1, 32]) for d in range(2)]
        for d in range(2):
            core.pool.done(nc.gpsimd.memset(self.w[d][:, :, :, :], 0.0))
            core.pool.done(nc.gpsimd.memset(self.bias[d][:, :, :], 0.0))
        self.once()

    def load(self, side, g):
        io = self.io
        load = lambda o, i: self.arrived[side].add(self.c.nc.sync.dma_start(o, i))
        for x, n in enumerate("kq"):
            W = io["L2_attn_W" + n][:, bass.ds(g * 32, 32)].rearrange("p (h d) -> p h d", h=4)
            b = io["L2_attn_b" + n][bass.ds(g * 32, 32)].rearrange("(h d) -> d h", h=4)
            for third in range(3):
                s = slice(32 * third, 32 * third + 8)
                load(self.w[side][:, x, :, s], W)
                with self.c.nc.allow_non_contiguous_dma("32 elements"):
                    load(self.bias[side][s, x, :], b)
        for h in range(4):
            load(self.Wo[side][h * 32:h * 32 + 8, h // 2, 129 * (h % 2):129 * (h % 2) + 128], io["L2_attn_Wo"][bass.ds(g * 32 + h * 8, 8), :])
        load(self.Wv[side][:, :], io["L2_attn_Wv"][:, bass.ds(g * 32, 32)])
        load(self.vbias[side][:, :], io["L2_attn_bv"][bass.ds(g * 32, 32)].rearrange("(a n) -> a n", a=1))

    def prepare(self, side):
        c = self.c
        c.dve.wait(self.arrived[side].all())
        t = c.dve.done(c.dve.e.tensor_scalar(self.qbias[side][:, :], self.bias[side][:, 1, :], self.factor[0:96, :], None, ALU.mult))
        c.act.wait(t)

    def proj(self, side, h, which):
        return [(self.w[side][:, which, h, :], self.xp, P)]

    def affine(self, side, h, which):
        if which:
            return self.factor[0:96, :], self.qbias[side][:, h:h + 1]
        return 1.0, self.bias[side][:, 0, h:h + 1]

    def vsrc(self):
        return self.xp, P


class NormedAttention(Attention):

    def __init__(self, core, psum, io, srcs):
        super().__init__(core, psum, "L3", 16, 64, last_key_mask=True)
        c, nc, ctx = core, core.nc, core.ctx
        self.io, self.srcs = io, srcs
        sb = lambda n, s, d=F32: ctx.enter_context(nc.sbuf_tensor("L3_" + n, s, d))
        self.w = [[[sb(f"w{d}{h}{x}", [P, P]) for x in "kq"] for h in range(2)] for d in range(2)]
        self.Wv = [sb(f"Wv{d}", [P, P]) for d in range(2)]
        self.bias = [sb(f"bias{d}", [P, 2, 2]) for d in range(2)]
        self.qbias = [sb(f"qbias{d}", [P, 2]) for d in range(2)]
        self.vbias = [sb(f"bv{d}", [1, P]) for d in range(2)]
        self.smax = 1.0 / float(D) ** 0.5
        self.once()

    def load(self, side, g):
        io = self.io
        load = lambda o, i: self.arrived[side].add(self.c.nc.sync.dma_start(o, i))
        for x, n in enumerate("kq"):
            for h in range(2):
                for half in (0, 64):
                    load(self.w[side][h][x][:, half:half + 64], io["L3_attn_W" + n][:, bass.ds(g * P + h * 64, 64)])
            for half in (0, 64):
                with self.c.nc.allow_non_contiguous_dma("128 elements"):
                    load(self.bias[side][half:half + 64, x, :], io["L3_attn_b" + n][bass.ds(g * P, P)].rearrange("(h d) -> d h", h=2))
        for h in range(2):
            load(self.Wo[side][h * 64:h * 64 + 64, 0, 129 * h:129 * h + 128], io["L3_attn_Wo"][bass.ds(g * P + h * 64, 64), :])
        load(self.Wv[side][:, :], io["L3_attn_Wv"][:, bass.ds(g * P, P)])
        load(self.vbias[side][:, :], io["L3_attn_bv"][bass.ds(g * P, P)].rearrange("(a n) -> a n", a=1))

    def prepare(self, side):
        c = self.c
        c.dve.wait(self.arrived[side].all())
        t = c.dve.done(c.dve.e.tensor_scalar(self.qbias[side][:, :], self.bias[side][:, 1, :], self.smax, None, ALU.mult))
        c.act.wait(t)

    def proj(self, side, h, which):
        return [(self.w[side][h][which], self.srcs[which], P)]

    def affine(self, side, h, which):
        if which:
            return self.smax, self.qbias[side][:, h:h + 1]
        return 1.0, self.bias[side][:, 0, h:h + 1]

    def vsrc(self):
        return self.srcs[2], P


class Psum:

    def __init__(self, nc, ctx):
        self.all = ctx.enter_context(nc.psum_tensor("banks", [P, 8 * BANK], F32))
        self.S = self.all[:, 0:4 * BANK]
        self.MX = self.all[:, 4 * BANK:6 * BANK]
        self.O = self.all[:, 6 * BANK:7 * BANK]
        self.Y = self.all[:, 7 * BANK:8 * BANK]

    def bank(self, i):
        return self.all[:, i * BANK:(i + 1) * BANK]


def rstd_of(core, var, eps, tmp, out, n):
    act, dve = core.act, core.dve
    a, b = tmp
    e = dve.done(dve.e.tensor_scalar(a, var, eps, None, ALU.add))
    act.wait(e)
    r = act.done(act.e.activation(b, a, ACT.Sqrt))
    dve.wait(r, e)
    y = dve.done(dve.e.reciprocal(out, b))
    dve.wait(y)
    t = dve.done(dve.e.tensor_tensor(b, out, out, ALU.mult))
    dve.wait(t)
    t = dve.done(dve.e.tensor_tensor(b, b, a, ALU.mult))
    dve.wait(t)
    t = dve.done(dve.e.tensor_scalar(b, b, -0.5, 1.5, ALU.mult, ALU.add))
    dve.wait(t)
    return dve.done(dve.e.tensor_tensor(out, out, b, ALU.mult))


class Norm:

    def __init__(self, core, name, n=NT):
        nc, ctx = core.nc, core.ctx
        self.c = core
        self.n = n
        sb = lambda x, s: ctx.enter_context(nc.sbuf_tensor(name + "_" + x, s, F32))
        self.stats = sb("stats", [P, n, 6])
        self.mv = sb("mv", [P, n, 2])
        self.a = sb("a", [P, n])
        self.b = sb("b", [P, n])
        self.rstd = sb("rstd", [P, n])

    def run(self, src, dst, eps=1e-5, ready=(), readers=()):
        dve = self.c.dve
        dve.wait(*ready)
        for i in range(self.n):
            t = dve.done(dve.e.bn_stats(self.stats[:, i, :], src(i)))
        dve.wait(t)
        for i in range(self.n):
            t = dve.done(dve.e.bn_aggr(self.mv[:, i, :], self.stats[:, i, :]))
        dve.wait(t)
        t = rstd_of(self.c, self.mv[:, :, 1], eps, (self.a[:, :], self.b[:, :]), self.rstd[:, :], self.n)
        dve.wait(t, *readers)
        out = []
        for i in range(self.n):
            out.append(dve.done(dve.e.tensor_scalar(dst(i), src(i), self.mv[:, i, 0:1], self.rstd[:, i:i + 1], ALU.subtract, ALU.mult)))
        return out


def to_features(core, psum, src, dst, made, scale=1.0, bias=0.0):
    pe, act = core.pe, core.act
    read = [None] * 2
    for b in range(4):
        ps = psum.bank(b % 2)
        pe.wait(read[b % 2], made[4 * b + 3])
        for j in range(4):
            m = pe.e.transpose(ps[:, j * P:(j + 1) * P], src[:, 4 * b + j, :], core.ident[:, :])
        m = pe.done(m)
        act.wait(m)
        read[b % 2] = act.done(act.e.activation(dst[:, b * BANK:(b + 1) * BANK], ps, ACT.Identity, scale=scale, bias=bias))
    return read[1]


def quantized_ffn(core, psum, io):
    nc = core.nc
    pe, act, dve = core.pe, core.act, core.dve
    with ExitStack() as ctx:
        sb = lambda n, s, d=F32: ctx.enter_context(nc.sbuf_tensor("F0_" + n, s, d))
        H = 384
        raw = [sb(f"raw{i}", [P, H], I32) for i in range(3)]
        w = [sb(f"w{i}", [P, H]) for i in range(3)]
        g = [sb(f"g{i}", [P, BANK]) for i in range(2)]
        h = sb("h", [P, 2, 3, BANK])
        core.load(raw[0][:, :], io["L0_ffn_w_gate"])
        core.load(raw[1][:, :], io["L0_ffn_w_up"])
        core.load(raw[2][:, :].rearrange("p (j d) -> p j d", j=3), io["L0_ffn_w_down"].rearrange("(j p) d -> p j d", p=P))
        dve.wait(core.loads.all())
        for i in range(3):
            ready = dve.done(dve.e.tensor_scalar(w[i][:, :], raw[i][:, :], 1.0 / 127.0, None, ALU.mult))
        pe.wait(ready)
        read = [None] * 8
        gread = [None] * 2
        hread = [None] * 2
        n = 0
        for c in range(4):
            s = slice(c * BANK, (c + 1) * BANK)
            for j in range(3):
                a, b = psum.bank(2 * (n % 2)), psum.bank(2 * (n % 2) + 1)
                pe.wait(read[2 * (n % 2)], read[2 * (n % 2) + 1])
                pe.e.matmul(a, w[0][:, j * P:(j + 1) * P], core.XNT[:, s], start=True, stop=True)
                made = pe.done(pe.e.matmul(b, w[1][:, j * P:(j + 1) * P], core.XNT[:, s], start=True, stop=True))
                act.wait(made, gread[n % 2])
                sg = read[2 * (n % 2)] = act.done(act.e.activation(g[n % 2][:, :], a, ACT.Silu))
                dve.wait(sg, hread[c % 2])
                up = read[2 * (n % 2) + 1] = gread[n % 2] = dve.done(dve.e.tensor_tensor(h[:, c % 2, j, :], g[n % 2][:, :], b, ALU.mult))
                n += 1
            y = psum.bank(4 + c % 2)
            pe.wait(up, read[4 + c % 2])
            for q in range(4):
                for j in range(3):
                    mm = pe.e.matmul(y[:, q * P:(q + 1) * P], h[:, c % 2, j, q * P:(q + 1) * P], w[2][:, j * P:(j + 1) * P], start=j == 0, stop=j == 2)
            hread[c % 2] = pe.done(mm)
            act.wait(hread[c % 2])
            read[4 + c % 2] = act.done(act.e.activation(core.GATE[:, 4 * c:4 * c + 4, :], y.rearrange("p (q d) -> p q d", q=4), ACT.Silu))
        core.barrier()


def transformer_gate(core, psum, io):
    nc = core.nc
    pe, act, dve, pool = core.pe, core.act, core.dve, core.pool
    HEADS, HID = 8, 341
    HT = [(0, 128), (128, 128), (256, 85)]
    with ExitStack() as ctx:
        sb = lambda n, s, d=F32: ctx.enter_context(nc.sbuf_tensor("F1_" + n, s, d))
        state = core.SACC
        xs = sb("xs", [P, 5, D])
        hT = sb("hT", [P, BANK])
        carry = sb("carry", [P, 1])
        wqkv = sb("wqkv", [P, 1536])
        wo = sb("wo", [P, 4, P])
        w1 = sb("w1", [P, 2 * HID])
        w2 = sb("w2", [P, 3, P])
        b1 = sb("b1", [P, 2, 3])
        b2 = sb("b2", [1, P])
        lgb = sb("lgb", [P, 2])
        gains = sb("gains", [P, 2, 64])
        tab = sb("tab", [P, 4, 4, 64])
        ssq = sb("ssq", [P, 3, 4, 2, HEADS])
        sq = [sb(f"sq{i}", [P, BANK]) for i in range(2)]
        qn = [[sb(f"{x}n{i}", [P, HEADS, 64]) for i in range(4)] for x in "qk"]
        rot = [sb(f"rot{i}", [P, HEADS, 64]) for i in range(2)]
        qT = [sb(f"qT{i}", [P, 4, P]) for i in range(2)]
        kT = sb("kT", [P, 4, 2, 5 * P])
        V = sb("V", [P, 5, BANK])
        mask = sb("mask", [P, 2, 256], BF16)
        maskf = sb("maskf", [P, 1])
        wts = [sb(f"wts{i}", [P, 4, 256]) for i in range(2)]
        wT = [sb(f"wT{i}", [P, 8, P]) for i in range(2)]
        nm = sb("nm", [P, 4, HEADS])
        den = sb("den", [P, 4, HEADS])
        o = [sb(f"o{i}", [P, BANK]) for i in range(2)]
        oT = [sb(f"oT{i}", [P, BANK]) for i in range(2)]
        z = sb("z", [P, 4, D])
        zT = sb("zT", [P, BANK])
        g = [sb(f"g{i}", [P, BANK]) for i in range(2)]
        u = sb("u", [P, 3, BANK])
        moves = sb("moves", [P, 2, P])
        st6, mv = sb("st6", [P, 4, 6]), sb("mv", [P, 4, 2])
        ra, rb, rstd = sb("ra", [P, 4]), sb("rb", [P, 4]), sb("rstd", [P, 4])
        S4 = psum.S
        core.load(moves[:, :, :], io["row_moves"])
        core.load(mask[:, 1, :], io["band_mask"].bitcast(BF16)[1])
        t = pool.done(pool.e.tensor_copy(state[:, :, :], core.XN[:, :, :]))
        pool.done(pool.e.memset(kT[:, :, :, :], 0.0))
        core.sp.wait(core.loads.all())
        core.barrier()
        for l in range(2):
            core.load(wqkv[:, :], io["L1_ffn_wqkv"][l])
            core.load(wo[:, :, :], io["L1_ffn_wo"][l].rearrange("(j p) d -> p j d", p=P))
            core.load(w1[:, :], io["L1_ffn_w1"][l])
            core.load(b2[:, :], io["L1_ffn_b2"][l].rearrange("(a d) -> a d", a=1))
            core.load(gains[:, 0, :], io["L1_ffn_q_scale"][l].partition_broadcast(P))
            core.load(gains[:, 1, :], io["L1_ffn_k_scale"][l].partition_broadcast(P))
            with nc.allow_non_contiguous_dma("small columns"):
                core.load(lgb[:, 0:1], io["L1_ffn_ln_g"][l].rearrange("(p a) -> p a", a=1))
                core.load(lgb[:, 1:2], io["L1_ffn_ln_b"][l].rearrange("(p a) -> p a", a=1))
                for j, (a, n) in enumerate(HT):
                    core.load(w2[0:n, j, :], io["L1_ffn_w2"][l][a:a + n, :])
                    for half in range(2):
                        core.load(b1[0:n, half, j:j + 1], io["L1_ffn_b1"][l][half * HID + a:half * HID + a + n].rearrange("(p a) -> p a", a=1))
            t = [pool.done(pool.e.memset(x, 0.0)) for x in (kT[:, :, :, 0:P], V[:, 0, :], xs[:, 0, :], carry[:, :])]
            core.sp.wait(core.loads.all())
            core.barrier()
            with nc.Fori(0, 4) as c:
                core.load(tab[:, :, :, :], io["xpos"][:, bass.ds(c * 4, 4), :, :])
                core.load(mask[:, 0, :], io["first_masks"].bitcast(BF16)[bass.ds(c, 1), :, :].rearrange("a p k -> p (a k)"))
                m = dve.done(dve.e.tensor_copy(xs[:, 1:5, :], state[:, bass.ds(c * 4, 4), :]))
                pe.wait(m)
                for j in range(4):
                    m = pe.e.transpose(psum.bank(0)[:, j * P:(j + 1) * P], xs[:, 1 + j, :], core.ident[:, :])
                m = pe.done(m)
                act.wait(m)
                a0 = act.done(act.e.activation(hT[0:64, :], psum.bank(0)[0:64, :], ACT.Copy))
                act.done(act.e.activation(hT[64:P, 1:BANK], psum.bank(0)[64:P, 0:BANK - 1], ACT.Copy))
                m = act.done(act.e.activation(hT[64:P, 0:1], carry[64:P, :], ACT.Copy))
                act.wait(m)
                hmade = act.done(act.e.activation(carry[64:P, :], psum.bank(0)[64:P, BANK - 1:BANK], ACT.Copy))
                dve.wait(core.loads.all())
                pe.wait(core.loads.all())
                for x in range(2):
                    gx = gains[:, x:x + 1, :]
                    dve.done(dve.e.tensor_tensor(tab[:, :, 2 * x, :], tab[:, :, 2 * x, :], gx.to_broadcast([P, 4, 64]), ALU.mult))
                    dve.done(dve.e.tensor_tensor(tab[:, :, 2 * x + 1, 0:32], tab[:, :, 2 * x + 1, 0:32], gx[:, :, 32:64].to_broadcast([P, 4, 32]), ALU.mult))
                    tabs = dve.done(dve.e.tensor_tensor(tab[:, :, 2 * x + 1, 32:64], tab[:, :, 2 * x + 1, 32:64], gx[:, :, 0:32].to_broadcast([P, 4, 32]), ALU.mult))
                read = [None] * 8
                n = 0
                sqread = [None] * 2
                pe.wait(hmade)
                for i in range(4):
                    for x in range(3):
                        b0 = n % 8
                        n += 1
                        ps = psum.bank(b0)
                        pe.wait(read[b0])
                        m = pe.done(pe.e.matmul(ps, hT[:, i * P:(i + 1) * P], wqkv[:, x * BANK:(x + 1) * BANK], start=True, stop=True))
                        act.wait(m)
                        if x == 2:
                            vmade = read[b0] = act.done(act.e.activation(V[:, 1 + i, :], ps, ACT.Copy))
                            continue
                        act.wait(sqread[x])
                        s2 = act.done(act.e.activation(sq[x][:, :], ps, ACT.Square))
                        dve.wait(s2)
                        copied = read[b0] = dve.done(dve.e.tensor_copy(qn[x][i][:, :, :], ps.rearrange("p (h d) -> p h d", h=HEADS)))
                        sqread[x] = dve.done(dve.e.tensor_reduce(ssq[:, 0, i, x, :], sq[x][:, :].rearrange("p (h d) -> p h d", h=HEADS), AX.X, ALU.add))
                A, B, C = (ssq[:, i, :, :, :] for i in range(3))
                act.wait(sqread[0], sqread[1])
                m = act.done(act.e.activation(B, A, ACT.Sqrt))
                dve.wait(m, sqread[1])

                def chain(ins):
                    t = dve.done(ins)
                    dve.wait(t)
                    return t

                chain(dve.e.tensor_scalar(B, B, 1e-12, None, ALU.max))
                chain(dve.e.reciprocal(C, B))
                chain(dve.e.tensor_tensor(C, C, A, ALU.mult))
                chain(dve.e.tensor_tensor(B, B, C, ALU.add))
                chain(dve.e.tensor_scalar(B, B, 0.5, 1e-12, ALU.mult, ALU.max))
                chain(dve.e.reciprocal(A, B))
                dve.wait(copied, tabs)
                rread = [None] * 2
                turned = {}

                def rotate(i, x):
                    v = qn[x][i]
                    over = lambda y, w=64: y.to_broadcast([P, HEADS, w])
                    chain(dve.e.tensor_tensor(v[:, :, :], v[:, :, :], ssq[:, 0, i, x, :].rearrange("p (h a) -> p h a", a=1).to_broadcast([P, HEADS, 64]), ALU.mult))
                    r = rot[x]
                    dve.wait(rread[x])
                    dve.done(dve.e.tensor_tensor(r[:, :, 0:32], v[:, :, 32:64], over(tab[:, i, 2 * x + 1:2 * x + 2, 0:32], 32), ALU.mult))
                    m = dve.done(dve.e.tensor_tensor(r[:, :, 32:64], v[:, :, 0:32], over(tab[:, i, 2 * x + 1:2 * x + 2, 32:64], 32), ALU.mult))
                    dve.wait(m)
                    m = dve.done(dve.e.tensor_tensor(v[:, :, :], v[:, :, :], over(tab[:, i, 2 * x:2 * x + 1, :]), ALU.mult))
                    pool.wait(m)
                    rread[x] = turned[x, i] = pool.done(pool.e.tensor_tensor(v[:, :, :], v[:, :, :], r[:, :, :], ALU.add))

                free4 = list(read[4:8])
                bufread = [(read[0], read[1]), (read[2], read[3])]
                qmade, kmade, qused = [None] * 4, [None] * 4, [None] * 2
                expd, wread = [None] * 8, [None] * 8
                copied, pvread = [None] * 8, [None] * 8
                xnew = [None] * 4

                def keys(i):
                    ps = psum.bank(4)
                    pe.wait(free4[0], turned[1, i])
                    for j in range(4):
                        m = pe.e.transpose(ps[:, j * P:(j + 1) * P], qn[1][i][:, 2 * j:2 * j + 2, :].rearrange("p h d -> p (h d)"), core.ident[:, :])
                    m = pe.done(m)
                    act.wait(m)
                    ps = ps.rearrange("p (j t) -> p j t", j=4)
                    s = slice((1 + i) * P, (2 + i) * P)
                    act.done(act.e.activation(kT[0:64, :, 0, s], ps[0:64, :, :], ACT.Copy))
                    kmade[i] = free4[0] = act.done(act.e.activation(kT[64:P, :, 1, s], ps[64:P, :, :], ACT.Copy))

                def queries(i):
                    ps = psum.bank(4)
                    pe.wait(free4[0], turned[0, i])
                    for j in range(4):
                        m = pe.e.transpose(ps[:, j * P:(j + 1) * P], qn[0][i][:, 2 * j:2 * j + 2, :].rearrange("p h d -> p (h d)"), core.ident[:, :])
                    m = pe.done(m)
                    act.wait(m, qused[i % 2])
                    qmade[i] = free4[0] = act.done(act.e.activation(qT[i % 2][:, :, :], ps.rearrange("p (j t) -> p j t", j=4), ACT.Copy))

                def softmax(v):
                    i, hs = v // 2, slice(4 * (v % 2), 4 * (v % 2) + 4)
                    S = S4[:, (v % 2) * 1024:(v % 2) * 1024 + 1024]
                    pe.wait(qmade[i], kmade[i], *bufread[v % 2])
                    for x in range(4):
                        h = hs.start + x
                        so = S[:, x * 256:(x + 1) * 256]
                        pe.e.matmul(so, qT[i % 2][:, h // 2, :], kT[:, h // 2, h % 2, i * P:(i + 2) * P], start=True, stop=False)
                        m = pe.e.matmul(so, core.identb[:, :], mask[:, min(i, 1), :], start=False, stop=True)
                    m = qused[i % 2] = pe.done(m)
                    dve.wait(m)
                    m = dve.done(dve.e.tensor_reduce(nm[:, i, hs], S.rearrange("p (h k) -> p h k", h=4), AX.X, ALU.max, negate=True))
                    dve.wait(m)
                    m = dve.done(dve.e.tensor_scalar(nm[:, i, hs], nm[:, i, hs], 8.0, None, ALU.mult))
                    act.wait(m, wread[v - 2] if v > 1 else None)
                    for x in range(4):
                        h = hs.start + x
                        m = act.done(act.e.activation(wts[v % 2][:, x, :], S[:, x * 256:(x + 1) * 256], ACT.Exp, bias=nm[:, i, h:h + 1], scale=8.0, accum_out=den[:, i, h:h + 1]))
                    expd[v] = m

                def turn(v):
                    S = S4[:, (v % 2) * 1024:(v % 2) * 1024 + 1024]
                    pe.wait(expd[v])
                    for x in range(8):
                        m = pe.e.transpose(S[:, x * P:(x + 1) * P], wts[v % 2][:, x // 2, x % 2 * P:(x % 2 + 1) * P], core.ident[:, :])
                    m = wread[v] = pe.done(m)
                    dve.wait(m, pvread[v - 2] if v > 1 else None)
                    copied[v] = dve.done(dve.e.tensor_copy(wT[v % 2][:, :, :].rearrange("p a b -> p (a b)"), S))
                    bufread[v % 2] = (copied[v],)

                def heads(v):
                    i = v // 2
                    ps = psum.bank(5)
                    pe.wait(copied[v], vmade)
                    if v % 2 == 0:
                        pe.wait(free4[1])
                    for x in range(4):
                        h = 4 * (v % 2) + x
                        for k in range(2):
                            m = pe.e.matmul(ps[:, h * 64:(h + 1) * 64], wT[v % 2][:, 2 * x + k, :], V[:, i + k, h * 64:(h + 1) * 64], start=k == 0, stop=k == 1)
                    m = pvread[v] = pe.done(m)
                    if v % 2:
                        dve.wait(expd[v], expd[v - 1])
                        rden = dve.done(dve.e.reciprocal(den[:, i, :], den[:, i, :]))
                        dve.wait(m, rden, oused[i % 2])
                        free4[1] = dve.done(dve.e.tensor_tensor(o[i % 2][:, :].rearrange("p (h d) -> p h d", h=HEADS), ps.rearrange("p (h d) -> p h d", h=HEADS), den[:, i, :].rearrange("p (h a) -> p h a", a=1).to_broadcast([P, HEADS, 64]), ALU.mult))

                oused, oTmade, oTused = [None] * 2, [None] * 4, [None] * 2

                def turn_heads(i):
                    ps = psum.bank(6)
                    pe.wait(free4[1], free4[2])
                    for j in range(4):
                        m = pe.e.transpose(ps[:, j * P:(j + 1) * P], o[i % 2][:, j * P:(j + 1) * P], core.ident[:, :])
                    m = oused[i % 2] = pe.done(m)
                    act.wait(m, oTused[i % 2])
                    oTmade[i] = free4[2] = act.done(act.e.activation(oT[i % 2][:, :], ps, ACT.Copy))

                def join_heads(i):
                    ps = psum.bank(7)
                    pe.wait(oTmade[i], free4[3])
                    for j in range(4):
                        m = pe.e.matmul(ps[:, 0:P], oT[i % 2][:, j * P:(j + 1) * P], wo[:, j, :], start=j == 0, stop=j == 3)
                    m = oTused[i % 2] = pe.done(m)
                    dve.wait(m)
                    xnew[i] = free4[3] = dve.done(dve.e.tensor_tensor(xs[:, 1 + i, :], xs[:, 1 + i, :], ps[:, 0:P], ALU.add))

                rotate(0, 1)
                rotate(0, 0)
                keys(0)
                queries(0)
                softmax(0)
                rotate(1, 1)
                rotate(1, 0)
                for v in range(11):
                    if v < 7:
                        softmax(v + 1)
                    if 1 <= v <= 8:
                        heads(v - 1)
                    if v < 8:
                        turn(v)
                    if v % 2 == 0 and v // 2 + 1 < 4:
                        keys(v // 2 + 1)
                        queries(v // 2 + 1)
                    if v // 2 + 2 < 4:
                        rotate(v // 2 + 2, 1 - v % 2)
                    if v == 7:
                        pool.wait(qused[0], qused[1], kmade[3])
                        pool.done(pool.e.tensor_copy(kT[:, :, :, 0:P], kT[:, :, :, 4 * P:5 * P]))
                    if v == 3:
                        pool.wait(pvread[1], vmade)
                        pool.done(pool.e.tensor_copy(V[:, 0, :], V[:, 4, :]))
                    if v >= 2 and v % 2 == 0 and v // 2 - 1 < 4:
                        turn_heads(v // 2 - 1)
                    if v >= 3 and v % 2 and v // 2 - 1 < 4:
                        join_heads(v // 2 - 1)
                sread = bufread[0] + bufread[1]
                bs = [4, 5, 6, 7]
                for i in range(4):
                    ps = psum.bank(bs[i])
                    pe.wait(xnew[i], free4[bs[i] - 4])
                    pe.e.matmul(ps[:, 0:64], core.ident[:, :], xs[:, 1 + i, 0:64], start=True, stop=True)
                    pe.e.matmul(ps[:, 64:P], moves[:, 0, :], xs[:, 1 + i, 64:P], start=True, stop=False)
                    m = pe.done(pe.e.matmul(ps[:, 64:P], moves[:, 1, :], xs[:, i, 64:P], start=False, stop=True))
                    dve.wait(m)
                    t = dve.done(dve.e.bn_stats(st6[:, i, :], ps[:, 0:P]))
                dve.wait(t)
                for i in range(4):
                    t = dve.done(dve.e.bn_aggr(mv[:, i, :], st6[:, i, :]))
                dve.wait(t)
                t = rstd_of(core, mv[:, :, 1], 1e-5, (ra[:, :], rb[:, :]), rstd[:, :], 4)
                dve.wait(t)
                for i in range(4):
                    t = free4[bs[i] - 4] = dve.done(dve.e.tensor_scalar(z[:, i, :], psum.bank(bs[i])[:, 0:P], mv[:, i, 0:1], rstd[:, i:i + 1], ALU.subtract, ALU.mult))
                pe.wait(t, *sread)
                for i in range(4):
                    m = pe.e.transpose(psum.bank(0)[:, i * P:(i + 1) * P], z[:, i, :], core.ident[:, :])
                m = pe.done(m)
                act.wait(m, core.loads.all())
                m = act.done(act.e.activation(zT[:, :], psum.bank(0), ACT.Identity, scale=lgb[:, 0:1], bias=lgb[:, 1:2]))
                pe.wait(m)
                for j, (a, w) in enumerate(HT):
                    pa, pg = psum.bank(1 + j), psum.bank(4 + j)
                    pe.wait(free4[j])
                    pe.e.matmul(pa[0:w, :], w1[:, a:a + w], zT[:, :], start=True, stop=True)
                    m = pe.done(pe.e.matmul(pg[0:w, :], w1[:, HID + a:HID + a + w], zT[:, :], start=True, stop=True))
                    act.wait(m)
                    if j == 2:
                        act.wait(umade)
                    m = act.done(act.e.activation(g[j % 2][0:w, :], pg[0:w, :], ACT.Gelu, bias=b1[0:w, 1, j:j + 1]))
                    dve.wait(m)
                    t = dve.done(dve.e.scalar_tensor_tensor(u[0:w, j, :], pa[0:w, :], b1[0:w, 0, j:j + 1], g[j % 2][0:w, :], ALU.add, ALU.mult))
                    if j == 0:
                        umade = t
                pe.wait(t, free4[3])
                ps = psum.bank(7)
                for i in range(4):
                    for j, (a, w) in enumerate(HT):
                        pe.e.matmul(ps[:, i * P:(i + 1) * P], u[0:w, j, i * P:(i + 1) * P], w2[0:w, j, :], start=j == 0, stop=False)
                    m = pe.e.matmul(ps[:, i * P:(i + 1) * P], core.onerow[:, 0:P], b2[:, :], start=False, stop=True)
                m = pe.done(m)
                dve.wait(m)
                t = dve.done(dve.e.tensor_tensor(state[:, bass.ds(c * 4, 4), :], xs[:, 1:5, :], ps.rearrange("p (i d) -> p i d", i=4), ALU.add))
                pool.wait(t, m)
                pool.done(pool.e.tensor_copy(xs[:, 0, :], xs[:, 4, :]))
                core.barrier()
        act.done(act.e.activation(core.GATE[:, :, :], state[:, :, :], ACT.Silu))
        core.barrier()
        pool.done(pool.e.memset(state[:, :, :], 0.0))
        core.barrier()


def ternary_ffn(core, psum, io):
    nc = core.nc
    pe, act, dve = core.pe, core.act, core.dve
    with ExitStack() as ctx:
        sb = lambda n, s, d=F32: ctx.enter_context(nc.sbuf_tensor("F2_" + n, s, d))
        H = 512
        w1, w2 = sb("w1", [P, H]), sb("w2", [P, H])
        h1, h2 = sb("h1", [P, 4, H]), sb("h2", [P, 4, H])
        w3 = sb("w3", [P, 4, P])
        s3 = sb("s3", [P, P])
        sc = sb("sc", [P, 4, 4])
        a = [sb(f"a{i}", [P, BANK]) for i in range(2)]
        u = [sb(f"u{i}", [P, 4, BANK]) for i in range(3)]
        core.load(w1[:, :], io["L2_ffn_w1_w"])
        core.load(w2[:, :], io["L2_ffn_w2_w"])
        for t, n in ((h1, "h1_w"), (h2, "h2_w"), (w3, "w3_w")):
            core.load(t[:, :, :], io["L2_ffn_" + n].rearrange("(j p) o -> p j o", p=P))
        core.load(s3[:, :], io["L2_ffn_w3_s"].partition_broadcast(P))
        with nc.allow_non_contiguous_dma("512 scales"):
            for i, n in enumerate(("w1_s", "w2_s", "h1_s", "h2_s")):
                core.load(sc[:, i, :], io["L2_ffn_" + n].rearrange("(j p) -> p j", p=P))
        dve.wait(core.loads.all())
        for j in range(4):
            ready = dve.done(dve.e.tensor_tensor(w3[:, j, :], w3[:, j, :], s3[:, :], ALU.mult))
        pe.wait(core.loads.all(), ready)
        act.wait(core.loads.all())
        read = [None] * 8
        n = 0
        aread = [None] * 2
        uread = [None] * 3
        for c in range(4):
            s = slice(c * BANK, (c + 1) * BANK)
            for j in range(4):
                js = slice(j * P, (j + 1) * P)
                b0, b1 = n % 8, (n + 1) % 8
                n += 2
                p0, p1 = psum.bank(b0), psum.bank(b1)
                pe.wait(read[b0], read[b1])
                pe.e.matmul(p0, w1[:, js], core.XNT[:, s], start=True, stop=True)
                made = pe.done(pe.e.matmul(p1, w2[:, js], core.XNT[:, s], start=True, stop=True))
                act.wait(made, aread[j % 2])
                sg = read[b0] = act.done(act.e.activation(a[j % 2][:, :], p0, ACT.Silu, scale=sc[:, 0, j:j + 1]))
                dve.wait(sg, uread[0])
                last = read[b1] = aread[j % 2] = dve.done(dve.e.scalar_tensor_tensor(u[0][:, j, :], p1, sc[:, 1, j:j + 1], a[j % 2][:, :], ALU.mult, ALU.mult))
            for layer, w in ((1, h1), (2, h2)):
                for j in range(4):
                    b0 = n % 8
                    n += 1
                    p0 = psum.bank(b0)
                    pe.wait(read[b0], last)
                    for i in range(4):
                        mm = pe.e.matmul(p0, w[:, i, j * P:(j + 1) * P], u[layer - 1][:, i, :], start=i == 0, stop=i == 3)
                    uread[layer - 1] = made = pe.done(mm)
                    act.wait(made, uread[layer])
                    nxt = read[b0] = act.done(act.e.activation(u[layer][:, j, :], p0, ACT.Gelu, scale=sc[:, layer + 1, j:j + 1]))
                last = nxt
            b0 = n % 8
            n += 1
            y = psum.bank(b0)
            pe.wait(read[b0], last)
            for q in range(4):
                for j in range(4):
                    mm = pe.e.matmul(y[:, q * P:(q + 1) * P], u[2][:, j, q * P:(q + 1) * P], w3[:, j, :], start=j == 0, stop=j == 3)
            uread[2] = made = pe.done(mm)
            act.wait(made)
            read[b0] = act.done(act.e.activation(core.GATE[:, 4 * c:4 * c + 4, :], y.rearrange("p (q d) -> p q d", q=4), ACT.Silu))
        core.barrier()


def attention2(core, psum, io):
    nc, ctx = core.nc, core.ctx
    pe, act, dve, pool = core.pe, core.act, core.dve, core.pool
    sb = lambda n, s, d=F32: ctx.enter_context(nc.sbuf_tensor("A2_" + n, s, d))
    rby = sb("rby", [P, 3])
    f = sb("f", [P, 8])
    factor = sb("factor", [P, 1])
    denom = sb("denom", [P, 2])
    core.load(denom[:, :], io["position_denominators"])
    core.load(rby[:, :], io["L2_attn_rby"].partition_broadcast(P))
    dve.wait(core.loads.all())
    red, blue, yellow = rby[:, 0:1], rby[:, 1:2], rby[:, 2:3]

    def chain(ins):
        t = dve.done(ins)
        dve.wait(t)
        return t

    chain(dve.e.tensor_scalar(f[:, 0:1], red, 0.1, 1.0, ALU.mult, ALU.add))
    chain(dve.e.scalar_tensor_tensor(f[:, 0:1], blue, 0.05, f[:, 0:1], ALU.mult, ALU.add))
    chain(dve.e.scalar_tensor_tensor(f[:, 0:1], yellow, 0.15, f[:, 0:1], ALU.mult, ALU.add))
    chain(dve.e.tensor_scalar(f[:, 1:2], red, 0.0, 1.0, ALU.mult, ALU.add))
    chain(dve.e.tensor_scalar(f[:, 1:2], f[:, 1:2], float(1.0 / np.sqrt(8.0)), None, ALU.mult))
    chain(dve.e.tensor_tensor(factor[:, :], f[:, 0:1], f[:, 1:2], ALU.mult))
    chain(dve.e.tensor_scalar(f[:, 2:3], yellow, float(0.1 * np.sin(np.pi)), 1.0, ALU.mult, ALU.add))
    chain(dve.e.tensor_scalar(f[:, 3:4], blue, 0.1, 1.0, ALU.mult, ALU.add))
    chain(dve.e.tensor_scalar(f[:, 3:4], f[:, 3:4], 1e-5, None, ALU.mult))
    chain(dve.e.tensor_scalar(f[:, 4:5], red, 0.1, 1.0, ALU.mult, ALU.add))
    chain(dve.e.scalar_tensor_tensor(f[:, 4:5], yellow, 0.05, f[:, 4:5], ALU.mult, ALU.add))
    xp = sb("xp", [P, T])
    xpt = sb("xpt", [P, NT, D])
    with ExitStack() as tmp:
        st = lambda n, s, d=F32: tmp.enter_context(nc.sbuf_tensor("A2p_" + n, s, d))
        pos = st("pos", [P, T])
        turns = st("turns", [P, T])
        whole = st("whole", [P, T], I32)
        iota = pool.done(pool.e.iota(pos[:, :], pattern=[[1, T]], base=0, channel_multiplier=0, allow_small_or_imprecise_dtypes=True))
        dve.wait(iota)
        chain(dve.e.tensor_scalar(f[:, 5:6], yellow, float(0.1 * np.sin(np.pi / 2)), 1.0, ALU.mult, ALU.add))
        chain(dve.e.tensor_tensor(f[:, 5:6], f[:, 5:6], denom[:, 0:1], ALU.mult))
        chain(dve.e.reciprocal(f[:, 6:7], f[:, 5:6]))
        chain(dve.e.tensor_scalar(pos[:, :], pos[:, :], f[:, 6:7], None, ALU.mult))
        chain(dve.e.tensor_scalar(turns[:, :], pos[:, :], float(1 / (2 * np.pi)), denom[:, 1:2], ALU.mult, ALU.add))
        chain(dve.e.tensor_copy(whole[:, :], turns[:, :]))
        chain(dve.e.tensor_copy(turns[:, :], whole[:, :]))
        rest = 2 * np.pi
        for bits in (2 ** 5, 2 ** 17, None):
            part = float(np.floor(rest * bits) / bits) if bits else float(np.float32(rest))
            rest -= part
            chain(dve.e.scalar_tensor_tensor(pos[:, :], turns[:, :], -part, pos[:, :], ALU.mult, ALU.add))
        chain(dve.e.tensor_scalar(f[:, 7:8], denom[:, 1:2], float(np.float32(2 * np.pi)), None, ALU.mult))
        chain(dve.e.tensor_scalar(pos[:, :], pos[:, :], f[:, 7:8], 3.1415925, ALU.add, ALU.min))
        t = chain(dve.e.tensor_scalar(pos[:, :], pos[:, :], -3.1415925, None, ALU.max))
        act.wait(t)
        t = act.done(act.e.activation(pos[:, :], pos[:, :], ACT.Sin))
        dve.wait(t)
        t = chain(dve.e.tensor_tensor(xp[:, :], core.XNT[:, :], pos[:, :], ALU.add))
        pe.wait(t)
        read = [None] * 2
        for b in range(4):
            ps = psum.bank(b % 2)
            pe.wait(read[b % 2])
            for j in range(4):
                m = pe.e.transpose(ps[:, j * P:(j + 1) * P], xp[:, (4 * b + j) * P:(4 * b + j + 1) * P], core.ident[:, :])
            m = pe.done(m)
            act.wait(m)
            read[b % 2] = act.done(act.e.activation(xpt[:, 4 * b:4 * b + 4, :], ps.rearrange("p (q d) -> p q d", q=4), ACT.Copy))
        core.barrier()
    with ExitStack() as own:
        core.ctx = own
        NarrowAttention(core, psum, io, factor, xp).run()
        core.ctx = ctx
    with ExitStack() as own:
        core.ctx = own
        rows = own.enter_context(nc.sbuf_tensor("A2_rows", [P, 3, D], F32))
        for i, n in enumerate(("bo", "ln_gamma", "ln_beta")):
            core.load(rows[:, i, :], io["L2_attn_" + n].partition_broadcast(P))
        dve.wait(core.loads.all())
        chain(dve.e.tensor_scalar(rows[:, 1, :], rows[:, 1, :], f[:, 4:5], None, ALU.mult))
        A = core.SACC
        over = lambda i: rows[:, i:i + 1, :].to_broadcast([P, NT, D])
        chain(dve.e.scalar_tensor_tensor(xpt[:, :, :], A[:, :, :], f[:, 2:3], xpt[:, :, :], ALU.mult, ALU.add))
        t = chain(dve.e.tensor_tensor(xpt[:, :, :], xpt[:, :, :], over(0), ALU.add))
        n = Norm(core, "A2n")
        made = n.run(lambda i: xpt[:, i, :], lambda i: A[:, i, :], eps=f[:, 3:4])
        dve.wait(made[-1])
        chain(dve.e.tensor_tensor(A[:, :, :], A[:, :, :], over(1), ALU.mult))
        chain(dve.e.tensor_tensor(A[:, :, :], A[:, :, :], over(2), ALU.add))
        core.ctx = ctx


def attention3(core, psum, io):
    nc, ctx = core.nc, core.ctx
    pe, act, dve, pool = core.pe, core.act, core.dve, core.pool
    sb = lambda n, s, d=F32: ctx.enter_context(nc.sbuf_tensor("A3_" + n, s, d))
    gains = sb("gains", [P, 8])
    with nc.allow_non_contiguous_dma("columns of 128"):
        for i, n in enumerate(("lnk_s", "lnk_b", "lnq_s", "lnq_b", "lnv_s", "lnv_b", "lnm_s", "lnm_b")):
            core.load(gains[:, i:i + 1], io["L3_attn_" + n].rearrange("(p a) -> p a", a=1))
    core.lastq = ctx.enter_context(nc.sbuf_tensor("lastq", [P, 2, P], BF16))
    core.lastk = ctx.enter_context(nc.sbuf_tensor("lastk", [P, 2, P], BF16))
    core.load(core.lastq[:, :, :], io["last_q"].bitcast(BF16))
    core.load(core.lastk[:, :, :], io["last_k"].bitcast(BF16))
    with ExitStack() as own:
        core.ctx = own
        srcs = [core.XNT] + [own.enter_context(nc.sbuf_tensor(f"A3_src{i}", [P, T], F32)) for i in range(2)]
        with ExitStack() as inner:
            core.ctx = inner
            z = inner.enter_context(nc.sbuf_tensor("A3_z", [P, NT, D], F32))
            n = Norm(core, "A3n")
            made = n.run(lambda i: core.XN[:, i, :], lambda i: z[:, i, :])
            act.wait(core.loads.all())
            to_features(core, psum, z, srcs[0], made)
            core.barrier()
            for i in (2, 1, 0):
                act.done(act.e.activation(srcs[i][:, :], srcs[0][:, :], ACT.Identity, scale=gains[:, 2 * i:2 * i + 1], bias=gains[:, 2 * i + 1:2 * i + 2]))
            core.barrier()
        core.ctx = own
        NormedAttention(core, psum, io, srcs).run()
        core.ctx = ctx
    with ExitStack() as own:
        core.ctx = own
        st = lambda n, s, d=F32: own.enter_context(nc.sbuf_tensor("A3m_" + n, s, d))
        rows = st("rows", [P, 2, D])
        core.load(rows[:, 0, :], io["L3_attn_bo"].partition_broadcast(P))
        core.load(rows[:, 1, :], io["L3_attn_b2"].partition_broadcast(P))
        W1, W2, b1 = st("W1", [P, 256]), st("W2", [P, 2, P]), st("b1", [P, 2])
        core.load(W1[:, :], io["L3_attn_W1"])
        core.load(W2[:, :, :], io["L3_attn_W2"].rearrange("(j p) d -> p j d", p=P))
        with nc.allow_non_contiguous_dma("256 biases"):
            core.load(b1[:, :], io["L3_attn_b1"].rearrange("(j p) -> p j", p=P))
        z, yT, u = st("z", [P, NT, D]), st("yT", [P, T]), st("u", [P, 2, 2, BANK])
        H = core.SACC
        over = lambda i, n=NT: rows[:, i:i + 1, :].to_broadcast([P, n, D])
        dve.wait(core.loads.all())
        t = dve.done(dve.e.tensor_tensor(H[:, :, :], H[:, :, :], core.XN[:, :, :], ALU.add))
        dve.wait(t)
        t = dve.done(dve.e.tensor_tensor(H[:, :, :], H[:, :, :], over(0), ALU.add))
        n = Norm(core, "A3o")
        made = n.run(lambda i: H[:, i, :], lambda i: z[:, i, :], ready=(t,))
        to_features(core, psum, z, yT, made, scale=gains[:, 6:7], bias=gains[:, 7:8])
        dve.wait(made[-1])
        t = dve.done(dve.e.tensor_tensor(H[:, :, :], H[:, :, :], over(1), ALU.add))
        dve.wait(t)
        pe.wait((act.sem, act.count), core.loads.all())
        act.wait(core.loads.all())
        read = [None] * 8
        uread = [None] * 2
        for c in range(4):
            s = slice(c * BANK, (c + 1) * BANK)
            for j in range(2):
                b0 = 2 + (2 * c + j) % 4
                pe.wait(read[b0])
                made = pe.done(pe.e.matmul(psum.bank(b0), W1[:, j * P:(j + 1) * P], yT[:, s], start=True, stop=True))
                act.wait(made, uread[c % 2])
                last = read[b0] = act.done(act.e.activation(u[:, c % 2, j, :], psum.bank(b0), ACT.Gelu_apprx_tanh, bias=b1[:, j:j + 1]))
            b0 = 6 + c % 2
            y = psum.bank(b0)
            pe.wait(last, read[b0])
            for q in range(4):
                for j in range(2):
                    mm = pe.e.matmul(y[:, q * P:(q + 1) * P], u[:, c % 2, j, q * P:(q + 1) * P], W2[:, j, :], start=j == 0, stop=j == 1)
            uread[c % 2] = made = pe.done(mm)
            dve.wait(made)
            read[b0] = dve.done(dve.e.tensor_tensor(H[:, 4 * c:4 * c + 4, :], H[:, 4 * c:4 * c + 4, :], y.rearrange("p (q d) -> p q d", q=4), ALU.add))
        core.barrier()
        core.ctx = ctx


def rms_rows(core, src, dst, sq, ss, gain, n, ready=()):
    act, dve = core.act, core.dve
    dve.wait(*ready)
    t = dve.done(dve.e.tensor_tensor(sq[:, 0:n, :], src, src, ALU.mult))
    dve.wait(t)
    t = dve.done(dve.e.tensor_reduce(ss[:, 0, 0:n], sq[:, 0:n, :], AX.X, ALU.add))
    act.wait(t)
    r = act.done(act.e.activation(ss[:, 1, 0:n], ss[:, 0, 0:n], ACT.Sqrt))
    dve.wait(r)
    t = dve.done(dve.e.tensor_scalar(ss[:, 1, 0:n], ss[:, 1, 0:n], 1e-12, None, ALU.max))
    dve.wait(t)
    t = dve.done(dve.e.reciprocal(ss[:, 2, 0:n], ss[:, 1, 0:n]))
    dve.wait(t)
    t = dve.done(dve.e.tensor_tensor(ss[:, 2, 0:n], ss[:, 2, 0:n], ss[:, 0, 0:n], ALU.mult))
    dve.wait(t)
    t = dve.done(dve.e.tensor_tensor(ss[:, 1, 0:n], ss[:, 1, 0:n], ss[:, 2, 0:n], ALU.add))
    dve.wait(t)
    t = dve.done(dve.e.tensor_scalar(ss[:, 1, 0:n], ss[:, 1, 0:n], 0.5, 1e-12, ALU.mult, ALU.max))
    dve.wait(t)
    t = dve.done(dve.e.reciprocal(ss[:, 0, 0:n], ss[:, 1, 0:n]))
    dve.wait(t)
    t = dve.done(dve.e.tensor_scalar(ss[:, 0, 0:n], ss[:, 0, 0:n], float(np.sqrt(np.float32(D))), None, ALU.mult))
    dve.wait(t)
    for i in range(n):
        t = dve.done(dve.e.scalar_tensor_tensor(dst[:, i, :], src[:, i, :], ss[:, 0, i:i + 1], gain, ALU.mult, ALU.mult))
    return t


def soft_moe(core, psum, io):
    nc = core.nc
    pe, act, dve, pool = core.pe, core.act, core.dve, core.pool
    NS = 4
    with ExitStack() as ctx:
        sb = lambda n, s, d=F32: ctx.enter_context(nc.sbuf_tensor("F3_" + n, s, d))
        xr = sb("xr", [P, NT, 129])
        xrT = sb("xrT", [P, T])
        se = sb("se", [P, NS, D])
        seT = sb("seT", [P, BANK])
        gain = sb("gain", [P, 2, D])
        sq = sb("sq", [P, NT, D])
        ss = sb("ss", [P, 3, NT])
        w1, w2 = sb("w1", [P, BANK]), sb("w2", [P, NS, D])
        tokmax = sb("tokmax", [P, NT])
        slotpart = sb("slotpart", [P, NS, 4])
        slotmax = sb("slotmax", [P, NS])
        rows = sb("rows", [1, T + BANK])
        E = [sb(f"E{i}", [P, BANK]) for i in range(2)]
        rden = sb("rden", [P, NT])
        slots = sb("slots", [P, NS, D])
        slotsT = sb("slotsT", [P, BANK])
        hid = sb("hid", [P, NS, BANK])
        proc = sb("proc", [P, NS, 129])
        Ct = [sb(f"C{i}", [P, NS, BANK]) for i in range(2)]
        core.load(se[:, :, :], io["L3_ffn_slot_embeds"].rearrange("(a e) t d -> (e t) a d", a=NS))
        core.load(gain[:, 0, :], io["L3_ffn_gamma_x"].partition_broadcast(P))
        core.load(gain[:, 1, :], io["L3_ffn_gamma_slot"].partition_broadcast(P))
        core.load(w1[:, :], io["L3_ffn_w1"])
        core.load(w2[:, :, :], io["L3_ffn_w2"].rearrange("(j p) d -> p j d", p=P))
        pool.done(pool.e.memset(xr[:, :, 128:129], 1.0))
        pool.done(pool.e.memset(proc[:, :, 128:129], 1.0))
        a = rms_rows(core, core.XN[:, :, :], xr[:, :, 0:128], sq, ss, gain[:, 0, :], NT, ready=(core.loads.all(),))
        dve.wait(a)
        b = rms_rows(core, se[:, :, :], se, sq, ss, gain[:, 1, :], NS)
        core.barrier()
        for i in range(5):
            src = (lambda j: xr[:, 4 * i + j, 0:128]) if i < 4 else (lambda j: se[:, j, :])
            for j in range(4):
                m = pe.e.transpose(psum.bank(i)[:, j * P:(j + 1) * P], src(j), core.ident[:, :])
            m = pe.done(m)
            act.wait(m)
            act.done(act.e.activation(xrT[:, i * BANK:(i + 1) * BANK] if i < 4 else seT[:, :], psum.bank(i), ACT.Copy))
        core.barrier()
        read = [None] * 8
        for i in range(NT):
            b0 = i % 4
            pe.wait(read[b0])
            m = pe.done(pe.e.matmul(psum.bank(b0), xrT[:, i * P:(i + 1) * P], seT[:, :], start=True, stop=True))
            dve.wait(m)
            t = read[b0] = dve.done(dve.e.tensor_reduce(tokmax[:, i:i + 1], psum.bank(b0), AX.X, ALU.max, negate=True))
        for i in range(NS):
            for j in range(4):
                b0 = (4 * i + j) % 4
                pe.wait(read[b0])
                m = pe.done(pe.e.matmul(psum.bank(b0), seT[:, i * P:(i + 1) * P], xrT[:, j * BANK:(j + 1) * BANK], start=True, stop=True))
                dve.wait(m)
                t = read[b0] = dve.done(dve.e.tensor_reduce(slotpart[:, i, j:j + 1], psum.bank(b0), AX.X, ALU.max))
        dve.wait(t)
        t = dve.done(dve.e.tensor_reduce(slotmax[:, :], slotpart[:, :, :], AX.X, ALU.max, negate=True))
        pe.wait(t)
        for i in range(NT + NS):
            src = tokmax[:, i:i + 1] if i < NT else slotmax[:, i - NT:i - NT + 1]
            m = pe.e.matmul(psum.all[0:1, i * P:(i + 1) * P], src, core.ident[:, :], start=True, stop=True)
        m = pe.done(m)
        act.wait(m)
        act.done(act.e.activation(rows[:, :], psum.all[0:1, 0:T + BANK], ACT.Copy))
        core.barrier()
        read = [None] * 8
        eread = [None] * 2
        for i in range(NT):
            b0 = 4 + i % 2
            pe.wait(read[b0])
            pe.e.matmul(psum.bank(b0), xrT[:, i * P:(i + 1) * P], seT[:, :], start=True, stop=False)
            m = pe.done(pe.e.matmul(psum.bank(b0), core.onerow[:, 0:P], rows[:, T:T + BANK], start=False, stop=True))
            act.wait(m, eread[i % 2])
            t = read[b0] = act.done(act.e.activation(E[i % 2][:, :], psum.bank(b0), ACT.Exp))
            pe.wait(t)
            for j in range(NS):
                m = pe.e.matmul(psum.bank(j)[:, 0:129], E[i % 2][:, j * P:(j + 1) * P], xr[:, i, :], start=i == 0, stop=i == NT - 1)
            eread[i % 2] = pe.done(m)
        dve.wait(eread[1])
        for j in range(NS):
            t = dve.done(dve.e.reciprocal(rden[:, j:j + 1], psum.bank(j)[:, 128:129]))
            dve.wait(t)
            t = dve.done(dve.e.tensor_scalar(slots[:, j, :], psum.bank(j)[:, 0:128], rden[:, j:j + 1], None, ALU.mult))
        pe.wait(t)
        for j in range(NS):
            m = pe.e.transpose(psum.bank(0)[:, j * P:(j + 1) * P], slots[:, j, :], core.ident[:, :])
        m = pe.done(m)
        act.wait(m)
        t = act.done(act.e.activation(slotsT[:, :], psum.bank(0), ACT.Copy))
        pe.wait(t)
        for j in range(NS):
            m = pe.done(pe.e.matmul(psum.bank(1 + j), w1[:, j * P:(j + 1) * P], slotsT[:, :], start=True, stop=True))
            act.wait(m)
            t = act.done(act.e.activation(hid[:, j, :], psum.bank(1 + j), ACT.Gelu))
        pe.wait(t)
        for q in range(NS):
            for j in range(NS):
                m = pe.e.matmul(psum.bank(5)[:, q * P:(q + 1) * P], hid[:, j, q * P:(q + 1) * P], w2[:, j, :], start=j == 0, stop=j == NS - 1)
        m = pe.done(m)
        act.wait(m)
        act.done(act.e.activation(proc[:, :, 0:128], psum.bank(5).rearrange("p (q d) -> p q d", q=NS), ACT.Copy))
        core.barrier()
        read = [None] * 8
        cread = [None] * 2
        n = 0
        for c in range(4):
            s = slice(c * BANK, (c + 1) * BANK)
            for j in range(NS):
                b0 = n % 4
                n += 1
                pe.wait(read[b0])
                pe.e.matmul(psum.bank(b0), seT[:, j * P:(j + 1) * P], xrT[:, s], start=True, stop=False)
                m = pe.done(pe.e.matmul(psum.bank(b0), core.onerow[:, 0:P], rows[:, s], start=False, stop=True))
                act.wait(m, cread[c % 2])
                t = read[b0] = act.done(act.e.activation(Ct[c % 2][:, j, :], psum.bank(b0), ACT.Exp))
            pe.wait(t)
            for q in range(4):
                b0 = 4 + q
                y = psum.bank(b0)
                pe.wait(read[b0])
                for j in range(NS):
                    m = pe.e.matmul(y[:, 0:129], Ct[c % 2][:, j, q * P:(q + 1) * P], proc[:, j, :], start=j == 0, stop=j == NS - 1)
                cread[c % 2] = m = pe.done(m)
                i = 4 * c + q
                dve.wait(m)
                r = dve.done(dve.e.reciprocal(rden[:, i:i + 1], y[:, 128:129]))
                dve.wait(r)
                read[b0] = dve.done(dve.e.tensor_scalar(core.GATE[:, i, :], y[:, 0:128], rden[:, i:i + 1], None, ALU.mult))
        act.wait(read[7])
        act.done(act.e.activation(core.GATE[:, :, :], core.GATE[:, :, :], ACT.Silu))
        core.barrier()


def residual(core, ready=()):
    dve, pool = core.dve, core.pool
    dve.wait(*ready)
    for i in range(4):
        s = slice(4 * i, 4 * i + 4)
        m = dve.done(dve.e.tensor_tensor(core.GATE[:, s, :], core.GATE[:, s, :], core.SACC[:, s, :], ALU.mult))
        dve.wait(m)
        t = dve.done(dve.e.tensor_tensor(core.X[:, s, :], core.X[:, s, :], core.GATE[:, s, :], ALU.add))
    return t


def norm_layer(core, psum):
    with ExitStack() as ctx:
        core.ctx, keep = ctx, core.ctx
        n = Norm(core, f"N{core.layer}")
        core.ctx = keep
        made = n.run(lambda i: core.X[:, i, :], lambda i: core.XN[:, i, :])
        to_features(core, psum, core.XN, core.XNT, made)
        core.pool.done(core.pool.e.memset(core.SACC[:, :, :], 0.0))
        core.barrier()


START = 0


def program(nc, io, out, stop=99):
    with ExitStack() as ctx:
        core = Core(nc, ctx)
        psum = Psum(nc, ctx)
        sb = lambda n, s, d=F32: ctx.enter_context(nc.sbuf_tensor(n, s, d))
        core.X = sb("X", [P, NT, D])
        core.XN = sb("XN", [P, NT, D])
        core.XNT = sb("XNT", [P, T])
        core.SACC = sb("SACC", [P, NT, D])
        core.GATE = sb("GATE", [P, NT, D])
        core.ident = sb("ident", [P, P])
        core.identb = sb("identb", [P, P], BF16)
        core.ones = sb("ones", [P, 1])
        core.onerow = sb("onerow", [1, P])
        core.load(core.X[:, :, :], io["L0_attn_x"].rearrange("a (t p) d -> p (a t) d", p=P))
        core.load(core.ident[:, :], io["identity"])
        core.dve.wait(core.loads.all())
        core.dve.done(core.dve.e.tensor_copy(core.identb[:, :], core.ident[:, :]))
        core.dve.done(core.dve.e.memset(core.ones[:, :], 1.0))
        core.dve.done(core.dve.e.memset(core.onerow[:, :], 1.0))
        core.barrier()

        def layer(n, gate, attention):
            core.layer = n
            norm_layer(core, psum)
            gate()
            with ExitStack() as own:
                core.ctx = own
                attention()
                residual(core)
                core.barrier()
            core.ctx = ctx

        def attention0():
            core.maskq = core.ctx.enter_context(nc.sbuf_tensor("maskq", [P, 4, BANK], BF16))
            core.maskk = core.ctx.enter_context(nc.sbuf_tensor("maskk", [P, 4, BANK], BF16))
            core.load(core.maskq[:, :, :], io["mask_q"].bitcast(BF16))
            core.load(core.maskk[:, :, :], io["mask_k"].bitcast(BF16))
            RotaryAttention(core, psum, io).run()

        def attention1():
            LatentAttention(core, psum, io).run()

        if START < 1:
            layer(0, lambda: quantized_ffn(core, psum, io), attention0)
        if stop > 1 and START < 2:
            layer(1, lambda: transformer_gate(core, psum, io), attention1)
        if stop > 2 and START < 3:
            layer(2, lambda: ternary_ffn(core, psum, io), lambda: attention2(core, psum, io))
        if stop > 3:
            layer(3, lambda: soft_moe(core, psum, io), lambda: attention3(core, psum, io))

        core.stores.add(nc.sync.dma_start(out.rearrange("a (t p) d -> p (a t) d", p=P), core.X[:, :, :]))
        core.sp.wait(core.stores.all())


def bf16_bits(a):
    return np.ascontiguousarray((a.astype(np.float32).view(np.uint32) >> 16).astype(np.uint16))


def constants():
    c = {"identity": np.eye(P, dtype=np.float32)}
    inv = (1.0 / 10000.0 ** (np.arange(0, 32, 2, dtype=np.float32) / np.float32(32))).astype(np.float32)
    f = np.arange(T, dtype=np.float32)[:, None] * inv[None, :]
    cos, sin = np.cos(f).T.astype(np.float32), np.sin(f).T.astype(np.float32)
    rest = np.ones((32, T), np.float32)
    c["rope_cos"] = np.concatenate([cos, cos, rest] * 2)
    c["rope_sin"] = np.concatenate([-sin, sin, 0 * rest] * 2)
    p = np.arange(P)[:, None, None]
    j = np.arange(4)[None, :, None]
    x = np.arange(BANK)[None, None, :]
    c["mask_q"] = bf16_bits(np.where(x <= P * j + p, 0.0, NEG))
    c["mask_k"] = bf16_bits(np.where(P * j + p <= x, 0.0, NEG))
    half = np.arange(0, 64, 2, dtype=np.float32)
    inv = (1.0 / 10000.0 ** (half / np.float32(64))).astype(np.float32)
    t = np.arange(T, dtype=np.float32)
    f = t[:, None] * inv[None, :]
    base = ((half + np.float32(25.6)) / np.float32(89.6)).astype(np.float32)
    power = (t - np.float32(T // 2)) / np.float32(32.0)
    scale = np.power(base[None, :], power[:, None]).astype(np.float32)
    scale, cos, sin = (np.concatenate([y, y], 1) for y in (scale, np.cos(f), np.sin(f)))
    sign = np.where(np.arange(64) < 32, -1.0, 1.0).astype(np.float32)
    tabs = np.stack([cos * scale, sin * sign * scale, cos / scale, sin * sign / scale], 1).astype(np.float32)
    c["xpos"] = np.ascontiguousarray(tabs.reshape(NT, P, 4, 64).transpose(1, 0, 2, 3))
    q, k = np.arange(P)[:, None], np.arange(-P, P)[None, :]
    band = np.where((k <= q) & (q <= k + 64), 0.0, NEG)
    nokeys = np.where(k < 0, NEG, band)
    c["band_mask"] = bf16_bits(np.stack([nokeys, band]))
    c["first_masks"] = bf16_bits(np.stack([nokeys, band, band, band]))
    moves = np.zeros((P, 2, P), np.float32)
    moves[np.arange(P - 1), 0, np.arange(1, P)] = 1.0
    moves[P - 1, 1, 0] = 1.0
    c["row_moves"] = moves
    even = (np.arange(D) // 2 * 2).astype(np.float32)
    c["position_denominators"] = np.stack([np.power(np.float32(10000.0), np.float32(2.0) * even / np.float32(D)), 0.25 * (np.arange(D) % 2)], 1).astype(np.float32)
    last = np.zeros((P, 2, P), np.float32)
    last[0, :, P - 1] = (-992.0, -7.0)
    c["last_q"] = bf16_bits(last)
    c["last_k"] = bf16_bits(last.transpose(2, 1, 0))
    return c


TURN = ["L0_ffn_w_gate", "L0_ffn_w_up", "L0_ffn_w_down", "L1_attn_Wq", "L1_attn_Wkv_down", "L1_attn_Wk_up",
        "L1_attn_Wv_up", "L1_attn_Wo", "L2_attn_Wq", "L2_attn_Wk", "L2_attn_Wv", "L2_attn_Wo",
        "L2_ffn_w1_w", "L2_ffn_w2_w", "L2_ffn_h1_w", "L2_ffn_h2_w", "L2_ffn_w3_w"]


def kernel(**inputs):
    import concourse.bacc as bacc
    from concourse.bass_utils import run_bass_kernel_spmd

    arrays = {}
    for name, a in inputs.items():
        a = np.asarray(a)
        arrays[name] = np.ascontiguousarray(a.T if name in TURN else a)
    arrays.update(constants())
    nc = bacc.Bacc("TRN2", target_bir_lowering=False, num_devices=1)
    io = {n: nc.dram_tensor(n, a.shape, mybir.dt.from_np(a.dtype), kind="ExternalInput").ap() for n, a in arrays.items()}
    out = nc.dram_tensor("out", (1, T, D), F32, kind="ExternalOutput").ap()
    program(nc, io, out)
    r = run_bass_kernel_spmd(nc, [arrays], core_ids=[0])
    return r.results[0]["out"]
```

```python
from contextlib import ExitStack

import numpy as np

import concourse.bass as bass
from concourse import mybir

F32 = mybir.dt.float32
F32R = mybir.dt.float32r
BF16 = mybir.dt.bfloat16
I32 = mybir.dt.int32
ACT = mybir.ActivationFunctionType
ALU = mybir.AluOpType
AX = mybir.AxisListType

P = 128
T = 2048
NT = T // P
D = 128
BANK = 512
KC = 512
NEG = -1.0e30


class Queue:

    def __init__(self, nc, engine, name):
        self.e = engine
        self.sem = nc.alloc_semaphore("done_" + name)
        self.count = 0
        self.seen = {}

    def done(self, ins):
        ins.then_inc(self.sem, 1)
        self.count += 1
        return (self.sem, self.count)

    def wait(self, *tickets):
        for t in tickets:
            if t is not None and self.seen.get(t[0].num, 0) < t[1]:
                self.e.wait_ge(t[0], t[1])
                self.seen[t[0].num] = t[1]


class Loads:

    def __init__(self, nc, name):
        self.sem = nc.alloc_semaphore("loaded_" + name)
        self.count = 0

    def add(self, ins):
        ins.then_inc(self.sem, 16)
        self.count += 16

    def all(self):
        return (self.sem, self.count)


class Core:

    def __init__(self, nc, ctx):
        self.nc = nc
        self.ctx = ctx
        self.pe = Queue(nc, nc.tensor, "pe")
        self.act = Queue(nc, nc.scalar, "act")
        self.dve = Queue(nc, nc.vector, "dve")
        self.pool = Queue(nc, nc.gpsimd, "pool")
        self.sp = Queue(nc, nc.sync, "sp")
        self.loads = Loads(nc, "all")
        self.stores = Loads(nc, "out")
        self.queues = [self.pe, self.act, self.dve, self.pool, self.sp]
        self.sides = [Loads(nc, f"side{d}") for d in range(2)]
        self.transfers = [self.loads, self.stores] + self.sides
        self.counts = [q.sem for q in self.queues + self.transfers]

    def barrier(self):
        for l in self.transfers:
            if l.count:
                self.sp.wait(l.all())
        nums = [s.num for s in self.counts]
        assert nums == list(range(nums[0], nums[0] + len(nums)))
        self.nc.all_engine_barrier(sems_to_clear=range(nums[0], nums[0] + len(nums)))
        for q in self.queues:
            q.count = 0
            q.seen = {}
        for l in self.transfers:
            l.count = 0

    def load(self, out, in_, queue=None):
        q = queue or self.sp
        self.loads.add(q.e.dma_start(out, in_))


def free(ap):
    return ap.bitcast(F32)


class Attention:

    def __init__(self, core, psum, name, heads, hd, causal=False, last_key_mask=False, scale=1.0):
        self.c = core
        self.name = name
        self.hd = hd
        self.scale = scale
        self.wide = hd == 64
        self.packed = hd == 8
        self.G = 4 if self.packed else 2
        self.M = P // self.G
        self.groups = heads // self.G
        self.QC = 1024 // self.G
        self.nchunk = T // self.QC
        self.qt = self.QC // P
        self.causal = causal
        self.last_key_mask = last_key_mask
        self.own = [slice(0, 64), slice(64, P)]
        self.far = [slice(64, P), slice(0, 64)]
        self.row = [64, 0] if self.wide else [0, 32, 64, 96] if self.packed else [96] * self.G
        self.rows = 96 if hd == 32 else P
        self.psum = psum
        self.vbias = [None, None]
        ctx, nc = core.ctx, core.nc
        sb = lambda n, s, d=F32: ctx.enter_context(nc.sbuf_tensor(name + "_" + n, s, d))
        G = self.G
        self.Ka = [[sb(f"Ka{d}{h}", [P, T], F32R) for h in range(1 if self.packed else G)] for d in range(2)]
        if self.packed:
            self.Ka = [side * G for side in self.Ka]
        self.Kb = [[sb(f"Kb{d}{h}", [P, T], F32R) for h in range(G)] for d in range(2)] if self.wide else self.Ka
        self.Qa = [sb(f"Qa{h}", [P, 2 * BANK], F32R) for h in range(G)]
        self.Qb = [sb(f"Qb{h}", [P, 2 * BANK], F32R) for h in range(G)] if self.wide else self.Qa
        self.V = [sb(f"V{d}", [P, NT, G, self.M]) for d in range(2)]
        self.W = [sb(f"weights{i}", [P, 1024]) for i in range(4)]
        self.wsum = [sb(f"wsum{i}", [P, 1024]) for i in range(2)] if self.wide else None
        self.Wo = [sb(f"Wo{d}", [P, G // 2, 258]) for d in range(2)]
        self.OT = [sb(f"OT{i}", [P, self.QC]) for i in range(2)]
        self.stage = [sb(f"stage{i}", [P, BANK]) for i in range(2)]
        self.part = [sb(f"part{i}", [P, G, self.qt, T // KC]) for i in range(2)]
        self.negmax = [sb(f"negmax{i}", [P, G, self.qt]) for i in range(2)]
        self.rden = [sb(f"rden{i}", [P, 2]) for i in range(2)]
        self.products = range(self.G) if hd == 32 else [0]
        self.lag = 1 if hd == 32 else 2
        self.arrived = core.sides
        self.scaled = None if self.wide else [sb(f"scaled{i}", [P, 2, D]) for i in range(2)]

    def once(self):
        c = self.c
        dve, pool = c.dve, c.pool
        w = [pool.done(pool.e.memset(self.Wo[d][:, :, :], 0.0)) for d in range(2)][-1]
        c.sp.wait(w)
        self.fetch(0, 0)
        zero, one = self.stage
        z = dve.done(dve.e.memset(zero[:, :], 0.0))
        z1 = dve.done(dve.e.memset(one[:, :], 1.0))
        for q, tensors in ((dve, [self.Kb[0], self.Qb]), (c.act, [self.Kb[1]])):
            q.wait(z, z1)
            if self.packed:
                for t in self.Qb[0:2] if q is dve else self.Qb[2:4]:
                    for b in range(2):
                        new = t[:, b * BANK:(b + 1) * BANK]
                        if q is dve:
                            dve.done(dve.e.tensor_copy(new, zero[:, :]))
                        else:
                            c.act.done(c.act.e.activation(new, zero[:, :], ACT.Copy))
                continue
            for src in (zero, one):
                for heads in tensors:
                    if heads is self.Qb and src is one:
                        continue
                    for h, t in enumerate(heads):
                        lo = self.row[h]
                        rows = slice(lo, lo + 1) if src is one else self.far[h] if self.wide else slice(lo, P)
                        for b in range(t.shape[1] // BANK):
                            new, old = t[rows, b * BANK:(b + 1) * BANK], src[rows, :]
                            if q is dve:
                                f = dve.done(dve.e.tensor_copy(new, old))
                            else:
                                f = c.act.done(c.act.e.activation(new, old, ACT.Copy))
                q.wait(f)
        for d in range(2):
            v = pool.done(pool.e.memset(self.V[d][:, :, :, :], 0.0))
            if not self.wide:
                pool.wait(v)
                pool.done(pool.e.memset(self.V[d][:, :, :, self.hd:self.hd + 1], 1.0))
                dve.wait(w)
                for h in range(self.G):
                    r = h * self.M + self.hd
                    dve.done(dve.e.tensor_copy(self.Wo[d][:, h // 2, 129 * (h % 2) + 128:129 * (h % 2) + 129], c.ident[:, r:r + 1]))
        c.barrier()

    def begin(self, banks, maxbanks):
        self.maxbanks = maxbanks
        self.qplace = {(0, 0): 0}
        self.banks = banks
        self.bankread = [()] * len(banks)
        self.bank = -1
        self.staged = [(), ()]
        self.k = 0
        self.mxread = [None] * len(maxbanks)
        self.mxn = 0
        self.qfree = {}
        self.kmade = {}
        self.qmade = {}
        self.vmade = {}
        self.s = 0
        self.chunks = 0
        self.exped, self.used, self.summed = {}, {}, {}
        self.otcopied, self.otread = {}, {}
        self.accw = {}
        self.turned_read = None
        self.un = 0
        self.rread = [None, None]
        self.units = []
        self.kused = None
        self.vread = {}

    def take(self):
        self.bank = (self.bank + 1) % len(self.banks)
        self.Y = self.banks[self.bank]
        self.c.pe.wait(*self.bankread[self.bank])

    def release(self, *readers):
        self.bankread[self.bank] = readers

    def fetch(self, side, g):
        c = self.c
        c.sp.wait((c.pe.sem, c.pe.count), (c.dve.sem, c.dve.count), (c.act.sem, c.act.count))
        self.load(side, g)

    def fetched(self, side):
        self.c.pe.wait(self.arrived[side].all())
        self.prepare(side)

    def prepare(self, side):
        pass

    def place(self, side, which, b):
        if which == 0:
            return slice(b * BANK, (b + 1) * BANK), self.kfree
        place = self.qplace[side, b]
        return slice(place * BANK, place * BANK + BANK), self.qfree.get(place)

    def split(self, side, h, which, b, staged, i):
        c = self.c
        dve, pool = c.dve, c.pool
        st = self.stage[i]
        R = self.rows
        s, before = self.place(side, which, b)
        X = self.Qa[h] if which else self.Ka[side][h]
        dve.wait(staged, before)
        hi = dve.done(dve.e.tensor_copy(X[0:R, s], st[0:R, :]))
        q = slice(64, 96) if which else slice(32, 64)
        pool.wait(hi, staged, (pool.sem, pool.count))
        last = pool.done(pool.e.tensor_tensor(X[q, s], st[q, :], free(X[q, s]), ALU.subtract))
        self.staged[i] = (last,)
        if which:
            self.qmade[self.qplace[side, b], h] = (last,)
        else:
            self.kmade[side, b] = (last,)

    def split_pair(self, side, which, b, staged, i):
        act, dve = self.c.act, self.c.dve
        st = self.stage[i]
        s, before = self.place(side, which, b)
        Xa = self.Qa if which else self.Ka[side]
        Xb = self.Qb if which else self.Kb[side]
        dve.wait(staged, before)
        act.wait(staged, before)
        for h in range(2):
            own, far = self.own[h], self.far[h]
            hi = dve.done(dve.e.tensor_copy(Xa[h][own, s], st[own, :]))
            again = Xa[h][far, s] if which else Xb[h][own, s]
            high = act.done(act.e.activation(again, st[own, :], ACT.Copy))

        def lows():
            for h in range(2):
                own, far = self.own[h], self.far[h]
                dve.wait(hi)
                low = Xb[h][own, s] if which else Xa[h][far, s]
                last = dve.done(dve.e.tensor_tensor(low, st[own, :], free(Xa[h][own, s]), ALU.subtract))
                if which:
                    self.qmade[self.qplace[side, b], h] = (last, high)
            self.staged[i] = (last, high)
            if which == 0:
                self.kmade[side, b] = (last, high)

        return lows

    def product(self, side, h, which, b, part):
        c = self.c
        w, src, K = self.proj(side, h, which)[part]
        self.take()
        s = slice(b * BANK, (b + 1) * BANK)
        return c.pe.done(c.pe.e.matmul(self.Y[0:self.rows, :], w[0:K, 0:self.rows], src[0:K, s], start=True, stop=True))

    def project(self, side, h, which, b):
        c = self.c

        lows = []

        def plain():
            made = self.product(side, h, which, b, 0)
            scale, bias = self.affine(side, h, which)
            i = self.k % 2
            self.k += 1
            st = self.stage[i]
            c.act.wait(made, *self.staged[i])
            got = c.act.done(c.act.e.activation(st[0:self.rows, :], self.Y[0:self.rows, :], ACT.Identity, scale=scale, bias=bias))
            self.release(got)
            if self.wide:
                lows.append(self.split_pair(side, which, b, got, i))
            else:
                self.split(side, h, which, b, got, i)

        return [plain, lambda: lows.pop()()] if self.wide else [plain]

    def vunit(self, side, b):
        c = self.c
        pe, act, dve = c.pe, c.act, c.dve
        hd, G = self.hd, self.G
        src, K = self.vsrc()
        self.take()
        for j in range(4):
            kt = 4 * b + j
            o = self.Y[:, j * P:j * P + G * hd]
            mm = pe.e.matmul(o, src[0:K, kt * P:(kt + 1) * P], self.Wv[side][0:K, 0:G * hd], start=True, stop=True)
        made = pe.done(mm)
        view = self.Y.rearrange("p (t x) -> p t x", t=4)[:, :, 0:G * hd].rearrange("p t (h d) -> p t h d", h=G)
        V = self.V[side][:, 4 * b:4 * b + 4, :, 0:hd]
        if self.vbias[side] is None:
            act.wait(made, self.vread.get(side))
            t = act.done(act.e.activation(V, view, ACT.Copy))
        else:
            dve.wait(made, self.vread.get(side))
            for h in range(G):
                bias = self.vbias[side][:, h:h + 1, :].to_broadcast([P, 4, hd])
                t = dve.done(dve.e.tensor_tensor(V[:, :, h, :], view[:, :, h, :], bias, ALU.add))
        self.release(t)
        self.vmade[side] = t

    def pieces(self, ch):
        out = []
        for h in range(self.G):
            for j in range(self.qt):
                n = (ch * self.qt + j) // 4 + 1 if self.causal else T // KC
                out += [(h, j, p, n) for p in range(n)]
        return out

    def half(self, side, ch):
        return self.qplace[side, ch * self.QC // BANK]

    def columns(self, side, ch, j=0):
        return self.half(side, ch) * BANK + ch * self.QC % BANK + j * P

    def piece(self, side, ch, slot, h, j, p, n):
        c = self.c
        tile = ch * self.qt + j
        i = self.mxn % len(self.maxbanks)
        self.mxn += 1
        ps = self.maxbanks[i]
        q = slice(self.columns(side, ch, j), self.columns(side, ch, j) + P)
        extra = []
        if self.causal and p == tile // 4:
            extra = [(c.maskq[:, tile % 4, :], slice(0, KC))]
        if self.last_key_mask and tile == 0 and p == T // KC - 1:
            extra = [(c.lastq[:, x, :], slice(KC - P, KC)) for x in range(2)]
        c.pe.wait(self.mxread[i], *self.kmade.get((side, p), ()), *self.qmade.get((self.half(side, ch), h), ()))
        K = self.rows
        mm = c.pe.e.matmul(ps, self.Qa[h][0:K, q], self.Ka[side][h][0:K, p * KC:(p + 1) * KC], start=True, stop=not extra)
        for x, (b, w) in enumerate(extra):
            mm = c.pe.e.matmul(ps[:, w], c.identb[:, :], b, start=False, stop=x == len(extra) - 1)
        made = c.pe.done(mm)
        c.dve.wait(made)
        self.mxread[i] = c.dve.done(c.dve.e.tensor_reduce(self.part[slot][:, h, j, p:p + 1], ps, AX.X, ALU.max))

    def maxima(self, ch, slot):
        n = (ch * self.qt) // 4 + 1 if self.causal else T // KC
        dve = self.c.dve
        dve.wait(*self.mxread)
        self.maxed = dve.done(dve.e.tensor_reduce(self.negmax[slot][:, :, :], self.part[slot][:, :, :, 0:n], AX.X, ALU.max, negate=True))

    def shift(self, side, ch, slot):
        c = self.c
        MX, QC = self.psum.MX, self.QC
        c.pe.wait(self.maxed, *self.mxread)
        for h in range(self.G):
            for j in range(self.qt):
                o, r = (h * self.qt + j) * P, self.row[h]
                mm = c.pe.e.matmul(MX[r:r + 1, o:o + P], self.negmax[slot][:, h, j:j + 1], c.ident[:, :], start=True, stop=True)
        made = c.pe.done(mm)
        block = self.half(side, ch)
        a = self.columns(side, ch)
        for q in (c.act, c.dve):
            q.wait(made, self.qfree.get(block), *(t for h in range(self.G) for t in self.qmade.get((block, h), ())))
        for h in range(self.G):
            r = self.row[h]
            row, new = self.Qb[h][r:r + 1, a:a + QC], MX[r:r + 1, h * QC:(h + 1) * QC]
            if h < self.G // 2:
                first = c.act.done(c.act.e.activation(row, new, ACT.Copy))
            else:
                second = c.dve.done(c.dve.e.tensor_copy(row, new))
        self.mxread = [first, second]
        self.shifted = (first, second)

    def scores(self, side, ch, kt, s, between=()):
        c = self.c
        G, QC = self.G, self.QC
        buf = self.psum.S[:, (s % 2) * 1024:(s % 2) * 1024 + 1024]
        between = list(between)
        c.pe.wait(self.exped.get(s - 2), *(self.shifted if kt == 0 else ()), *self.kmade.get((side, kt // 4), ()))
        kk = slice(kt * P, (kt + 1) * P)
        a = self.columns(side, ch)
        qq = slice(a, a + QC)
        for h in range(G):
            o = buf[:, h * QC:(h + 1) * QC]
            extra = []
            if self.causal and kt >= ch * self.qt:
                extra = [(c.maskk[:, kt - ch * self.qt, :], slice(0, QC))]
            if self.last_key_mask and ch == 0 and kt == NT - 1:
                extra = [(c.lastk[:, x, :], slice(0, P)) for x in range(2)]
            mm = c.pe.e.matmul(o, self.Ka[side][h][:, kk], self.Qa[h][:, qq], start=True, stop=not (self.wide or extra))
            if self.wide:
                mm = c.pe.e.matmul(o, self.Kb[side][h][:, kk], self.Qb[h][:, qq], start=False, stop=not extra)
            for x, (b, w) in enumerate(extra):
                mm = c.pe.e.matmul(o[:, w], c.identb[:, :], b, start=False, stop=x == len(extra) - 1)
            if h == G - 1:
                made = c.pe.done(mm)
            elif self.wide and between:
                between.pop(0)()
        self.qfree[self.half(side, ch)] = made
        self.kused = made
        c.act.wait(made, *self.used.get(s - 4, ()))
        self.exped[s] = c.act.done(c.act.e.activation(self.W[s % 4][:, :], buf, ACT.Exp, scale=self.scale))
        for f in between:
            f()

    def sums(self, s, kt, n):
        pool = self.c.pool
        if not self.wide or kt == 0:
            return ()
        acc = self.wsum[n % 2]
        a = self.W[(s - 1) % 4] if kt == 1 else acc
        pool.wait(self.exped[s], self.summed.get(s - 1), self.otread.get(n - 2))
        self.summed[s] = pool.done(pool.e.tensor_tensor(acc[:, :], a[:, :], self.W[s % 4][:, :], ALU.add))
        if kt == 1:
            self.used[s - 1] += (self.summed[s],)
        return (self.summed[s],)

    def values(self, side, kt, nk, s, n, between=()):
        c = self.c
        G, QC, M = self.G, self.QC, self.M
        O = self.psum.O
        c.pe.wait(self.exped[s])
        if kt == 0:
            c.pe.wait(self.vmade.get(side), self.otcopied.get(n - 1))
        for h in range(G):
            if h == G // 2:
                for f in between:
                    f()
            mm = c.pe.e.matmul(O[h * M:(h + 1) * M, 0:QC], self.V[side][:, kt, h, :], self.W[s % 4][:, h * QC:(h + 1) * QC], start=kt == 0, stop=kt == nk - 1)
        t = self.vread[side] = c.pe.done(mm)
        self.used[s] = (t,)
        self.used[s] += self.sums(s, kt, n)
        if kt == nk - 1:
            c.act.wait(t, self.otread.get(n - 2))
            self.otcopied[n] = c.act.done(c.act.e.activation(self.OT[n % 2][:, :], O[:, 0:QC], ACT.Copy))

    def unit(self, side, ch, n, s, j, half):
        c = self.c
        dve, acc = c.dve, c.SACC
        self.take()
        Y = self.Y
        tile = ch * self.qt + j
        c.pe.wait(self.otcopied[n], self.summed.get(s))
        mm = c.pe.e.matmul(Y[:, 0:258], self.OT[n % 2][:, j * P:(j + 1) * P], self.Wo[side][:, half, :], start=True, stop=True)
        if self.wide:
            for i in range(2):
                mm = c.pe.e.matmul(Y[:, 258 + i:259 + i], self.wsum[n % 2][:, i * self.QC + j * P:i * self.QC + (j + 1) * P], c.ones[:, 0:1], start=True, stop=True)
        made = self.otread[n] = c.pe.done(mm)
        r = self.rden[self.un % 2]
        dve.wait(made, self.rread[self.un % 2])
        t = dve.done(dve.e.reciprocal(r[:, :], Y[:, 258:260] if self.wide else Y[:, 128:258:129]))
        if self.wide:
            dve.wait(t, self.accw.get(tile))
            t = dve.done(dve.e.scalar_tensor_tensor(acc[:, tile, :], Y[:, 0:128], r[:, 0:1], acc[:, tile, :], ALU.mult, ALU.add))
            dve.wait(t)
            t = self.accw[tile] = read = dve.done(dve.e.scalar_tensor_tensor(acc[:, tile, :], Y[:, 129:257], r[:, 1:2], acc[:, tile, :], ALU.mult, ALU.add))
        else:
            two = self.scaled[self.un % 2]
            c.act.wait(t, self.rread[self.un % 2])
            for x in range(2):
                read = c.act.done(c.act.e.activation(two[:, x, :], Y[:, 129 * x:129 * x + 128], ACT.Copy, scale=r[:, x:x + 1]))
            c.pool.wait(read, self.accw.get(tile))
            for x in range(2):
                c.pool.wait((c.pool.sem, c.pool.count))
                t = self.accw[tile] = c.pool.done(c.pool.e.tensor_tensor(acc[:, tile, :], acc[:, tile, :], two[:, x, :], ALU.add))
        self.rread[self.un % 2] = t
        self.release(read)
        self.un += 1

    def qblock(self, side, b):
        return [u for h in self.products for u in self.project(side, h, 1, b)]

    def keys(self, side):
        return [u for b in range(T // BANK) for h in self.products for u in self.project(side, h, 0, b)]

    def preparation(self, side, ch, slot):
        per = BANK // self.QC
        pieces = [[lambda a=a: self.piece(side, ch, slot, *a) for a in self.pieces(ch) if a[0] == h] for h in range(self.G)]
        out, lead, queries = [], [], []
        if ch % per == 0:
            self.qplace[side, ch // per] = slot if self.causal else ch // per % 2
            queries = [self.project(side, h, 1, ch // per) for h in self.products]
            lead = queries.pop(0)
        for h in range(self.G):
            if queries:
                out += queries.pop(0)
            out += pieces[h]
        return lead, out + [lambda: self.maxima(ch, slot)]

    def first(self):
        bank = self.psum.bank
        self.begin([self.psum.Y, bank(0), bank(1)], [bank(4), bank(5), bank(2), bank(3)])
        self.kfree = None
        self.fetched(0)
        for f in self.qblock(0, 0):
            f()
        for b in range(T // BANK + 1):
            if b < T // BANK:
                for h in self.products:
                    for f in self.project(0, h, 0, b):
                        f()
                self.vunit(0, b)
            for a in self.pieces(0):
                if a[2] == b - 1:
                    self.piece(0, 0, 0, *a)
        self.maxima(0, 0)
        self.shift(0, 0, 0)
        self.c.barrier()

    def stretch(self, plan):
        self.begin([self.psum.Y], [self.psum.bank(4), self.psum.bank(5)])
        self.shifted = ()
        G, per = self.G, BANK // self.QC
        for at, (side, nxt) in enumerate(plan):
            other = 1 - side
            orders = [list(range(self.nchunk))] * 2
            if self.causal:
                orders[1] = orders[0][::-1]
            order, following = orders[at % 2], orders[1 - at % 2]
            steps = []
            for ch in order:
                nk = (ch + 1) * self.qt if self.causal else NT
                steps += [(ch, kt, nk) for kt in range(nk)]
            self.kfree = self.kused
            ahead = []
            if nxt is not None:
                ahead = [lambda: self.fetched(other)] + self.keys(other) + [lambda b=b: self.vunit(other, b) for b in range(4)]
            last = len(steps) if self.causal and at % 2 else sum(1 for ch, kt, nk in steps if ch < self.nchunk - per)
            done, begun = 0, None
            if at == 0:
                self.scores(side, 0, 0, self.s)
            for i, (ch, kt, nk) in enumerate(steps):
                s = self.s
                n = self.chunks
                at_end = ch == order[-1]
                nch = following[0] if at_end else order[order.index(ch) + 1]
                nside = other if at_end else side
                more = not at_end or nxt is not None
                if kt == 0:
                    lead, todo = self.preparation(nside, nch, (n + 1) % 2) if more else ([], [])
                    total, due, turn = len(todo), max(2, nk - 2), None
                    rest = min(self.lag, nk // 4 - 1) if lead else 0
                between = lead if kt == 0 else []
                while todo and kt >= rest and (len(todo) > total - total * (kt + 1 - rest) // (due - rest) or kt + 1 >= due):
                    between.append(todo.pop(0))
                    if not todo:
                        turn = kt + 1
                for f in between[:1]:
                    f()
                keep = 2 if len(between) > 3 or self.wide and len(between) == 2 else 1
                late = between[1 + keep:]
                between = between[1:1 + keep]
                if i + 1 < len(steps):
                    self.scores(side, steps[i + 1][0], steps[i + 1][1], s + 1, between)
                elif nxt is not None and at + 1 < len(plan):
                    self.scores(other, following[0], 0, s + 1, between)
                else:
                    for f in between:
                        f()
                if begun is None and not self.units and nxt is not None:
                    begun = len(steps) // 2 if self.causal and at % 2 else i + (6 if self.wide else 8)
                    self.fetch(other, nxt)
                if begun is not None and i >= begun:
                    want = min(len(ahead) + done, -(-(i - begun + 1) * (len(ahead) + done) // (last - begun - 1)))
                    while done < want and ahead:
                        ahead.pop(0)()
                        done += 1
                if kt == turn:
                    self.shift(nside, nch, (n + 1) % 2)
                self.values(side, kt, nk, s, n, late)
                if self.units and (nk <= 8 or kt % 2):
                    self.unit(*self.units.pop(0))
                if kt == nk - 1:
                    while self.units:
                        self.unit(*self.units.pop(0))
                    self.units = [(side, ch, n, s, j, half) for j in range(self.qt) for half in range(G // 2)]
                    self.chunks += 1
                self.s += 1
        while self.units:
            self.unit(*self.units.pop(0))
        self.c.barrier()

    def run(self):
        self.first()
        if self.groups > 2:
            with self.c.nc.Fori(0, self.groups // 2 - 1) as i:
                self.stretch([(0, i * 2 + 1), (1, i * 2 + 2)])
        self.stretch([(0, self.groups - 1), (1, None)])


class RotaryAttention(Attention):

    def __init__(self, core, psum, io):
        super().__init__(core, psum, "L0", 16, 64, causal=True, scale=64 ** -0.5)
        c, nc, ctx = core, core.nc, core.ctx
        self.io = io
        sb = lambda n, s, d=F32: ctx.enter_context(nc.sbuf_tensor("L0_" + n, s, d))
        self.w = [[sb(f"w{d}{x}", [P, P]) for x in "kq"] for d in range(2)]
        self.wturned = [[sb(f"wt{d}{x}", [P, P]) for x in "kq"] for d in range(2)]
        self.Wv = [sb(f"Wv{d}", [P, P]) for d in range(2)]
        self.cosT = sb("cos", [P, T])
        self.sinT = sb("sin", [P, T])
        self.turned = sb("turned", [P, BANK])
        core.load(self.cosT[:, :], io["rope_cos"])
        core.load(self.sinT[:, :], io["rope_sin"])
        for t in (t for side in self.wturned for t in side):
            core.pool.done(nc.gpsimd.memset(t[:, :], 0.0))
        self.once()

    def load(self, side, g):
        io = self.io
        load = lambda o, i: self.arrived[side].add(self.c.nc.sync.dma_start(o, i))
        kv = io["L0_attn_w_kv"]
        for x, src in enumerate((kv, io["L0_attn_w_q"])):
            w = src[:, bass.ds(g * P, P)]
            load(self.w[side][x][:, :], w)
            w = w.rearrange("p (h d) -> p h d", h=2)
            turned = self.wturned[side][x][:, :].rearrange("p (h d) -> p h d", h=2)
            load(turned[:, :, 0:16], w[:, :, 16:32])
            load(turned[:, :, 16:32], w[:, :, 0:16])
        for h in range(2):
            wo = io["L0_attn_w_out"][bass.ds(g * P + h * 64, 64), :]
            load(self.Wo[side][h * 64:h * 64 + 64, 0, 129 * h:129 * h + 128], wo)
        load(self.Wv[side][:, :], kv[:, bass.ds(g * P + 1024, P)])

    def proj(self, side, h, which):
        return [(self.w[side][which], self.c.XNT, P), (self.wturned[side][which], self.c.XNT, P)]

    def project(self, side, h, which, b):
        c = self.c
        s = slice(b * BANK, (b + 1) * BANK)

        lows = []

        def straight():
            made = self.product(side, h, which, b, 0)
            c.dve.wait(made, *self.staged[which])
            t = c.dve.done(c.dve.e.tensor_tensor(self.stage[which][:, :], self.Y, self.cosT[:, s], ALU.mult))
            self.release(t)

        def turned():
            made = self.product(side, h, which, b, 1)
            c.dve.wait(made, self.turned_read)
            t = c.dve.done(c.dve.e.tensor_tensor(self.turned[:, :], self.Y, self.sinT[:, s], ALU.mult))
            self.release(t)
            c.dve.wait(t)
            st = self.stage[which]
            c.dve.wait(t)
            got = self.turned_read = c.dve.done(c.dve.e.tensor_tensor(st[:, :], st[:, :], self.turned[:, :], ALU.add))
            lows.append(self.split_pair(side, which, b, got, which))

        return [straight, turned, lambda: lows.pop()()]

    def vsrc(self):
        return self.c.XNT, P


class LatentAttention(Attention):

    def __init__(self, core, psum, io):
        super().__init__(core, psum, "L1", 8, 32, scale=32 ** -0.5)
        c, nc, ctx = core, core.nc, core.ctx
        self.io = io
        sb = lambda n, s, d=F32: ctx.enter_context(nc.sbuf_tensor("L1_" + n, s, d))
        self.w = [[[sb(f"w{d}{h}{x}", [P, 96]) for x in "kq"] for h in range(2)] for d in range(2)]
        self.Wv = [sb(f"Wv{d}", [64, 64]) for d in range(2)]
        self.down = sb("down", [P, 64])
        self.latent = sb("latent", [64, T])
        core.load(self.down[:, :], io["L1_attn_Wkv_down"])
        c.pe.wait(c.loads.all())
        for b in range(4):
            s = slice(b * BANK, (b + 1) * BANK)
            ps = psum.S[0:64, s]
            made = c.pe.done(c.pe.e.matmul(ps, self.down[:, :], c.XNT[:, s], start=True, stop=True))
            c.act.wait(made)
            c.act.done(c.act.e.activation(self.latent[:, s], ps, ACT.Copy))
        self.once()

    def load(self, side, g):
        io = self.io
        load = lambda o, i: self.arrived[side].add(self.c.nc.sync.dma_start(o, i))
        for h in range(2):
            for third in range(3):
                s = slice(32 * third, 32 * third + 32)
                load(self.w[side][h][0][0:64, s], io["L1_attn_Wk_up"][:, bass.ds(g * 64 + h * 32, 32)])
                load(self.w[side][h][1][:, s], io["L1_attn_Wq"][:, bass.ds(g * 64 + h * 32, 32)])
            load(self.Wo[side][h * 64:h * 64 + 32, 0, 129 * h:129 * h + 128], io["L1_attn_Wo"][bass.ds(g * 64 + h * 32, 32), :])
        load(self.Wv[side][:, :], io["L1_attn_Wv_up"][:, bass.ds(g * 64, 64)])

    def proj(self, side, h, which):
        return [(self.w[side][h][which], (self.latent, self.c.XNT)[which], (64, P)[which])]

    def affine(self, side, h, which):
        return 1.0, 0.0

    def vsrc(self):
        return self.latent, 64


class NarrowAttention(Attention):

    def __init__(self, core, psum, io, factor, xp):
        super().__init__(core, psum, "L2", 16, 8)
        c, nc, ctx = core, core.nc, core.ctx
        self.io, self.factor, self.xp = io, factor, xp
        sb = lambda n, s, d=F32: ctx.enter_context(nc.sbuf_tensor("L2_" + n, s, d))
        self.w = [[sb(f"w{d}{x}", [P, P]) for x in "kq"] for d in range(2)]
        self.brow = [[sb(f"brow{d}{x}", [1, 4, 32]) for x in "kq"] for d in range(2)]
        self.bias = [sb(f"bias{d}", [P, 2, 2]) for d in range(2)]
        self.parts = sb("parts", [P, 4])
        self.scaled_low = sb("scaled_low", [P, 1])
        self.low = [sb(f"low{i}", [P, BANK]) for i in range(2)]
        self.high = sb("high", [P, BANK], F32R)
        self.joined = sb("joined", [P, BANK], F32R)
        self.Wv = [sb(f"Wv{d}", [P, 32]) for d in range(2)]
        self.vbias = [sb(f"bv{d}", [P, 4, 8]) for d in range(2)]
        core.load(self.parts[:, :], io["narrow_parts"])
        for d in range(2):
            for x in range(2):
                core.pool.done(nc.gpsimd.memset(self.w[d][x][:, :], 0.0))
                t = core.pool.done(nc.gpsimd.memset(self.brow[d][x][:, :, :], 0.0))
            core.pool.wait(t)
            core.pool.done(nc.gpsimd.memset(self.brow[d][0][:, :, 0:1], 1.0))
        core.dve.wait(core.loads.all())
        core.dve.done(core.dve.e.tensor_tensor(self.scaled_low[:, :], self.factor[:, :], self.parts[:, 2:3], ALU.mult))
        self.once()

    def load(self, side, g):
        io = self.io
        load = lambda o, i: self.arrived[side].add(self.c.nc.sync.dma_start(o, i))
        for x, n in enumerate("kq"):
            W = io["L2_attn_W" + n][:, bass.ds(g * 32, 32)].rearrange("p (h d) -> p h d", h=4)
            b = io["L2_attn_b" + n][bass.ds(g * 32, 32)].rearrange("(a h d) -> a h d", a=1, h=4)
            w = self.w[side][x][:, :].rearrange("p (h d) -> p h d", h=4)
            for third in range(3):
                s = slice(8 * third + 1, 8 * third + 9)
                load(w[:, :, s], W)
                load(self.brow[side][x][:, :, s], b)
        for h in range(4):
            load(self.Wo[side][h * 32:h * 32 + 8, h // 2, 129 * (h % 2):129 * (h % 2) + 128], io["L2_attn_Wo"][bass.ds(g * 32 + h * 8, 8), :])
        load(self.Wv[side][:, :], io["L2_attn_Wv"][:, bass.ds(g * 32, 32)])
        load(self.vbias[side][:, :, :].rearrange("p h d -> p (h d)"), io["L2_attn_bv"][bass.ds(g * 32, 32)].partition_broadcast(P))

    def prepare(self, side):
        c = self.c
        dve, bias = c.dve, self.bias[side]
        self.take()
        for x in range(2):
            row = self.brow[side][x][:, :, :].rearrange("p h d -> p (h d)")
            m = c.pe.done(c.pe.e.matmul(self.Y[:, x:x + 1], row, c.onerow[:, 0:1], start=True, stop=True))
        dve.wait(m, self.arrived[side].all())
        dve.done(dve.e.tensor_copy(bias[:, 0, 0:1], self.Y[:, 0:1]))
        t = dve.done(dve.e.tensor_tensor(bias[:, 1, 0:1], self.Y[:, 1:2], self.factor[:, :], ALU.mult))
        self.release(t)
        dve.wait(t)
        for x in range(2):
            t = dve.done(dve.e.tensor_tensor(bias[:, x, 1:2], bias[:, x, 0:1], self.parts[:, 2 * x:2 * x + 1], ALU.mult))
        c.act.wait(t)

    def begin(self, banks, maxbanks):
        super().begin(banks, maxbanks)
        self.highread, self.joinedread = None, ()

    def project(self, side, h, which, b):
        c = self.c
        act, dve = c.act, c.dve
        held = []

        def unit():
            self.take()
            made = c.pe.done(c.pe.e.matmul(self.Y, self.w[side][which][:, :], self.xp[:, b * BANK:(b + 1) * BANK], start=True, stop=True))
            i = self.k % 2
            self.k += 1
            st, low, bias = self.stage[i], self.low[i], self.bias[side][:, which, :]
            act.wait(made, *self.staged[i])
            all_rows = act.done(act.e.activation(st[:, :], self.Y, ACT.Identity, scale=self.factor[:, :] if which else 1.0, bias=bias[:, 0:1]))
            low_rows = act.done(act.e.activation(low[:, :], self.Y, ACT.Identity, scale=self.scaled_low[:, :] if which else self.parts[:, 0:1], bias=bias[:, 1:2]))
            self.release(low_rows)
            held.append((i, st, low, all_rows, low_rows))

        def join():
            i, st, low, all_rows, low_rows = held.pop()
            s, before = self.place(side, which, b)
            dve.wait(all_rows, self.highread)
            hi = dve.done(dve.e.tensor_copy(self.high[:, :], st[:, :]))
            out = self.joined[:, :] if which else self.Ka[side][0][:, s]
            dve.wait(hi, low_rows, *(self.joinedread if which else (before,)))
            t = dve.done(dve.e.scalar_tensor_tensor(out, free(self.high[:, :]), self.parts[:, 2 * which + 1:2 * which + 2], low[:, :], ALU.mult, ALU.add))
            self.staged[i] = (t,)
            self.highread = t
            if which == 0:
                self.kmade[side, b] = (t,)
                return
            for h in range(4):
                rows = slice(32 * h, 32 * h + 32)
                q = c.pool if h else dve
                q.wait(t, before, (q.sem, q.count))
                done = q.done(q.e.tensor_copy(self.Qa[h][rows, s], free(self.joined[rows, :])))
                self.qmade[self.qplace[side, b], h] = (done,)
            self.joinedread = (self.qmade[self.qplace[side, b], 0] + (done,))

        return [unit, join]

    def vsrc(self):
        return self.xp, P


class NormedAttention(Attention):

    def __init__(self, core, psum, io, srcs):
        super().__init__(core, psum, "L3", 16, 64, last_key_mask=True)
        c, nc, ctx = core, core.nc, core.ctx
        self.io, self.srcs = io, srcs
        sb = lambda n, s, d=F32: ctx.enter_context(nc.sbuf_tensor("L3_" + n, s, d))
        self.w = [[sb(f"w{d}{x}", [P, P]) for x in "kq"] for d in range(2)]
        self.Wv = [sb(f"Wv{d}", [P, P]) for d in range(2)]
        self.bias = [sb(f"bias{d}", [P, 2]) for d in range(2)]
        self.qbias = [sb(f"qbias{d}", [P, 1]) for d in range(2)]
        self.vbias = [sb(f"bv{d}", [P, 2, 64]) for d in range(2)]
        self.smax = 1.0 / float(D) ** 0.5
        self.once()

    def load(self, side, g):
        io = self.io
        load = lambda o, i: self.arrived[side].add(self.c.nc.sync.dma_start(o, i))
        for x, n in enumerate("kq"):
            load(self.w[side][x][:, :], io["L3_attn_W" + n][:, bass.ds(g * P, P)])
            with self.c.nc.allow_non_contiguous_dma("128 elements"):
                load(self.bias[side][:, x:x + 1], io["L3_attn_b" + n][bass.ds(g * P, P)].rearrange("(p a) -> p a", a=1))
        for h in range(2):
            load(self.Wo[side][h * 64:h * 64 + 64, 0, 129 * h:129 * h + 128], io["L3_attn_Wo"][bass.ds(g * P + h * 64, 64), :])
        load(self.Wv[side][:, :], io["L3_attn_Wv"][:, bass.ds(g * P, P)])
        load(self.vbias[side][:, :, :].rearrange("p h d -> p (h d)"), io["L3_attn_bv"][bass.ds(g * P, P)].partition_broadcast(P))

    def prepare(self, side):
        c = self.c
        c.dve.wait(self.arrived[side].all())
        t = c.dve.done(c.dve.e.tensor_scalar(self.qbias[side][:, :], self.bias[side][:, 1:2], self.smax, None, ALU.mult))
        c.act.wait(t)

    def proj(self, side, h, which):
        return [(self.w[side][which], self.srcs[which], P)]

    def affine(self, side, h, which):
        if which:
            return self.smax, self.qbias[side][:, :]
        return 1.0, self.bias[side][:, 0:1]

    def vsrc(self):
        return self.srcs[2], P


class Psum:

    def __init__(self, nc, ctx):
        self.all = ctx.enter_context(nc.psum_tensor("banks", [P, 8 * BANK], F32))
        self.S = self.all[:, 0:4 * BANK]
        self.MX = self.all[:, 4 * BANK:6 * BANK]
        self.O = self.all[:, 6 * BANK:7 * BANK]
        self.Y = self.all[:, 7 * BANK:8 * BANK]

    def bank(self, i):
        return self.all[:, i * BANK:(i + 1) * BANK]


def rstd_of(core, var, eps, tmp, out, n):
    act, dve = core.act, core.dve
    a, b = tmp
    e = dve.done(dve.e.tensor_scalar(a, var, eps, None, ALU.add))
    act.wait(e)
    r = act.done(act.e.activation(b, a, ACT.Sqrt))
    dve.wait(r, e)
    y = dve.done(dve.e.reciprocal(out, b))
    dve.wait(y)
    t = dve.done(dve.e.tensor_tensor(b, out, out, ALU.mult))
    dve.wait(t)
    t = dve.done(dve.e.tensor_tensor(b, b, a, ALU.mult))
    dve.wait(t)
    t = dve.done(dve.e.tensor_scalar(b, b, -0.5, 1.5, ALU.mult, ALU.add))
    dve.wait(t)
    return dve.done(dve.e.tensor_tensor(out, out, b, ALU.mult))


class Norm:

    def __init__(self, core, name, n=NT):
        nc, ctx = core.nc, core.ctx
        self.c = core
        self.n = n
        sb = lambda x, s: ctx.enter_context(nc.sbuf_tensor(name + "_" + x, s, F32))
        self.stats = sb("stats", [P, n, 6])
        self.mv = sb("mv", [P, n, 2])
        self.a = sb("a", [P, n])
        self.b = sb("b", [P, n])
        self.rstd = sb("rstd", [P, n])

    def run(self, src, dst, eps=1e-5, ready=(), readers=()):
        dve = self.c.dve
        dve.wait(*ready)
        for i in range(self.n):
            t = dve.done(dve.e.bn_stats(self.stats[:, i, :], src(i)))
        dve.wait(t)
        for i in range(self.n):
            t = dve.done(dve.e.bn_aggr(self.mv[:, i, :], self.stats[:, i, :]))
        dve.wait(t)
        t = rstd_of(self.c, self.mv[:, :, 1], eps, (self.a[:, :], self.b[:, :]), self.rstd[:, :], self.n)
        dve.wait(t, *readers)
        out = []
        for i in range(self.n):
            out.append(dve.done(dve.e.tensor_scalar(dst(i), src(i), self.mv[:, i, 0:1], self.rstd[:, i:i + 1], ALU.subtract, ALU.mult)))
        return out


def to_features(core, psum, src, dst, made, scale=1.0, bias=0.0):
    pe, act = core.pe, core.act
    read = [None] * 2
    for b in range(4):
        ps = psum.bank(b % 2)
        pe.wait(read[b % 2], made[4 * b + 3])
        for j in range(4):
            m = pe.e.transpose(ps[:, j * P:(j + 1) * P], src[:, 4 * b + j, :], core.ident[:, :])
        m = pe.done(m)
        act.wait(m)
        read[b % 2] = act.done(act.e.activation(dst[:, b * BANK:(b + 1) * BANK], ps, ACT.Identity, scale=scale, bias=bias))
    return read[1]


def quantized_ffn(core, psum, io):
    nc = core.nc
    pe, act, dve = core.pe, core.act, core.dve
    with ExitStack() as ctx:
        sb = lambda n, s, d=F32: ctx.enter_context(nc.sbuf_tensor("F0_" + n, s, d))
        H = 384
        raw = [sb(f"raw{i}", [P, H], I32) for i in range(3)]
        w = [sb(f"w{i}", [P, H]) for i in range(3)]
        g = [sb(f"g{i}", [P, BANK]) for i in range(2)]
        h = sb("h", [P, 2, 3, BANK])
        core.load(raw[0][:, :], io["L0_ffn_w_gate"])
        core.load(raw[1][:, :], io["L0_ffn_w_up"])
        core.load(raw[2][:, :].rearrange("p (j d) -> p j d", j=3), io["L0_ffn_w_down"].rearrange("(j p) d -> p j d", p=P))
        dve.wait(core.loads.all())
        for i in range(3):
            ready = dve.done(dve.e.tensor_scalar(w[i][:, :], raw[i][:, :], 1.0 / 127.0, None, ALU.mult))
        pe.wait(ready)
        read = [None] * 8
        gread = [None] * 2
        hread = [None] * 2
        n = 0
        for c in range(4):
            s = slice(c * BANK, (c + 1) * BANK)
            for j in range(3):
                a, b = psum.bank(2 * (n % 2)), psum.bank(2 * (n % 2) + 1)
                pe.wait(read[2 * (n % 2)], read[2 * (n % 2) + 1])
                pe.e.matmul(a, w[0][:, j * P:(j + 1) * P], core.XNT[:, s], start=True, stop=True)
                made = pe.done(pe.e.matmul(b, w[1][:, j * P:(j + 1) * P], core.XNT[:, s], start=True, stop=True))
                act.wait(made, gread[n % 2])
                sg = read[2 * (n % 2)] = act.done(act.e.activation(g[n % 2][:, :], a, ACT.Silu))
                dve.wait(sg, hread[c % 2])
                up = read[2 * (n % 2) + 1] = gread[n % 2] = dve.done(dve.e.tensor_tensor(h[:, c % 2, j, :], g[n % 2][:, :], b, ALU.mult))
                n += 1
            y = psum.bank(4 + c % 2)
            pe.wait(up, read[4 + c % 2])
            for q in range(4):
                for j in range(3):
                    mm = pe.e.matmul(y[:, q * P:(q + 1) * P], h[:, c % 2, j, q * P:(q + 1) * P], w[2][:, j * P:(j + 1) * P], start=j == 0, stop=j == 2)
            hread[c % 2] = pe.done(mm)
            act.wait(hread[c % 2])
            read[4 + c % 2] = act.done(act.e.activation(core.GATE[:, 4 * c:4 * c + 4, :], y.rearrange("p (q d) -> p q d", q=4), ACT.Silu))
        core.barrier()


def transformer_gate(core, psum, io):
    nc = core.nc
    pe, act, dve, pool = core.pe, core.act, core.dve, core.pool
    HEADS, HID = 8, 341
    HT = [(0, 128), (128, 128), (256, 85)]
    with ExitStack() as ctx:
        sb = lambda n, s, d=F32: ctx.enter_context(nc.sbuf_tensor("F1_" + n, s, d))
        state = core.SACC
        xs = sb("xs", [P, 5, D])
        hT = sb("hT", [P, BANK])
        carry = sb("carry", [P, 1])
        wqkv = sb("wqkv", [P, 1536])
        wo = sb("wo", [P, 4, P])
        w1 = sb("w1", [P, 2 * HID])
        w2 = sb("w2", [P, 3, P])
        b1 = sb("b1", [P, 2, 3])
        b2 = sb("b2", [1, P])
        lgb = sb("lgb", [P, 2])
        gains = sb("gains", [P, 2, 64])
        tab = sb("tab", [P, 4, 4, 64])
        ssq = sb("ssq", [P, 3, 4, 2, HEADS])
        sq = [sb(f"sq{i}", [P, BANK]) for i in range(2)]
        qn = [[sb(f"{x}n{i}", [P, HEADS, 64]) for i in range(4)] for x in "qk"]
        rot = [sb(f"rot{i}", [P, HEADS, 64]) for i in range(2)]
        qT = [sb(f"qT{i}", [P, 4, P]) for i in range(2)]
        kT = sb("kT", [P, 4, 2, 5 * P])
        V = sb("V", [P, 5, BANK])
        mask = sb("mask", [P, 2, 256], BF16)
        maskf = sb("maskf", [P, 1])
        wts = [sb(f"wts{i}", [P, 4, 256]) for i in range(2)]
        wT = [sb(f"wT{i}", [P, 8, P]) for i in range(2)]
        nm = sb("nm", [P, 4, HEADS])
        den = sb("den", [P, 4, HEADS])
        o = [sb(f"o{i}", [P, BANK]) for i in range(2)]
        oT = [sb(f"oT{i}", [P, BANK]) for i in range(2)]
        z = sb("z", [P, 4, D])
        zT = sb("zT", [P, BANK])
        g = [sb(f"g{i}", [P, BANK]) for i in range(2)]
        u = sb("u", [P, 3, BANK])
        moves = sb("moves", [P, 2, P])
        st6, mv = sb("st6", [P, 4, 6]), sb("mv", [P, 4, 2])
        ra, rb, rstd = sb("ra", [P, 4]), sb("rb", [P, 4]), sb("rstd", [P, 4])
        S4 = psum.S
        core.load(moves[:, :, :], io["row_moves"])
        core.load(mask[:, 1, :], io["band_mask"].bitcast(BF16)[1])
        t = pool.done(pool.e.tensor_copy(state[:, :, :], core.XN[:, :, :]))
        pool.done(pool.e.memset(kT[:, :, :, :], 0.0))
        core.sp.wait(core.loads.all())
        core.barrier()
        for l in range(2):
            core.load(wqkv[:, :], io["L1_ffn_wqkv"][l])
            core.load(wo[:, :, :], io["L1_ffn_wo"][l].rearrange("(j p) d -> p j d", p=P))
            core.load(w1[:, :], io["L1_ffn_w1"][l])
            core.load(b2[:, :], io["L1_ffn_b2"][l].rearrange("(a d) -> a d", a=1))
            core.load(gains[:, 0, :], io["L1_ffn_q_scale"][l].partition_broadcast(P))
            core.load(gains[:, 1, :], io["L1_ffn_k_scale"][l].partition_broadcast(P))
            with nc.allow_non_contiguous_dma("small columns"):
                core.load(lgb[:, 0:1], io["L1_ffn_ln_g"][l].rearrange("(p a) -> p a", a=1))
                core.load(lgb[:, 1:2], io["L1_ffn_ln_b"][l].rearrange("(p a) -> p a", a=1))
                for j, (a, n) in enumerate(HT):
                    core.load(w2[0:n, j, :], io["L1_ffn_w2"][l][a:a + n, :])
                    for half in range(2):
                        core.load(b1[0:n, half, j:j + 1], io["L1_ffn_b1"][l][half * HID + a:half * HID + a + n].rearrange("(p a) -> p a", a=1))
            t = [pool.done(pool.e.memset(x, 0.0)) for x in (kT[:, :, :, 0:P], V[:, 0, :], xs[:, 0, :], carry[:, :])]
            core.sp.wait(core.loads.all())
            core.barrier()
            with nc.Fori(0, 4) as c:
                core.load(tab[:, :, :, :], io["xpos"][:, bass.ds(c * 4, 4), :, :])
                core.load(mask[:, 0, :], io["first_masks"].bitcast(BF16)[bass.ds(c, 1), :, :].rearrange("a p k -> p (a k)"))
                m = dve.done(dve.e.tensor_copy(xs[:, 1:5, :], state[:, bass.ds(c * 4, 4), :]))
                pe.wait(m)
                for j in range(4):
                    m = pe.e.transpose(psum.bank(0)[:, j * P:(j + 1) * P], xs[:, 1 + j, :], core.ident[:, :])
                m = pe.done(m)
                act.wait(m)
                a0 = act.done(act.e.activation(hT[0:64, :], psum.bank(0)[0:64, :], ACT.Copy))
                act.done(act.e.activation(hT[64:P, 1:BANK], psum.bank(0)[64:P, 0:BANK - 1], ACT.Copy))
                m = act.done(act.e.activation(hT[64:P, 0:1], carry[64:P, :], ACT.Copy))
                act.wait(m)
                hmade = act.done(act.e.activation(carry[64:P, :], psum.bank(0)[64:P, BANK - 1:BANK], ACT.Copy))
                dve.wait(core.loads.all())
                pe.wait(core.loads.all())
                for x in range(2):
                    gx = gains[:, x:x + 1, :]
                    dve.done(dve.e.tensor_tensor(tab[:, :, 2 * x, :], tab[:, :, 2 * x, :], gx.to_broadcast([P, 4, 64]), ALU.mult))
                    dve.done(dve.e.tensor_tensor(tab[:, :, 2 * x + 1, 0:32], tab[:, :, 2 * x + 1, 0:32], gx[:, :, 32:64].to_broadcast([P, 4, 32]), ALU.mult))
                    tabs = dve.done(dve.e.tensor_tensor(tab[:, :, 2 * x + 1, 32:64], tab[:, :, 2 * x + 1, 32:64], gx[:, :, 0:32].to_broadcast([P, 4, 32]), ALU.mult))
                def chain(ins):
                    t = dve.done(ins)
                    dve.wait(t)
                    return t

                def norms(tiles):
                    A, B, C = (ssq[:, i, tiles, :, :] for i in range(3))
                    act.wait(sqread[0], sqread[1])
                    m = act.done(act.e.activation(B, A, ACT.Sqrt))
                    dve.wait(m, sqread[1])
                    chain(dve.e.tensor_scalar(B, B, 1e-12, None, ALU.max))
                    chain(dve.e.reciprocal(C, B))
                    chain(dve.e.tensor_tensor(C, C, A, ALU.mult))
                    chain(dve.e.tensor_tensor(B, B, C, ALU.add))
                    chain(dve.e.tensor_scalar(B, B, 0.5, 1e-12, ALU.mult, ALU.max))
                    chain(dve.e.reciprocal(A, B))

                rread = [None] * 2
                turned = {}

                def rotate(i, x):
                    dve.wait(plain, tabs)
                    v = qn[x][i]
                    over = lambda y, w=64: y.to_broadcast([P, HEADS, w])
                    chain(dve.e.tensor_tensor(v[:, :, :], v[:, :, :], ssq[:, 0, i, x, :].rearrange("p (h a) -> p h a", a=1).to_broadcast([P, HEADS, 64]), ALU.mult))
                    r = rot[x]
                    dve.wait(rread[x])
                    dve.done(dve.e.tensor_tensor(r[:, :, 0:32], v[:, :, 32:64], over(tab[:, i, 2 * x + 1:2 * x + 2, 0:32], 32), ALU.mult))
                    m = dve.done(dve.e.tensor_tensor(r[:, :, 32:64], v[:, :, 0:32], over(tab[:, i, 2 * x + 1:2 * x + 2, 32:64], 32), ALU.mult))
                    dve.wait(m)
                    m = dve.done(dve.e.tensor_tensor(v[:, :, :], v[:, :, :], over(tab[:, i, 2 * x:2 * x + 1, :]), ALU.mult))
                    pool.wait(m)
                    rread[x] = turned[x, i] = pool.done(pool.e.tensor_tensor(v[:, :, :], v[:, :, :], r[:, :, :], ALU.add))

                read = [None] * 8
                n = 0
                sqread = [None] * 2
                pe.wait(hmade)
                for i in range(4):
                    for x in range(3):
                        b0 = n % 8
                        n += 1
                        ps = psum.bank(b0)
                        pe.wait(read[b0])
                        m = pe.done(pe.e.matmul(ps, hT[:, i * P:(i + 1) * P], wqkv[:, x * BANK:(x + 1) * BANK], start=True, stop=True))
                        act.wait(m)
                        if x == 2:
                            vmade = read[b0] = act.done(act.e.activation(V[:, 1 + i, :], ps, ACT.Copy))
                            continue
                        act.wait(sqread[x])
                        s2 = act.done(act.e.activation(sq[x][:, :], ps, ACT.Square))
                        plain = read[b0] = act.done(act.e.activation(qn[x][i][:, :, :], ps.rearrange("p (h d) -> p h d", h=HEADS), ACT.Copy))
                        dve.wait(s2)
                        sqread[x] = dve.done(dve.e.tensor_reduce(ssq[:, 0, i, x, :], sq[x][:, :].rearrange("p (h d) -> p h d", h=HEADS), AX.X, ALU.add))
                    if i == 2:
                        norms(slice(0, 1))
                        rotate(0, 1)
                        rotate(0, 0)
                norms(slice(1, 4))
                free4 = list(read[4:8])
                bufread = [(read[0], read[1]), (read[2], read[3])]
                qmade, kmade, qused = [None] * 4, [None] * 4, [None] * 2
                expd, wread = [None] * 8, [None] * 8
                copied, pvread = [None] * 8, [None] * 8
                xnew = [None] * 4

                def keys(i):
                    ps = psum.bank(4)
                    pe.wait(free4[0], turned[1, i])
                    for j in range(4):
                        m = pe.e.transpose(ps[:, j * P:(j + 1) * P], qn[1][i][:, 2 * j:2 * j + 2, :].rearrange("p h d -> p (h d)"), core.ident[:, :])
                    m = pe.done(m)
                    act.wait(m)
                    ps = ps.rearrange("p (j t) -> p j t", j=4)
                    s = slice((1 + i) * P, (2 + i) * P)
                    act.done(act.e.activation(kT[0:64, :, 0, s], ps[0:64, :, :], ACT.Copy))
                    kmade[i] = free4[0] = act.done(act.e.activation(kT[64:P, :, 1, s], ps[64:P, :, :], ACT.Copy))

                def queries(i):
                    ps = psum.bank(4)
                    pe.wait(free4[0], turned[0, i])
                    for j in range(4):
                        m = pe.e.transpose(ps[:, j * P:(j + 1) * P], qn[0][i][:, 2 * j:2 * j + 2, :].rearrange("p h d -> p (h d)"), core.ident[:, :])
                    m = pe.done(m)
                    act.wait(m, qused[i % 2])
                    qmade[i] = free4[0] = act.done(act.e.activation(qT[i % 2][:, :, :], ps.rearrange("p (j t) -> p j t", j=4), ACT.Copy))

                def softmax(v):
                    i, hs = v // 2, slice(4 * (v % 2), 4 * (v % 2) + 4)
                    S = S4[:, (v % 2) * 1024:(v % 2) * 1024 + 1024]
                    pe.wait(qmade[i], kmade[i], *bufread[v % 2])
                    for x in range(4):
                        h = hs.start + x
                        so = S[:, x * 256:(x + 1) * 256]
                        pe.e.matmul(so, qT[i % 2][:, h // 2, :], kT[:, h // 2, h % 2, i * P:(i + 2) * P], start=True, stop=False)
                        m = pe.e.matmul(so, core.identb[:, :], mask[:, min(i, 1), :], start=False, stop=True)
                    m = qused[i % 2] = pe.done(m)
                    dve.wait(m)
                    m = dve.done(dve.e.tensor_reduce(nm[:, i, hs], S.rearrange("p (h k) -> p h k", h=4), AX.X, ALU.max, negate=True))
                    dve.wait(m)
                    m = dve.done(dve.e.tensor_scalar(nm[:, i, hs], nm[:, i, hs], 8.0, None, ALU.mult))
                    act.wait(m, wread[v - 2] if v > 1 else None)
                    for x in range(4):
                        h = hs.start + x
                        m = act.done(act.e.activation(wts[v % 2][:, x, :], S[:, x * 256:(x + 1) * 256], ACT.Exp, bias=nm[:, i, h:h + 1], scale=8.0, accum_out=den[:, i, h:h + 1]))
                    expd[v] = m

                def turn(v):
                    S = S4[:, (v % 2) * 1024:(v % 2) * 1024 + 1024]
                    pe.wait(expd[v])
                    for x in range(8):
                        m = pe.e.transpose(S[:, x * P:(x + 1) * P], wts[v % 2][:, x // 2, x % 2 * P:(x % 2 + 1) * P], core.ident[:, :])
                    m = wread[v] = pe.done(m)
                    dve.wait(m, pvread[v - 2] if v > 1 else None)
                    copied[v] = dve.done(dve.e.tensor_copy(wT[v % 2][:, :, :].rearrange("p a b -> p (a b)"), S))
                    bufread[v % 2] = (copied[v],)

                def heads(v):
                    i = v // 2
                    ps = psum.bank(5)
                    pe.wait(copied[v], vmade)
                    if v % 2 == 0:
                        pe.wait(free4[1])
                    for x in range(4):
                        h = 4 * (v % 2) + x
                        for k in range(2):
                            m = pe.e.matmul(ps[:, h * 64:(h + 1) * 64], wT[v % 2][:, 2 * x + k, :], V[:, i + k, h * 64:(h + 1) * 64], start=k == 0, stop=k == 1)
                    m = pvread[v] = pe.done(m)
                    if v % 2:
                        dve.wait(expd[v], expd[v - 1])
                        rden = dve.done(dve.e.reciprocal(den[:, i, :], den[:, i, :]))
                        dve.wait(m, rden, oused[i % 2])
                        free4[1] = dve.done(dve.e.tensor_tensor(o[i % 2][:, :].rearrange("p (h d) -> p h d", h=HEADS), ps.rearrange("p (h d) -> p h d", h=HEADS), den[:, i, :].rearrange("p (h a) -> p h a", a=1).to_broadcast([P, HEADS, 64]), ALU.mult))

                oused, oTmade, oTused = [None] * 2, [None] * 4, [None] * 2

                def turn_heads(i):
                    ps = psum.bank(6)
                    pe.wait(free4[1], free4[2])
                    for j in range(4):
                        m = pe.e.transpose(ps[:, j * P:(j + 1) * P], o[i % 2][:, j * P:(j + 1) * P], core.ident[:, :])
                    m = oused[i % 2] = pe.done(m)
                    act.wait(m, oTused[i % 2])
                    oTmade[i] = free4[2] = act.done(act.e.activation(oT[i % 2][:, :], ps, ACT.Copy))

                def join_heads(i):
                    ps = psum.bank(7)
                    pe.wait(oTmade[i], free4[3])
                    for j in range(4):
                        m = pe.e.matmul(ps[:, 0:P], oT[i % 2][:, j * P:(j + 1) * P], wo[:, j, :], start=j == 0, stop=j == 3)
                    m = oTused[i % 2] = pe.done(m)
                    dve.wait(m)
                    xnew[i] = free4[3] = dve.done(dve.e.tensor_tensor(xs[:, 1 + i, :], xs[:, 1 + i, :], ps[:, 0:P], ALU.add))

                keys(0)
                queries(0)
                softmax(0)
                zmade = [None] * 4
                rotate(1, 1)
                rotate(1, 0)
                def shift(i):
                    ps = psum.bank(7)[:, P:2 * P]
                    pe.wait(xnew[i], free4[3])
                    pe.e.matmul(ps[:, 0:64], core.ident[:, :], xs[:, 1 + i, 0:64], start=True, stop=True)
                    pe.e.matmul(ps[:, 64:P], moves[:, 0, :], xs[:, 1 + i, 64:P], start=True, stop=False)
                    m = pe.done(pe.e.matmul(ps[:, 64:P], moves[:, 1, :], xs[:, i, 64:P], start=False, stop=True))
                    dve.wait(m)
                    t = free4[3] = dve.done(dve.e.tensor_copy(z[:, i, :], ps))
                    dve.wait(t)
                    zmade[i] = dve.done(dve.e.bn_stats(st6[:, i, :], z[:, i, :]))

                for v in range(11):
                    if v < 7:
                        softmax(v + 1)
                    if 1 <= v <= 8:
                        heads(v - 1)
                    if v < 8:
                        turn(v)
                    if v % 2 == 0 and v // 2 + 1 < 4:
                        keys(v // 2 + 1)
                        queries(v // 2 + 1)
                    if v // 2 + 2 < 4:
                        rotate(v // 2 + 2, 1 - v % 2)
                    if v == 7:
                        pool.wait(qused[0], qused[1], kmade[3])
                        pool.done(pool.e.tensor_copy(kT[:, :, :, 0:P], kT[:, :, :, 4 * P:5 * P]))
                    if v == 3:
                        pool.wait(pvread[1], vmade)
                        pool.done(pool.e.tensor_copy(V[:, 0, :], V[:, 4, :]))
                    if v >= 2 and v % 2 == 0 and v // 2 - 1 < 4:
                        turn_heads(v // 2 - 1)
                    if v >= 3 and v % 2 and v // 2 - 1 < 4:
                        join_heads(v // 2 - 1)
                    if v >= 4 and v % 2 == 0 and v // 2 - 2 < 3:
                        shift(v // 2 - 2)
                shift(3)
                sread = bufread[0] + bufread[1]
                t = zmade[3]
                dve.wait(t)
                for i in range(4):
                    t = dve.done(dve.e.bn_aggr(mv[:, i, :], st6[:, i, :]))
                dve.wait(t)
                t = rstd_of(core, mv[:, :, 1], 1e-5, (ra[:, :], rb[:, :]), rstd[:, :], 4)
                dve.wait(t)
                for i in range(4):
                    t = dve.done(dve.e.tensor_scalar(z[:, i, :], z[:, i, :], mv[:, i, 0:1], rstd[:, i:i + 1], ALU.subtract, ALU.mult))
                pe.wait(t, *sread)
                for i in range(4):
                    m = pe.e.transpose(psum.bank(0)[:, i * P:(i + 1) * P], z[:, i, :], core.ident[:, :])
                m = pe.done(m)
                act.wait(m, core.loads.all())
                m = act.done(act.e.activation(zT[:, :], psum.bank(0), ACT.Identity, scale=lgb[:, 0:1], bias=lgb[:, 1:2]))
                pe.wait(m)
                for j, (a, w) in enumerate(HT):
                    pa, pg = psum.bank(1 + j), psum.bank(4 + j)
                    pe.wait(free4[j])
                    pe.e.matmul(pa[0:w, :], w1[:, a:a + w], zT[:, :], start=True, stop=True)
                    m = pe.done(pe.e.matmul(pg[0:w, :], w1[:, HID + a:HID + a + w], zT[:, :], start=True, stop=True))
                    act.wait(m)
                    if j == 2:
                        act.wait(umade)
                    m = act.done(act.e.activation(g[j % 2][0:w, :], pg[0:w, :], ACT.Gelu, bias=b1[0:w, 1, j:j + 1]))
                    dve.wait(m)
                    t = dve.done(dve.e.scalar_tensor_tensor(u[0:w, j, :], pa[0:w, :], b1[0:w, 0, j:j + 1], g[j % 2][0:w, :], ALU.add, ALU.mult))
                    if j == 0:
                        umade = t
                pe.wait(t, free4[3])
                ps = psum.bank(7)
                for i in range(4):
                    for j, (a, w) in enumerate(HT):
                        pe.e.matmul(ps[:, i * P:(i + 1) * P], u[0:w, j, i * P:(i + 1) * P], w2[0:w, j, :], start=j == 0, stop=False)
                    m = pe.e.matmul(ps[:, i * P:(i + 1) * P], core.onerow[:, 0:P], b2[:, :], start=False, stop=True)
                m = pe.done(m)
                dve.wait(m)
                t = dve.done(dve.e.tensor_tensor(state[:, bass.ds(c * 4, 4), :], xs[:, 1:5, :], ps.rearrange("p (i d) -> p i d", i=4), ALU.add))
                pool.wait(t, m)
                pool.done(pool.e.tensor_copy(xs[:, 0, :], xs[:, 4, :]))
                core.barrier()
        act.done(act.e.activation(core.GATE[:, :, :], state[:, :, :], ACT.Silu))
        core.barrier()
        pool.done(pool.e.memset(state[:, :, :], 0.0))
        core.barrier()


def ternary_ffn(core, psum, io, positions):
    nc = core.nc
    pe, act, dve = core.pe, core.act, core.dve
    with ExitStack() as ctx:
        sb = lambda n, s, d=F32: ctx.enter_context(nc.sbuf_tensor("F2_" + n, s, d))
        H = 512
        w1, w2 = sb("w1", [P, H]), sb("w2", [P, H])
        h1, h2 = sb("h1", [P, 4, H]), sb("h2", [P, 4, H])
        w3 = sb("w3", [P, 4, P])
        s3 = sb("s3", [P, P])
        sc = sb("sc", [P, 4, 4])
        a = [sb(f"a{i}", [P, BANK]) for i in range(2)]
        u = [sb(f"u{i}", [P, 4, BANK]) for i in range(3)]
        core.load(w1[:, :], io["L2_ffn_w1_w"])
        core.load(w2[:, :], io["L2_ffn_w2_w"])
        for t, n in ((h1, "h1_w"), (h2, "h2_w"), (w3, "w3_w")):
            core.load(t[:, :, :], io["L2_ffn_" + n].rearrange("(j p) o -> p j o", p=P))
        core.load(s3[:, :], io["L2_ffn_w3_s"].partition_broadcast(P))
        with nc.allow_non_contiguous_dma("512 scales"):
            for i, n in enumerate(("w1_s", "w2_s", "h1_s", "h2_s")):
                core.load(sc[:, i, :], io["L2_ffn_" + n].rearrange("(j p) -> p j", p=P))
        dve.wait(core.loads.all())
        for j in range(4):
            ready = dve.done(dve.e.tensor_tensor(w3[:, j, :], w3[:, j, :], s3[:, :], ALU.mult))
        pe.wait(core.loads.all(), ready)
        act.wait(core.loads.all())
        read = [None] * 8
        n = 0
        aread = [None] * 2
        uread = [None] * 3
        for c in range(4):
            s = slice(c * BANK, (c + 1) * BANK)
            for j in range(4):
                js = slice(j * P, (j + 1) * P)
                b0, b1 = n % 8, (n + 1) % 8
                n += 2
                p0, p1 = psum.bank(b0), psum.bank(b1)
                pe.wait(read[b0], read[b1])
                pe.e.matmul(p0, w1[:, js], core.XNT[:, s], start=True, stop=True)
                made = pe.done(pe.e.matmul(p1, w2[:, js], core.XNT[:, s], start=True, stop=True))
                act.wait(made, aread[j % 2])
                sg = read[b0] = act.done(act.e.activation(a[j % 2][:, :], p0, ACT.Silu, scale=sc[:, 0, j:j + 1]))
                dve.wait(sg, uread[0])
                last = read[b1] = aread[j % 2] = dve.done(dve.e.scalar_tensor_tensor(u[0][:, j, :], p1, sc[:, 1, j:j + 1], a[j % 2][:, :], ALU.mult, ALU.mult))
            if c == 0:
                positions.begin()
            for layer, w in ((1, h1), (2, h2)):
                for j in range(4):
                    b0 = n % 8
                    n += 1
                    p0 = psum.bank(b0)
                    pe.wait(read[b0], last)
                    for i in range(4):
                        mm = pe.e.matmul(p0, w[:, i, j * P:(j + 1) * P], u[layer - 1][:, i, :], start=i == 0, stop=i == 3)
                    uread[layer - 1] = made = pe.done(mm)
                    act.wait(made, uread[layer])
                    nxt = read[b0] = act.done(act.e.activation(u[layer][:, j, :], p0, ACT.Gelu, scale=sc[:, layer + 1, j:j + 1]))
                last = nxt
            b0 = n % 8
            n += 1
            y = psum.bank(b0)
            pe.wait(read[b0], last)
            for q in range(4):
                for j in range(4):
                    mm = pe.e.matmul(y[:, q * P:(q + 1) * P], u[2][:, j, q * P:(q + 1) * P], w3[:, j, :], start=j == 0, stop=j == 3)
            uread[2] = made = pe.done(mm)
            act.wait(made)
            read[b0] = act.done(act.e.activation(core.GATE[:, 4 * c:4 * c + 4, :], y.rearrange("p (q d) -> p q d", q=4), ACT.Silu))
        for i in range(2):
            pe.wait(read[i])
        positions.finish()
        core.barrier()


class Positions:

    def __init__(self, core, psum, io, ctx):
        self.core, self.psum = core, psum
        sb = lambda n, s, d=F32: ctx.enter_context(core.nc.sbuf_tensor("A2_" + n, s, d))
        self.rby = sb("rby", [P, 3])
        self.f = sb("f", [P, 8])
        self.factor = sb("factor", [P, 1])
        self.denom = sb("denom", [P, 2])
        self.xp = sb("xp", [P, T])
        self.xpt = sb("xpt", [P, NT, D])
        self.pos = sb("pos", [P, T])
        self.turns = sb("turns", [P, T])
        self.whole = sb("whole", [P, T], I32)
        core.load(self.denom[:, :], io["position_denominators"])
        core.load(self.rby[:, :], io["L2_attn_rby"].partition_broadcast(P))

    def chain(self, ins):
        t = self.core.dve.done(ins)
        self.core.dve.wait(t)
        return t

    def begin(self):
        dve, pool, chain = self.core.dve, self.core.pool, self.chain
        f, factor, denom, pos, turns, whole = self.f, self.factor, self.denom, self.pos, self.turns, self.whole
        red, blue, yellow = (self.rby[:, i:i + 1] for i in range(3))
        chain(dve.e.tensor_scalar(f[:, 0:1], red, 0.1, 1.0, ALU.mult, ALU.add))
        chain(dve.e.scalar_tensor_tensor(f[:, 0:1], blue, 0.05, f[:, 0:1], ALU.mult, ALU.add))
        chain(dve.e.scalar_tensor_tensor(f[:, 0:1], yellow, 0.15, f[:, 0:1], ALU.mult, ALU.add))
        chain(dve.e.tensor_scalar(f[:, 1:2], red, 0.0, 1.0, ALU.mult, ALU.add))
        chain(dve.e.tensor_scalar(f[:, 1:2], f[:, 1:2], float(1.0 / np.sqrt(8.0)), None, ALU.mult))
        chain(dve.e.tensor_tensor(factor[:, :], f[:, 0:1], f[:, 1:2], ALU.mult))
        chain(dve.e.tensor_scalar(f[:, 2:3], yellow, float(0.1 * np.sin(np.pi)), 1.0, ALU.mult, ALU.add))
        chain(dve.e.tensor_scalar(f[:, 3:4], blue, 0.1, 1.0, ALU.mult, ALU.add))
        chain(dve.e.tensor_scalar(f[:, 3:4], f[:, 3:4], 1e-5, None, ALU.mult))
        chain(dve.e.tensor_scalar(f[:, 4:5], red, 0.1, 1.0, ALU.mult, ALU.add))
        chain(dve.e.scalar_tensor_tensor(f[:, 4:5], yellow, 0.05, f[:, 4:5], ALU.mult, ALU.add))
        iota = pool.done(pool.e.iota(pos[:, :], pattern=[[1, T]], base=0, channel_multiplier=0, allow_small_or_imprecise_dtypes=True))
        dve.wait(iota)
        chain(dve.e.tensor_scalar(f[:, 5:6], yellow, float(0.1 * np.sin(np.pi / 2)), 1.0, ALU.mult, ALU.add))
        chain(dve.e.tensor_tensor(f[:, 5:6], f[:, 5:6], denom[:, 0:1], ALU.mult))
        chain(dve.e.reciprocal(f[:, 6:7], f[:, 5:6]))
        chain(dve.e.tensor_scalar(pos[:, :], pos[:, :], f[:, 6:7], None, ALU.mult))
        chain(dve.e.tensor_scalar(turns[:, :], pos[:, :], float(1 / (2 * np.pi)), denom[:, 1:2], ALU.mult, ALU.add))
        chain(dve.e.tensor_copy(whole[:, :], turns[:, :]))
        chain(dve.e.tensor_copy(turns[:, :], whole[:, :]))
        rest = 2 * np.pi
        for bits in (2 ** 5, 2 ** 17, None):
            part = float(np.floor(rest * bits) / bits) if bits else float(np.float32(rest))
            rest -= part
            chain(dve.e.scalar_tensor_tensor(pos[:, :], turns[:, :], -part, pos[:, :], ALU.mult, ALU.add))
        chain(dve.e.tensor_scalar(f[:, 7:8], denom[:, 1:2], float(np.float32(2 * np.pi)), None, ALU.mult))
        chain(dve.e.tensor_scalar(pos[:, :], pos[:, :], f[:, 7:8], 3.1415925, ALU.add, ALU.min))
        t = chain(dve.e.tensor_scalar(pos[:, :], pos[:, :], -3.1415925, None, ALU.max))
        self.angle = t

    def finish(self):
        core, psum, chain = self.core, self.psum, self.chain
        pe, act, dve = core.pe, core.act, core.dve
        pos, xp, xpt = self.pos, self.xp, self.xpt
        t = self.angle
        act.wait(t)
        t = act.done(act.e.activation(pos[:, :], pos[:, :], ACT.Sin))
        dve.wait(t)
        t = chain(dve.e.tensor_tensor(xp[:, :], core.XNT[:, :], pos[:, :], ALU.add))
        pe.wait(t)
        read = [None] * 2
        for b in range(4):
            ps = psum.bank(b % 2)
            pe.wait(read[b % 2])
            for j in range(4):
                m = pe.e.transpose(ps[:, j * P:(j + 1) * P], xp[:, (4 * b + j) * P:(4 * b + j + 1) * P], core.ident[:, :])
            m = pe.done(m)
            act.wait(m)
            read[b % 2] = act.done(act.e.activation(xpt[:, 4 * b:4 * b + 4, :], ps.rearrange("p (q d) -> p q d", q=4), ACT.Copy))


def attention2(core, psum, io, positions):
    nc, ctx = core.nc, core.ctx
    dve, chain = core.dve, positions.chain
    f, factor, xp, xpt = positions.f, positions.factor, positions.xp, positions.xpt
    with ExitStack() as own:
        core.ctx = own
        NarrowAttention(core, psum, io, factor, xp).run()
        core.ctx = ctx
    with ExitStack() as own:
        core.ctx = own
        rows = own.enter_context(nc.sbuf_tensor("A2_rows", [P, 3, D], F32))
        for i, n in enumerate(("bo", "ln_gamma", "ln_beta")):
            core.load(rows[:, i, :], io["L2_attn_" + n].partition_broadcast(P))
        dve.wait(core.loads.all())
        chain(dve.e.tensor_scalar(rows[:, 1, :], rows[:, 1, :], f[:, 4:5], None, ALU.mult))
        A = core.SACC
        over = lambda i: rows[:, i:i + 1, :].to_broadcast([P, NT, D])
        chain(dve.e.scalar_tensor_tensor(xpt[:, :, :], A[:, :, :], f[:, 2:3], xpt[:, :, :], ALU.mult, ALU.add))
        t = chain(dve.e.tensor_tensor(xpt[:, :, :], xpt[:, :, :], over(0), ALU.add))
        n = Norm(core, "A2n")
        made = n.run(lambda i: xpt[:, i, :], lambda i: A[:, i, :], eps=f[:, 3:4])
        dve.wait(made[-1])
        chain(dve.e.tensor_tensor(A[:, :, :], A[:, :, :], over(1), ALU.mult))
        chain(dve.e.tensor_tensor(A[:, :, :], A[:, :, :], over(2), ALU.add))
        core.ctx = ctx


def attention3(core, psum, io):
    nc, ctx = core.nc, core.ctx
    pe, act, dve, pool = core.pe, core.act, core.dve, core.pool
    sb = lambda n, s, d=F32: ctx.enter_context(nc.sbuf_tensor("A3_" + n, s, d))
    gains = sb("gains", [P, 8])
    with nc.allow_non_contiguous_dma("columns of 128"):
        for i, n in enumerate(("lnk_s", "lnk_b", "lnq_s", "lnq_b", "lnv_s", "lnv_b", "lnm_s", "lnm_b")):
            core.load(gains[:, i:i + 1], io["L3_attn_" + n].rearrange("(p a) -> p a", a=1))
    core.lastq = ctx.enter_context(nc.sbuf_tensor("lastq", [P, 2, P], BF16))
    core.lastk = ctx.enter_context(nc.sbuf_tensor("lastk", [P, 2, P], BF16))
    core.load(core.lastq[:, :, :], io["last_q"].bitcast(BF16))
    core.load(core.lastk[:, :, :], io["last_k"].bitcast(BF16))
    with ExitStack() as own:
        core.ctx = own
        srcs = [core.XNT] + [own.enter_context(nc.sbuf_tensor(f"A3_src{i}", [P, T], F32)) for i in range(2)]
        with ExitStack() as inner:
            core.ctx = inner
            z = inner.enter_context(nc.sbuf_tensor("A3_z", [P, NT, D], F32))
            n = Norm(core, "A3n")
            made = n.run(lambda i: core.XN[:, i, :], lambda i: z[:, i, :])
            act.wait(core.loads.all())
            to_features(core, psum, z, srcs[0], made)
            core.barrier()
            for i in (2, 1, 0):
                dve.done(dve.e.tensor_scalar(srcs[i][:, :], srcs[0][:, :], gains[:, 2 * i:2 * i + 1], gains[:, 2 * i + 1:2 * i + 2], ALU.mult, ALU.add))
            core.barrier()
        core.ctx = own
        NormedAttention(core, psum, io, srcs).run()
        core.ctx = ctx
    with ExitStack() as own:
        core.ctx = own
        st = lambda n, s, d=F32: own.enter_context(nc.sbuf_tensor("A3m_" + n, s, d))
        rows = st("rows", [P, 2, D])
        core.load(rows[:, 0, :], io["L3_attn_bo"].partition_broadcast(P))
        core.load(rows[:, 1, :], io["L3_attn_b2"].partition_broadcast(P))
        W1, W2, b1 = st("W1", [P, 256]), st("W2", [P, 2, P]), st("b1", [P, 2])
        core.load(W1[:, :], io["L3_attn_W1"])
        core.load(W2[:, :, :], io["L3_attn_W2"].rearrange("(j p) d -> p j d", p=P))
        with nc.allow_non_contiguous_dma("256 biases"):
            core.load(b1[:, :], io["L3_attn_b1"].rearrange("(j p) -> p j", p=P))
        z, yT, u = st("z", [P, NT, D]), st("yT", [P, T]), st("u", [P, 2, 2, BANK])
        H = core.SACC
        over = lambda i, n=NT: rows[:, i:i + 1, :].to_broadcast([P, n, D])
        dve.wait(core.loads.all())
        t = dve.done(dve.e.tensor_tensor(H[:, :, :], H[:, :, :], core.XN[:, :, :], ALU.add))
        dve.wait(t)
        t = dve.done(dve.e.tensor_tensor(H[:, :, :], H[:, :, :], over(0), ALU.add))
        n = Norm(core, "A3o")
        made = n.run(lambda i: H[:, i, :], lambda i: z[:, i, :], ready=(t,))
        to_features(core, psum, z, yT, made, scale=gains[:, 6:7], bias=gains[:, 7:8])
        dve.wait(made[-1])
        t = dve.done(dve.e.tensor_tensor(H[:, :, :], H[:, :, :], over(1), ALU.add))
        dve.wait(t)
        pe.wait((act.sem, act.count), core.loads.all())
        act.wait(core.loads.all())
        read = [None] * 8
        uread = [None] * 2
        for c in range(4):
            s = slice(c * BANK, (c + 1) * BANK)
            for j in range(2):
                b0 = 2 + (2 * c + j) % 4
                pe.wait(read[b0])
                made = pe.done(pe.e.matmul(psum.bank(b0), W1[:, j * P:(j + 1) * P], yT[:, s], start=True, stop=True))
                act.wait(made, uread[c % 2])
                last = read[b0] = act.done(act.e.activation(u[:, c % 2, j, :], psum.bank(b0), ACT.Gelu_apprx_tanh, bias=b1[:, j:j + 1]))
            b0 = 6 + c % 2
            y = psum.bank(b0)
            pe.wait(last, read[b0])
            for q in range(4):
                for j in range(2):
                    mm = pe.e.matmul(y[:, q * P:(q + 1) * P], u[:, c % 2, j, q * P:(q + 1) * P], W2[:, j, :], start=j == 0, stop=j == 1)
            uread[c % 2] = made = pe.done(mm)
            dve.wait(made)
            read[b0] = dve.done(dve.e.tensor_tensor(H[:, 4 * c:4 * c + 4, :], H[:, 4 * c:4 * c + 4, :], y.rearrange("p (q d) -> p q d", q=4), ALU.add))
        core.barrier()
        core.ctx = ctx


def rms_rows(core, src, dst, sq, ss, gain, n, ready=()):
    act, dve = core.act, core.dve
    dve.wait(*ready)
    t = dve.done(dve.e.tensor_tensor(sq[:, 0:n, :], src, src, ALU.mult))
    dve.wait(t)
    t = dve.done(dve.e.tensor_reduce(ss[:, 0, 0:n], sq[:, 0:n, :], AX.X, ALU.add))
    act.wait(t)
    r = act.done(act.e.activation(ss[:, 1, 0:n], ss[:, 0, 0:n], ACT.Sqrt))
    dve.wait(r)
    t = dve.done(dve.e.tensor_scalar(ss[:, 1, 0:n], ss[:, 1, 0:n], 1e-12, None, ALU.max))
    dve.wait(t)
    t = dve.done(dve.e.reciprocal(ss[:, 2, 0:n], ss[:, 1, 0:n]))
    dve.wait(t)
    t = dve.done(dve.e.tensor_tensor(ss[:, 2, 0:n], ss[:, 2, 0:n], ss[:, 0, 0:n], ALU.mult))
    dve.wait(t)
    t = dve.done(dve.e.tensor_tensor(ss[:, 1, 0:n], ss[:, 1, 0:n], ss[:, 2, 0:n], ALU.add))
    dve.wait(t)
    t = dve.done(dve.e.tensor_scalar(ss[:, 1, 0:n], ss[:, 1, 0:n], 0.5, 1e-12, ALU.mult, ALU.max))
    dve.wait(t)
    t = dve.done(dve.e.reciprocal(ss[:, 0, 0:n], ss[:, 1, 0:n]))
    dve.wait(t)
    t = dve.done(dve.e.tensor_scalar(ss[:, 0, 0:n], ss[:, 0, 0:n], float(np.sqrt(np.float32(D))), None, ALU.mult))
    dve.wait(t)
    for i in range(n):
        t = dve.done(dve.e.scalar_tensor_tensor(dst[:, i, :], src[:, i, :], ss[:, 0, i:i + 1], gain, ALU.mult, ALU.mult))
    return t


def soft_moe(core, psum, io):
    nc = core.nc
    pe, act, dve, pool = core.pe, core.act, core.dve, core.pool
    NS = 4
    with ExitStack() as ctx:
        sb = lambda n, s, d=F32: ctx.enter_context(nc.sbuf_tensor("F3_" + n, s, d))
        xr = sb("xr", [P, NT, 129])
        xrT = sb("xrT", [P, T])
        se = sb("se", [P, NS, D])
        seT = sb("seT", [P, BANK])
        gain = sb("gain", [P, 2, D])
        sq = sb("sq", [P, NT, D])
        ss = sb("ss", [P, 3, NT])
        w1, w2 = sb("w1", [P, BANK]), sb("w2", [P, NS, D])
        tokmax = sb("tokmax", [P, NT])
        slotpart = sb("slotpart", [P, NS, 4])
        slotmax = sb("slotmax", [P, NS])
        rows = sb("rows", [1, T + BANK])
        halves = [sb(f"rows{i}", [1, T + BANK], F32R) for i in range(2)]
        one = sb("one", [1, P], F32R)
        E = [sb(f"E{i}", [P, BANK]) for i in range(2)]
        rden = sb("rden", [P, NT])
        slots = sb("slots", [P, NS, D])
        slotsT = sb("slotsT", [P, BANK])
        hid = sb("hid", [P, NS, BANK])
        proc = sb("proc", [P, NS, 129])
        Ct = [sb(f"C{i}", [P, NS, BANK]) for i in range(2)]
        core.load(se[:, :, :], io["L3_ffn_slot_embeds"].rearrange("(a e) t d -> (e t) a d", a=NS))
        core.load(gain[:, 0, :], io["L3_ffn_gamma_x"].partition_broadcast(P))
        core.load(gain[:, 1, :], io["L3_ffn_gamma_slot"].partition_broadcast(P))
        core.load(w1[:, :], io["L3_ffn_w1"])
        core.load(w2[:, :, :], io["L3_ffn_w2"].rearrange("(j p) d -> p j d", p=P))
        pool.done(pool.e.memset(xr[:, :, 128:129], 1.0))
        pool.done(pool.e.memset(proc[:, :, 128:129], 1.0))
        a = rms_rows(core, core.XN[:, :, :], xr[:, :, 0:128], sq, ss, gain[:, 0, :], NT, ready=(core.loads.all(),))
        dve.wait(a)
        b = rms_rows(core, se[:, :, :], se, sq, ss, gain[:, 1, :], NS)
        core.barrier()
        for i in range(5):
            src = (lambda j: xr[:, 4 * i + j, 0:128]) if i < 4 else (lambda j: se[:, j, :])
            for j in range(4):
                m = pe.e.transpose(psum.bank(i)[:, j * P:(j + 1) * P], src(j), core.ident[:, :])
            m = pe.done(m)
            act.wait(m)
            act.done(act.e.activation(xrT[:, i * BANK:(i + 1) * BANK] if i < 4 else seT[:, :], psum.bank(i), ACT.Copy))
        core.barrier()
        read = [None] * 8
        for i in range(NT):
            b0 = i % 4
            pe.wait(read[b0])
            m = pe.done(pe.e.matmul(psum.bank(b0), xrT[:, i * P:(i + 1) * P], seT[:, :], start=True, stop=True))
            dve.wait(m)
            t = read[b0] = dve.done(dve.e.tensor_reduce(tokmax[:, i:i + 1], psum.bank(b0), AX.X, ALU.max, negate=True))
        for i in range(NS):
            for j in range(4):
                b0 = (4 * i + j) % 4
                pe.wait(read[b0])
                m = pe.done(pe.e.matmul(psum.bank(b0), seT[:, i * P:(i + 1) * P], xrT[:, j * BANK:(j + 1) * BANK], start=True, stop=True))
                dve.wait(m)
                t = read[b0] = dve.done(dve.e.tensor_reduce(slotpart[:, i, j:j + 1], psum.bank(b0), AX.X, ALU.max))
        dve.wait(t)
        t = dve.done(dve.e.tensor_reduce(slotmax[:, :], slotpart[:, :, :], AX.X, ALU.max, negate=True))
        pe.wait(t)
        for i in range(NT + NS):
            src = tokmax[:, i:i + 1] if i < NT else slotmax[:, i - NT:i - NT + 1]
            m = pe.e.matmul(psum.all[0:1, i * P:(i + 1) * P], src, core.ident[:, :], start=True, stop=True)
        m = pe.done(m)
        act.wait(m)
        t = act.done(act.e.activation(rows[:, :], psum.all[0:1, 0:T + BANK], ACT.Copy))
        act.done(act.e.activation(one[:, :], core.onerow[:, :], ACT.Copy))
        dve.wait(t)
        t = dve.done(dve.e.tensor_copy(halves[0][:, :], rows[:, :]))
        dve.wait(t)
        dve.done(dve.e.tensor_tensor(halves[1][:, :], rows[:, :], free(halves[0][:, :]), ALU.subtract))
        core.barrier()

        def shifted(ps, by, what, s):
            pe.e.matmul(ps, by, what, start=True, stop=False)
            pe.e.matmul(ps, one[:, :], halves[0][:, s], start=False, stop=False)
            return pe.done(pe.e.matmul(ps, one[:, :], halves[1][:, s], start=False, stop=True))

        read = [None] * 8
        eread = [None] * 2

        def weights(i):
            b0 = 4 + i % 2
            pe.wait(read[b0])
            m = shifted(psum.bank(b0), xrT[:, i * P:(i + 1) * P], seT[:, :], slice(T, T + BANK))
            act.wait(m, eread[i % 2])
            read[b0] = act.done(act.e.activation(E[i % 2][:, :], psum.bank(b0), ACT.Exp))

        weights(0)
        for i in range(NT):
            made = read[4 + i % 2]
            if i + 1 < NT:
                weights(i + 1)
            pe.wait(made)
            for j in range(NS):
                m = pe.e.matmul(psum.bank(j)[:, 0:129], E[i % 2][:, j * P:(j + 1) * P], xr[:, i, :], start=i == 0, stop=i == NT - 1)
            eread[i % 2] = pe.done(m)
        dve.wait(eread[1])
        for j in range(NS):
            t = dve.done(dve.e.reciprocal(rden[:, j:j + 1], psum.bank(j)[:, 128:129]))
            dve.wait(t)
            t = dve.done(dve.e.tensor_scalar(slots[:, j, :], psum.bank(j)[:, 0:128], rden[:, j:j + 1], None, ALU.mult))
        pe.wait(t)
        for j in range(NS):
            m = pe.e.transpose(psum.bank(0)[:, j * P:(j + 1) * P], slots[:, j, :], core.ident[:, :])
        m = pe.done(m)
        act.wait(m)
        t = act.done(act.e.activation(slotsT[:, :], psum.bank(0), ACT.Copy))
        pe.wait(t)
        for j in range(NS):
            m = pe.done(pe.e.matmul(psum.bank(1 + j), w1[:, j * P:(j + 1) * P], slotsT[:, :], start=True, stop=True))
            act.wait(m)
            t = act.done(act.e.activation(hid[:, j, :], psum.bank(1 + j), ACT.Gelu))
        pe.wait(t)
        for q in range(NS):
            for j in range(NS):
                m = pe.e.matmul(psum.bank(5)[:, q * P:(q + 1) * P], hid[:, j, q * P:(q + 1) * P], w2[:, j, :], start=j == 0, stop=j == NS - 1)
        m = pe.done(m)
        act.wait(m)
        act.done(act.e.activation(proc[:, :, 0:128], psum.bank(5).rearrange("p (q d) -> p q d", q=NS), ACT.Copy))
        core.barrier()
        read = [None] * 8
        cread = [None] * 2

        def combine(c):
            for j in range(NS):
                pe.wait(read[j])
                m = shifted(psum.bank(j), seT[:, j * P:(j + 1) * P], xrT[:, c * BANK:(c + 1) * BANK], slice(c * BANK, (c + 1) * BANK))
                act.wait(m, cread[c % 2])
                read[j] = act.done(act.e.activation(Ct[c % 2][:, j, :], psum.bank(j), ACT.Exp))

        combine(0)
        for c in range(4):
            made = read[NS - 1]
            if c < 3:
                combine(c + 1)
            pe.wait(made)
            for q in range(4):
                b0 = 4 + q
                y = psum.bank(b0)
                pe.wait(read[b0])
                for j in range(NS):
                    m = pe.e.matmul(y[:, 0:129], Ct[c % 2][:, j, q * P:(q + 1) * P], proc[:, j, :], start=j == 0, stop=j == NS - 1)
                cread[c % 2] = m = pe.done(m)
                i = 4 * c + q
                dve.wait(m)
                r = dve.done(dve.e.reciprocal(rden[:, i:i + 1], y[:, 128:129]))
                dve.wait(r)
                read[b0] = dve.done(dve.e.tensor_scalar(core.GATE[:, i, :], y[:, 0:128], rden[:, i:i + 1], None, ALU.mult))
        act.wait(read[7])
        act.done(act.e.activation(core.GATE[:, :, :], core.GATE[:, :, :], ACT.Silu))
        core.barrier()


def residual(core, ready=()):
    dve, pool = core.dve, core.pool
    dve.wait(*ready)
    for i in range(4):
        s = slice(4 * i, 4 * i + 4)
        m = dve.done(dve.e.tensor_tensor(core.GATE[:, s, :], core.GATE[:, s, :], core.SACC[:, s, :], ALU.mult))
        dve.wait(m)
        t = dve.done(dve.e.tensor_tensor(core.X[:, s, :], core.X[:, s, :], core.GATE[:, s, :], ALU.add))
    return t


def norm_layer(core, psum):
    with ExitStack() as ctx:
        core.ctx, keep = ctx, core.ctx
        n = Norm(core, f"N{core.layer}")
        core.ctx = keep
        made = n.run(lambda i: core.X[:, i, :], lambda i: core.XN[:, i, :])
        to_features(core, psum, core.XN, core.XNT, made)
        core.pool.done(core.pool.e.memset(core.SACC[:, :, :], 0.0))
        core.barrier()


def program(nc, io, out):
    with ExitStack() as ctx:
        core = Core(nc, ctx)
        psum = Psum(nc, ctx)
        sb = lambda n, s, d=F32: ctx.enter_context(nc.sbuf_tensor(n, s, d))
        core.X = sb("X", [P, NT, D])
        core.XN = sb("XN", [P, NT, D])
        core.XNT = sb("XNT", [P, T])
        core.SACC = sb("SACC", [P, NT, D])
        core.GATE = sb("GATE", [P, NT, D])
        core.ident = sb("ident", [P, P])
        core.identb = sb("identb", [P, P], BF16)
        core.ones = sb("ones", [P, 1])
        core.onerow = sb("onerow", [1, P])
        core.load(core.X[:, :, :], io["L0_attn_x"].rearrange("a (t p) d -> p (a t) d", p=P))
        core.load(core.ident[:, :], io["identity"])
        core.dve.wait(core.loads.all())
        core.dve.done(core.dve.e.tensor_copy(core.identb[:, :], core.ident[:, :]))
        core.dve.done(core.dve.e.memset(core.ones[:, :], 1.0))
        core.dve.done(core.dve.e.memset(core.onerow[:, :], 1.0))
        core.barrier()

        def layer(n, gate, attention):
            core.layer = n
            norm_layer(core, psum)
            gate()
            with ExitStack() as own:
                core.ctx = own
                attention()
                residual(core)
                core.barrier()
            core.ctx = ctx

        def attention0():
            core.maskq = core.ctx.enter_context(nc.sbuf_tensor("maskq", [P, 4, BANK], BF16))
            core.maskk = core.ctx.enter_context(nc.sbuf_tensor("maskk", [P, 4, BANK], BF16))
            core.load(core.maskq[:, :, :], io["mask_q"].bitcast(BF16))
            core.load(core.maskk[:, :, :], io["mask_k"].bitcast(BF16))
            RotaryAttention(core, psum, io).run()

        def attention1():
            LatentAttention(core, psum, io).run()

        layer(0, lambda: quantized_ffn(core, psum, io), attention0)
        layer(1, lambda: transformer_gate(core, psum, io), attention1)
        with ExitStack() as kept:
            positions = Positions(core, psum, io, kept)
            layer(2, lambda: ternary_ffn(core, psum, io, positions), lambda: attention2(core, psum, io, positions))
        layer(3, lambda: soft_moe(core, psum, io), lambda: attention3(core, psum, io))

        core.stores.add(nc.sync.dma_start(out.rearrange("a (t p) d -> p (a t) d", p=P), core.X[:, :, :]))
        core.sp.wait(core.stores.all())


def bf16_bits(a):
    return np.ascontiguousarray((a.astype(np.float32).view(np.uint32) >> 16).astype(np.uint16))


def constants():
    c = {"identity": np.eye(P, dtype=np.float32)}
    inv = (1.0 / 10000.0 ** (np.arange(0, 32, 2, dtype=np.float32) / np.float32(32))).astype(np.float32)
    f = np.arange(T, dtype=np.float32)[:, None] * inv[None, :]
    cos, sin = np.cos(f).T.astype(np.float32), np.sin(f).T.astype(np.float32)
    rest = np.ones((32, T), np.float32)
    c["rope_cos"] = np.concatenate([cos, cos, rest] * 2)
    c["rope_sin"] = np.concatenate([-sin, sin, 0 * rest] * 2)
    p = np.arange(P)[:, None, None]
    j = np.arange(4)[None, :, None]
    x = np.arange(BANK)[None, None, :]
    c["mask_q"] = bf16_bits(np.where(x <= P * j + p, 0.0, NEG))
    c["mask_k"] = bf16_bits(np.where(P * j + p <= x, 0.0, NEG))
    half = np.arange(0, 64, 2, dtype=np.float32)
    inv = (1.0 / 10000.0 ** (half / np.float32(64))).astype(np.float32)
    t = np.arange(T, dtype=np.float32)
    f = t[:, None] * inv[None, :]
    base = ((half + np.float32(25.6)) / np.float32(89.6)).astype(np.float32)
    power = (t - np.float32(T // 2)) / np.float32(32.0)
    scale = np.power(base[None, :], power[:, None]).astype(np.float32)
    scale, cos, sin = (np.concatenate([y, y], 1) for y in (scale, np.cos(f), np.sin(f)))
    sign = np.where(np.arange(64) < 32, -1.0, 1.0).astype(np.float32)
    tabs = np.stack([cos * scale, sin * sign * scale, cos / scale, sin * sign / scale], 1).astype(np.float32)
    c["xpos"] = np.ascontiguousarray(tabs.reshape(NT, P, 4, 64).transpose(1, 0, 2, 3))
    q, k = np.arange(P)[:, None], np.arange(-P, P)[None, :]
    band = np.where((k <= q) & (q <= k + 64), 0.0, NEG)
    nokeys = np.where(k < 0, NEG, band)
    c["band_mask"] = bf16_bits(np.stack([nokeys, band]))
    c["first_masks"] = bf16_bits(np.stack([nokeys, band, band, band]))
    moves = np.zeros((P, 2, P), np.float32)
    moves[np.arange(P - 1), 0, np.arange(1, P)] = 1.0
    moves[P - 1, 1, 0] = 1.0
    c["row_moves"] = moves
    even = (np.arange(D) // 2 * 2).astype(np.float32)
    c["position_denominators"] = np.stack([np.power(np.float32(10000.0), np.float32(2.0) * even / np.float32(D)), 0.25 * (np.arange(D) % 2)], 1).astype(np.float32)
    row = np.arange(P) % 32
    low = [(row > 8) & (row < 17), (row > 16) & (row < 25)]
    c["narrow_parts"] = np.stack([f for l in low for f in (np.where(l, 1.0, 0.0), np.where(l, -1.0, 1.0))], 1).astype(np.float32)
    last = np.zeros((P, 2, P), np.float32)
    last[0, :, P - 1] = (-992.0, -7.0)
    c["last_q"] = bf16_bits(last)
    c["last_k"] = bf16_bits(last.transpose(2, 1, 0))
    return c


TURN = ["L0_ffn_w_gate", "L0_ffn_w_up", "L0_ffn_w_down", "L1_attn_Wq", "L1_attn_Wkv_down", "L1_attn_Wk_up",
        "L1_attn_Wv_up", "L1_attn_Wo", "L2_attn_Wq", "L2_attn_Wk", "L2_attn_Wv", "L2_attn_Wo",
        "L2_ffn_w1_w", "L2_ffn_w2_w", "L2_ffn_h1_w", "L2_ffn_h2_w", "L2_ffn_w3_w"]


def kernel(**inputs):
    import concourse.bacc as bacc
    from concourse.bass_utils import run_bass_kernel_spmd

    arrays = {}
    for name, a in inputs.items():
        a = np.asarray(a)
        arrays[name] = np.ascontiguousarray(a.T if name in TURN else a)
    arrays.update(constants())
    nc = bacc.Bacc("TRN2", target_bir_lowering=False, num_devices=1)
    io = {n: nc.dram_tensor(n, a.shape, mybir.dt.from_np(a.dtype), kind="ExternalInput").ap() for n, a in arrays.items()}
    out = nc.dram_tensor("out", (1, T, D), F32, kind="ExternalOutput").ap()
    program(nc, io, out)
    r = run_bass_kernel_spmd(nc, [arrays], core_ids=[0])
    return r.results[0]["out"]
```
